# Optimizing a Trainium2 kernel written in Bass

```python
import numpy as np
import jax
import jax.numpy as jnp

def _softmax(x, axis=-1):
    return jax.nn.softmax(x, axis=axis)

def _gelu(x):
    return jax.nn.gelu(x, approximate=True)

def _silu(x):
    return jax.nn.silu(x)

def _sigmoid(x):
    return jax.nn.sigmoid(x)

def _layernorm(x, axis=-1, eps=1e-05):
    m = jnp.mean(x, axis=axis, keepdims=True)
    v = jnp.var(x, axis=axis, keepdims=True)
    return (x - m) / jnp.sqrt(v + eps)

def _scatter_add(tgt, idx, src, axis=0):
    return tgt.at[idx].add(src)

def _segment_sum(src, seg, n):
    return jax.ops.segment_sum(src, seg, n)
kernel_name = 'mk_adj_ffn_d4_adj_r2_c92a9f'

def setup_inputs(seed: int=0):
    np.random.seed(seed)
    _w = jnp.asarray

    def _rec_inputs():
        import jax
        import jax.numpy as jnp
        _gk = jax.random.key(seed)
        x = -0.0002928 + 1 * jax.random.normal(jax.random.fold_in(_gk, 1), (2048, 128), jnp.float32)
        _a = jax.random.bernoulli(jax.random.fold_in(_gk, 2), 0.00390625, (2048, 2048))
        _a = jnp.logical_or(_a, jnp.swapaxes(_a, -1, -2))
        _a = jnp.logical_or(_a, jnp.eye(2048, dtype=bool))
        adj = _a.astype(jnp.int32)
        return (x, adj)
    x, adj = _rec_inputs()

    def _L0_gnn_setup():
        import jax, jax.numpy as jnp
        import numpy as np
        N = 8192
        D = 128
        key = jax.random.key(seed)
        k1, k2, k3, k4 = jax.random.split(key, 4)
        x = jax.random.normal(k1, (N, D), dtype=jnp.float32)
        adj = jax.random.randint(k2, (N, N), 0, 2, dtype=jnp.int32)
        W = jax.random.normal(k3, (D, D), dtype=jnp.float32) * 0.05
        b = jax.random.normal(k4, (D,), dtype=jnp.float32) * 0.05
        return {'x': x, 'adj': adj, 'W': W, 'b': b}
    _L0_gnn_all = _L0_gnn_setup()
    _L0_gnn_in = {k: v for k, v in _L0_gnn_all.items() if k in ('W', 'b')}
    del _L0_gnn_all

    def _L0_ffn_setup():
        import jax, jax.numpy as jnp
        import numpy as np
        D_MODEL = 128
        D_STATE = 64
        D_CONV = 4
        EXPAND = 2
        HEADDIM = 64
        D_INNER = EXPAND * D_MODEL
        NHEADS = D_INNER // HEADDIM
        CONV_DIM = D_INNER + 2 * D_STATE
        D_IN_PROJ = 2 * D_INNER + 2 * D_STATE + NHEADS
        CHUNK = 128
        EPS = 1e-05

        def segsum(a):
            T = a.shape[-1]
            cs = jnp.cumsum(a, axis=-1)
            ss = cs[..., :, None] - cs[..., None, :]
            mask = jnp.tril(jnp.ones((T, T), dtype=bool))
            return jnp.where(mask, ss, -jnp.inf)

        def mamba2_block(x, W_in, conv_w, conv_b, dt_bias, A_log, D, norm_w, W_out, W_lin, b_lin):
            Bsz, L, _ = x.shape
            zxbcdt = x @ W_in
            z, xBC, dt = jnp.split(zxbcdt, [D_INNER, D_INNER + CONV_DIM], axis=-1)
            xp = jnp.pad(xBC, ((0, 0), (D_CONV - 1, 0), (0, 0)))
            conv = conv_b + sum((xp[:, k:k + L, :] * conv_w[:, k] for k in range(D_CONV)))
            xBC = jax.nn.silu(conv)
            xh, Bmat, Cmat = jnp.split(xBC, [D_INNER, D_INNER + D_STATE], axis=-1)
            dt = jax.nn.softplus(dt + dt_bias)
            A = -jnp.exp(A_log)
            nc = L // CHUNK
            xh = xh.reshape(Bsz, nc, CHUNK, NHEADS, HEADDIM)
            Bc = Bmat.reshape(Bsz, nc, CHUNK, D_STATE)
            Cc = Cmat.reshape(Bsz, nc, CHUNK, D_STATE)
            dtc = dt.reshape(Bsz, nc, CHUNK, NHEADS)
            dA = jnp.einsum('bclh,h->bhcl', dtc, A)
            A_cum = jnp.cumsum(dA, axis=-1)
            Lmat = jnp.exp(segsum(dA))
            xdt = xh * dtc[..., None]
            Y_diag = jnp.einsum('bcln,bcsn,bhcls,bcshp->bclhp', Cc, Bc, Lmat, xdt)
            decay_states = jnp.exp(A_cum[..., -1:] - A_cum)
            states = jnp.einsum('bcln,bhcl,bclhp->bchpn', Bc, decay_states, xdt)
            chunk_decay = jnp.exp(A_cum[..., -1])

            def step(h, inp):
                s, d = inp
                return (h * d[..., None, None] + s, h)
            _, prevs = jax.lax.scan(step, jnp.zeros_like(states[:, 0]), (jnp.moveaxis(states, 1, 0), jnp.moveaxis(chunk_decay, 2, 0)))
            prevs = jnp.moveaxis(prevs, 0, 1)
            Y_off = jnp.einsum('bcln,bchpn,bhcl->bclhp', Cc, prevs, jnp.exp(A_cum))
            Y = (Y_diag + Y_off + xh * D[:, None]).reshape(Bsz, L, D_INNER)
            Y = Y * jax.nn.silu(z)
            Y = Y * jax.lax.rsqrt(jnp.mean(Y * Y, axis=-1, keepdims=True) + EPS) * norm_w
            out = Y @ W_out
            return out @ W_lin + b_lin
        key = jax.random.key(seed)
        ks = jax.random.split(key, 12)
        B, L = (8, 2048)

        def gauss(k, shape, scale):
            return jax.random.normal(k, shape, dtype=jnp.float32) * scale
        return {'x': gauss(ks[0], (B, L, D_MODEL), 1.0), 'W_in': gauss(ks[1], (D_MODEL, D_IN_PROJ), D_MODEL ** (-0.5)), 'conv_w': gauss(ks[2], (CONV_DIM, D_CONV), 0.3), 'conv_b': gauss(ks[3], (CONV_DIM,), 0.1), 'dt_bias': jax.random.uniform(ks[4], (NHEADS,), minval=-4.0, maxval=-1.0), 'A_log': jnp.log(jax.random.uniform(ks[5], (NHEADS,), minval=1.0, maxval=16.0)), 'D': jnp.ones((NHEADS,), jnp.float32), 'norm_w': jnp.ones((D_INNER,), jnp.float32), 'W_out': gauss(ks[6], (D_INNER, D_MODEL), D_INNER ** (-0.5)), 'W_lin': gauss(ks[7], (D_MODEL, D_MODEL), D_MODEL ** (-0.5)), 'b_lin': jnp.zeros((D_MODEL,), jnp.float32)}
    _L0_ffn_all = _L0_ffn_setup()
    _L0_ffn_in = {k: v for k, v in _L0_ffn_all.items() if k in ('W_in', 'conv_w', 'conv_b', 'dt_bias', 'A_log', 'D', 'norm_w', 'W_out', 'W_lin', 'b_lin')}
    del _L0_ffn_all

    def _L1_gnn_setup():
        import jax, jax.numpy as jnp
        import numpy as np
        N, IN_DIM, OUT_DIM, HEADS = (4096, 128, 128, 2)
        C = OUT_DIM // HEADS
        ALPHA = 0.2
        NEG = -9000000000000000.0
        key = jax.random.key(seed)
        ks = jax.random.split(key, 9)
        h = jax.random.normal(ks[0], (N, IN_DIM), dtype=jnp.float32)
        adj = jax.random.randint(ks[1], (N, N), 0, 2, dtype=jnp.int32)

        def xav(k, shape):
            fan_in, fan_out = (shape[1], shape[0])
            s = 1.414 * np.sqrt(6.0 / (fan_in + fan_out))
            return jax.random.uniform(k, shape, jnp.float32, -s, s)
        W1 = xav(ks[2], (HEADS * C, IN_DIM))
        W2 = xav(ks[3], (HEADS * C, IN_DIM))
        W3 = xav(ks[4], (HEADS * C, IN_DIM))
        b1 = jnp.zeros((HEADS * C,), jnp.float32)
        b2 = jnp.zeros((HEADS * C,), jnp.float32)
        b3 = jnp.zeros((HEADS * C,), jnp.float32)
        sa = 1.414 * np.sqrt(6.0 / (HEADS + 2 * C))
        a = jax.random.uniform(ks[5], (HEADS, 2 * C), jnp.float32, -sa, sa)
        return {'h': h, 'adj': adj, 'W1': W1, 'b1': b1, 'W2': W2, 'b2': b2, 'W3': W3, 'b3': b3, 'a': a}
    _L1_gnn_all = _L1_gnn_setup()
    _L1_gnn_in = {k: v for k, v in _L1_gnn_all.items() if k in ('W1', 'b1', 'W2', 'b2', 'W3', 'b3', 'a')}
    del _L1_gnn_all

    def _L1_ffn_setup():
        import jax, jax.numpy as jnp
        import numpy as np
        B, S, D, E, H, K = (4, 2048, 128, 8, 256, 2)
        key = jax.random.key(seed)
        ks = jax.random.split(key, 6)
        x = jax.random.normal(ks[0], (B, S, D), jnp.float32)
        Wg = jax.random.normal(ks[1], (D, E), jnp.float32) * 0.02
        bg = jnp.zeros((E,), jnp.float32)
        W1 = jax.random.normal(ks[2], (E, D, H), jnp.float32) * 0.02
        b1 = jnp.zeros((E, H), jnp.float32)
        W2 = jax.random.normal(ks[3], (E, H, D), jnp.float32) * 0.02
        b2 = jnp.zeros((E, D), jnp.float32)
        return {'x': x, 'Wg': Wg, 'bg': bg, 'W1': W1, 'b1': b1, 'W2': W2, 'b2': b2}
    _L1_ffn_all = _L1_ffn_setup()
    _L1_ffn_in = {k: v for k, v in _L1_ffn_all.items() if k in ('Wg', 'bg', 'W1', 'b1', 'W2', 'b2')}
    del _L1_ffn_all

    def _L2_gnn_setup():
        import jax, jax.numpy as jnp
        import numpy as np
        N, D, H = (4096, 128, 128)
        KEEP_RATIO = 0.5
        TEMP = 1.0
        COS_EPS = 0.0001
        NEG = -9000000000000000.0

        def _cos_normalize(x):
            n = jnp.linalg.norm(x, axis=-1, keepdims=True)
            return x / jnp.maximum(n, COS_EPS)
        key = jax.random.key(seed)
        k1, k2, k3, k4 = jax.random.split(key, 4)
        features = jax.random.normal(k1, (N, D), dtype=jnp.float32)
        adj = jax.random.randint(k2, (N, N), 0, 2, dtype=jnp.int32)
        Wq = jax.random.normal(k3, (H, D), dtype=jnp.float32) * 0.001
        Wk = jax.random.normal(k4, (H, D), dtype=jnp.float32) * 0.001
        return {'features': features, 'adj': adj, 'Wq': Wq, 'Wk': Wk}
    _L2_gnn_all = _L2_gnn_setup()
    _L2_gnn_in = {k: v for k, v in _L2_gnn_all.items() if k in ('Wq', 'Wk')}
    del _L2_gnn_all

    def _L2_ffn_setup():
        import jax, jax.numpy as jnp
        import numpy as np
        B, S, D = (8, 2048, 128)
        H = 4 * D
        CAPACITY = 0.5
        key = jax.random.key(seed)
        ks = jax.random.split(key, 6)
        x = jax.random.normal(ks[0], (B, S, D), dtype=jnp.float32)
        attention_mask = jnp.zeros((B, 1, 1, S), dtype=jnp.float32)
        wr = jax.random.normal(ks[1], (D, 1), dtype=jnp.float32) * 0.02
        br = jnp.zeros((1,), dtype=jnp.float32)
        w1 = jax.random.normal(ks[2], (D, H), dtype=jnp.float32) * 0.02
        b1 = jnp.zeros((H,), dtype=jnp.float32)
        w2 = jax.random.normal(ks[3], (H, D), dtype=jnp.float32) * 0.02
        b2 = jnp.zeros((D,), dtype=jnp.float32)
        return {'x': x, 'attention_mask': attention_mask, 'wr': wr, 'br': br, 'w1': w1, 'b1': b1, 'w2': w2, 'b2': b2}
    _L2_ffn_all = _L2_ffn_setup()
    _L2_ffn_in = {k: v for k, v in _L2_ffn_all.items() if k in ('attention_mask', 'wr', 'br', 'w1', 'b1', 'w2', 'b2')}
    del _L2_ffn_all

    def _L3_gnn_setup():
        import jax, jax.numpy as jnp
        import numpy as np
        ALPHA = 0.2
        NEG_INF = -9000000000000000.0
        N, F_IN, F_OUT = (4096, 128, 128)
        key = jax.random.key(seed)
        k_h, k_adj, k_W, k_a = jax.random.split(key, 4)
        h = jax.random.normal(k_h, (N, F_IN), dtype=jnp.float32)
        adj = jax.random.randint(k_adj, (N, N), 0, 2, dtype=jnp.int32)
        gain = 1.414
        limit_W = gain * np.sqrt(6.0 / (F_IN + F_OUT))
        W = jax.random.uniform(k_W, (F_IN, F_OUT), dtype=jnp.float32, minval=-limit_W, maxval=limit_W)
        limit_a = gain * np.sqrt(6.0 / (2 * F_OUT + 1))
        a = jax.random.uniform(k_a, (2 * F_OUT, 1), dtype=jnp.float32, minval=-limit_a, maxval=limit_a)
        return {'h': h, 'adj': adj, 'W': W, 'a': a}
    _L3_gnn_all = _L3_gnn_setup()
    _L3_gnn_in = {k: v for k, v in _L3_gnn_all.items() if k in ('W', 'a')}
    del _L3_gnn_all

    def _L3_ffn_setup():
        import jax, jax.numpy as jnp
        import numpy as np
        B, S, D_MODEL, FFN, P = (8, 2048, 128, 512, 8)
        BLK = 128
        key = jax.random.key(seed)
        ks = jax.random.split(key, 12)
        x = jax.random.normal(ks[0], (B, S, D_MODEL), jnp.float32)
        Wt = 0.05 * jax.random.normal(ks[1], (FFN, D_MODEL), jnp.float32)
        bt = 0.05 * jax.random.normal(ks[2], (FFN,), jnp.float32)
        sl_cvx = 1.0 + 0.1 * jax.random.normal(ks[3], (FFN, P), jnp.float32)
        of_cvx = 0.1 * jax.random.normal(ks[4], (FFN, P), jnp.float32)
        sl_ccv = 1.0 + 0.1 * jax.random.normal(ks[5], (FFN, P), jnp.float32)
        of_ccv = 0.1 * jax.random.normal(ks[6], (FFN, P), jnp.float32)
        alpha = jnp.zeros((FFN,), jnp.float32)
        Wc = jax.random.normal(ks[7], (D_MODEL, FFN), jnp.float32) / np.sqrt(D_MODEL)
        bc = jnp.zeros((FFN,), jnp.float32)
        Wg = 0.01 * jax.random.normal(ks[8], (D_MODEL, FFN), jnp.float32)
        bg = 2.0 * jnp.ones((FFN,), jnp.float32)
        Wd = jax.random.normal(ks[9], (FFN, D_MODEL), jnp.float32) / np.sqrt(FFN)
        bd = jnp.zeros((D_MODEL,), jnp.float32)
        return {'x': x, 'Wt': Wt, 'bt': bt, 'sl_cvx': sl_cvx, 'of_cvx': of_cvx, 'sl_ccv': sl_ccv, 'of_ccv': of_ccv, 'alpha': alpha, 'Wc': Wc, 'bc': bc, 'Wg': Wg, 'bg': bg, 'Wd': Wd, 'bd': bd}
    _L3_ffn_all = _L3_ffn_setup()
    _L3_ffn_in = {k: v for k, v in _L3_ffn_all.items() if k in ('Wt', 'bt', 'sl_cvx', 'of_cvx', 'sl_ccv', 'of_ccv', 'alpha', 'Wc', 'bc', 'Wg', 'bg', 'Wd', 'bd')}
    del _L3_ffn_all
    return {'x': x, 'adj': adj, 'L0_gnn_W': _L0_gnn_in['W'], 'L0_gnn_b': _L0_gnn_in['b'], 'L0_ffn_W_in': _L0_ffn_in['W_in'], 'L0_ffn_conv_w': _L0_ffn_in['conv_w'], 'L0_ffn_conv_b': _L0_ffn_in['conv_b'], 'L0_ffn_dt_bias': _L0_ffn_in['dt_bias'], 'L0_ffn_A_log': _L0_ffn_in['A_log'], 'L0_ffn_D': _L0_ffn_in['D'], 'L0_ffn_norm_w': _L0_ffn_in['norm_w'], 'L0_ffn_W_out': _L0_ffn_in['W_out'], 'L0_ffn_W_lin': _L0_ffn_in['W_lin'], 'L0_ffn_b_lin': _L0_ffn_in['b_lin'], 'L1_gnn_W1': _L1_gnn_in['W1'], 'L1_gnn_b1': _L1_gnn_in['b1'], 'L1_gnn_W2': _L1_gnn_in['W2'], 'L1_gnn_b2': _L1_gnn_in['b2'], 'L1_gnn_W3': _L1_gnn_in['W3'], 'L1_gnn_b3': _L1_gnn_in['b3'], 'L1_gnn_a': _L1_gnn_in['a'], 'L1_ffn_Wg': _L1_ffn_in['Wg'], 'L1_ffn_bg': _L1_ffn_in['bg'], 'L1_ffn_W1': _L1_ffn_in['W1'], 'L1_ffn_b1': _L1_ffn_in['b1'], 'L1_ffn_W2': _L1_ffn_in['W2'], 'L1_ffn_b2': _L1_ffn_in['b2'], 'L2_gnn_Wq': _L2_gnn_in['Wq'], 'L2_gnn_Wk': _L2_gnn_in['Wk'], 'L2_ffn_attention_mask': _L2_ffn_in['attention_mask'], 'L2_ffn_wr': _L2_ffn_in['wr'], 'L2_ffn_br': _L2_ffn_in['br'], 'L2_ffn_w1': _L2_ffn_in['w1'], 'L2_ffn_b1': _L2_ffn_in['b1'], 'L2_ffn_w2': _L2_ffn_in['w2'], 'L2_ffn_b2': _L2_ffn_in['b2'], 'L3_gnn_W': _L3_gnn_in['W'], 'L3_gnn_a': _L3_gnn_in['a'], 'L3_ffn_Wt': _L3_ffn_in['Wt'], 'L3_ffn_bt': _L3_ffn_in['bt'], 'L3_ffn_sl_cvx': _L3_ffn_in['sl_cvx'], 'L3_ffn_of_cvx': _L3_ffn_in['of_cvx'], 'L3_ffn_sl_ccv': _L3_ffn_in['sl_ccv'], 'L3_ffn_of_ccv': _L3_ffn_in['of_ccv'], 'L3_ffn_alpha': _L3_ffn_in['alpha'], 'L3_ffn_Wc': _L3_ffn_in['Wc'], 'L3_ffn_bc': _L3_ffn_in['bc'], 'L3_ffn_Wg': _L3_ffn_in['Wg'], 'L3_ffn_bg': _L3_ffn_in['bg'], 'L3_ffn_Wd': _L3_ffn_in['Wd'], 'L3_ffn_bd': _L3_ffn_in['bd']}

def reference(x, adj, L0_gnn_W, L0_gnn_b, L0_ffn_W_in, L0_ffn_conv_w, L0_ffn_conv_b, L0_ffn_dt_bias, L0_ffn_A_log, L0_ffn_D, L0_ffn_norm_w, L0_ffn_W_out, L0_ffn_W_lin, L0_ffn_b_lin, L1_gnn_W1, L1_gnn_b1, L1_gnn_W2, L1_gnn_b2, L1_gnn_W3, L1_gnn_b3, L1_gnn_a, L1_ffn_Wg, L1_ffn_bg, L1_ffn_W1, L1_ffn_b1, L1_ffn_W2, L1_ffn_b2, L2_gnn_Wq, L2_gnn_Wk, L2_ffn_attention_mask, L2_ffn_wr, L2_ffn_br, L2_ffn_w1, L2_ffn_b1, L2_ffn_w2, L2_ffn_b2, L3_gnn_W, L3_gnn_a, L3_ffn_Wt, L3_ffn_bt, L3_ffn_sl_cvx, L3_ffn_of_cvx, L3_ffn_sl_ccv, L3_ffn_of_ccv, L3_ffn_alpha, L3_ffn_Wc, L3_ffn_bc, L3_ffn_Wg, L3_ffn_bg, L3_ffn_Wd, L3_ffn_bd):
    import jax
    import jax.numpy as jnp

    def _L0_gnn_ref(x, adj, W, b):
        import jax, jax.numpy as jnp
        import numpy as np
        N = 8192
        D = 128
        a = (adj == 1).astype(x.dtype)
        deg = jnp.sum(a, axis=1, keepdims=True)
        agg = jnp.einsum('ij,jf->if', a, x) / deg
        return agg @ W.T + b

    def _L0_ffn_ref(x, W_in, conv_w, conv_b, dt_bias, A_log, D, norm_w, W_out, W_lin, b_lin):
        import jax, jax.numpy as jnp
        import numpy as np
        D_MODEL = 128
        D_STATE = 64
        D_CONV = 4
        EXPAND = 2
        HEADDIM = 64
        D_INNER = EXPAND * D_MODEL
        NHEADS = D_INNER // HEADDIM
        CONV_DIM = D_INNER + 2 * D_STATE
        D_IN_PROJ = 2 * D_INNER + 2 * D_STATE + NHEADS
        CHUNK = 128
        EPS = 1e-05

        def segsum(a):
            T = a.shape[-1]
            cs = jnp.cumsum(a, axis=-1)
            ss = cs[..., :, None] - cs[..., None, :]
            mask = jnp.tril(jnp.ones((T, T), dtype=bool))
            return jnp.where(mask, ss, -jnp.inf)

        def mamba2_block(x, W_in, conv_w, conv_b, dt_bias, A_log, D, norm_w, W_out, W_lin, b_lin):
            Bsz, L, _ = x.shape
            zxbcdt = x @ W_in
            z, xBC, dt = jnp.split(zxbcdt, [D_INNER, D_INNER + CONV_DIM], axis=-1)
            xp = jnp.pad(xBC, ((0, 0), (D_CONV - 1, 0), (0, 0)))
            conv = conv_b + sum((xp[:, k:k + L, :] * conv_w[:, k] for k in range(D_CONV)))
            xBC = jax.nn.silu(conv)
            xh, Bmat, Cmat = jnp.split(xBC, [D_INNER, D_INNER + D_STATE], axis=-1)
            dt = jax.nn.softplus(dt + dt_bias)
            A = -jnp.exp(A_log)
            nc = L // CHUNK
            xh = xh.reshape(Bsz, nc, CHUNK, NHEADS, HEADDIM)
            Bc = Bmat.reshape(Bsz, nc, CHUNK, D_STATE)
            Cc = Cmat.reshape(Bsz, nc, CHUNK, D_STATE)
            dtc = dt.reshape(Bsz, nc, CHUNK, NHEADS)
            dA = jnp.einsum('bclh,h->bhcl', dtc, A)
            A_cum = jnp.cumsum(dA, axis=-1)
            Lmat = jnp.exp(segsum(dA))
            xdt = xh * dtc[..., None]
            Y_diag = jnp.einsum('bcln,bcsn,bhcls,bcshp->bclhp', Cc, Bc, Lmat, xdt)
            decay_states = jnp.exp(A_cum[..., -1:] - A_cum)
            states = jnp.einsum('bcln,bhcl,bclhp->bchpn', Bc, decay_states, xdt)
            chunk_decay = jnp.exp(A_cum[..., -1])

            def step(h, inp):
                s, d = inp
                return (h * d[..., None, None] + s, h)
            _, prevs = jax.lax.scan(step, jnp.zeros_like(states[:, 0]), (jnp.moveaxis(states, 1, 0), jnp.moveaxis(chunk_decay, 2, 0)))
            prevs = jnp.moveaxis(prevs, 0, 1)
            Y_off = jnp.einsum('bcln,bchpn,bhcl->bclhp', Cc, prevs, jnp.exp(A_cum))
            Y = (Y_diag + Y_off + xh * D[:, None]).reshape(Bsz, L, D_INNER)
            Y = Y * jax.nn.silu(z)
            Y = Y * jax.lax.rsqrt(jnp.mean(Y * Y, axis=-1, keepdims=True) + EPS) * norm_w
            out = Y @ W_out
            return out @ W_lin + b_lin
        return mamba2_block(x, W_in, conv_w, conv_b, dt_bias, A_log, D, norm_w, W_out, W_lin, b_lin)

    def _L1_gnn_ref(h, adj, W1, b1, W2, b2, W3, b3, a):
        import jax, jax.numpy as jnp
        import numpy as np
        N, IN_DIM, OUT_DIM, HEADS = (4096, 128, 128, 2)
        C = OUT_DIM // HEADS
        ALPHA = 0.2
        NEG = -9000000000000000.0
        n = h.shape[0]
        W1h = (h @ W1.T + b1).reshape(n, HEADS, C)
        W2h = (h @ W2.T + b2).reshape(n, HEADS, C)
        W3h = (h @ W3.T + b3).reshape(n, HEADS, C)
        a1, a2 = (a[:, :C], a[:, C:])
        s1 = jnp.einsum('nhc,hc->nh', W1h, a1)
        s2 = jnp.einsum('nhc,hc->nh', W2h, a2)
        e = jax.nn.leaky_relu(s1[:, None, :] + s2[None, :, :], ALPHA)
        e = jnp.where(adj[:, :, None] == 1, e, NEG)
        att = jax.nn.softmax(e, axis=1)
        h_prime = jnp.einsum('ijh,jhc->ihc', att, W3h)
        return h_prime.reshape(n, HEADS * C)

    def _L1_ffn_ref(x, Wg, bg, W1, b1, W2, b2):
        import jax, jax.numpy as jnp
        import numpy as np
        B, S, D, E, H, K = (4, 2048, 128, 8, 256, 2)
        Bv, Sv, Dv = x.shape
        gate_scores = x @ Wg + bg
        _, idx = jax.lax.top_k(gate_scores, K)
        mask = jax.nn.one_hot(idx, E, dtype=x.dtype).sum(axis=-2)
        xf = x.reshape(-1, Dv)
        mf = mask.reshape(-1, E)
        h = jax.nn.gelu(jnp.einsum('td,edh->teh', xf, W1) + b1[None], approximate=False)
        y = jnp.einsum('teh,ehd->ted', h, W2) + b2[None]
        out = jnp.einsum('ted,te->td', y, mf)
        return out.reshape(Bv, Sv, Dv)

    def _L2_gnn_ref(features, adj, Wq, Wk):
        import jax, jax.numpy as jnp
        import numpy as np
        N, D, H = (4096, 128, 128)
        KEEP_RATIO = 0.5
        TEMP = 1.0
        COS_EPS = 0.0001
        NEG = -9000000000000000.0

        def _cos_normalize(x):
            n = jnp.linalg.norm(x, axis=-1, keepdims=True)
            return x / jnp.maximum(n, COS_EPS)
        Qn = _cos_normalize(features @ Wq.T)
        Kn = _cos_normalize(features @ Wk.T)
        raw_att = Kn @ Qn.T
        att = jnp.where(adj > 0, raw_att, NEG) * TEMP
        att = jax.nn.softmax(att, axis=1)
        prop_fea = att @ features
        adj_mask = (jnp.sum(adj, axis=1) > 0).astype(features.dtype)[:, None]
        prop_fea = adj_mask * prop_fea + (1.0 - adj_mask) * features
        return (1.0 - KEEP_RATIO) * prop_fea + KEEP_RATIO * features

    def _L2_ffn_ref(x, attention_mask, wr, br, w1, b1, w2, b2):
        import jax, jax.numpy as jnp
        import numpy as np
        B, S, D = (8, 2048, 128)
        H = 4 * D
        CAPACITY = 0.5
        b, s, d = x.shape
        weights = (jnp.einsum('bsd,do->bso', x, wr) + br)[..., 0]
        k = max(1, int(CAPACITY * s))
        kk = k - 1 if k > 1 else 1
        _, idx = jax.lax.top_k(weights, k)
        sel_idx = idx[:, :kk]
        sel = jnp.take_along_axis(x, sel_idx[:, :, None], axis=1)
        h = jax.nn.gelu(jnp.einsum('bkd,dh->bkh', sel, w1) + b1)
        y = jnp.einsum('bkh,hd->bkd', h, w2) + b2
        w_sel = jnp.take_along_axis(weights, sel_idx, axis=1)
        y = y * w_sel[..., None]
        batch_idx = jnp.arange(b)[:, None]
        processed = jnp.zeros_like(x).at[batch_idx, sel_idx].set(y)
        return processed + x

    def _L3_gnn_ref(h, adj, W, a):
        import jax, jax.numpy as jnp
        import numpy as np
        ALPHA = 0.2
        NEG_INF = -9000000000000000.0
        N, F_IN, F_OUT = (4096, 128, 128)
        Wh = h @ W
        a1, a2 = (a[:F_OUT, 0], a[F_OUT:, 0])
        f1 = Wh @ a1
        f2 = Wh @ a2
        e = jax.nn.leaky_relu(f1[:, None] + f2[None, :], negative_slope=ALPHA)
        e = jnp.where(adj > 0, e, NEG_INF)
        attention = jax.nn.softmax(e, axis=1)
        h_prime = attention @ Wh
        return jax.nn.elu(h_prime)

    def _L3_ffn_ref(x, Wt, bt, sl_cvx, of_cvx, sl_ccv, of_ccv, alpha, Wc, bc, Wg, bg, Wd, bd):
        import jax, jax.numpy as jnp
        import numpy as np
        B, S, D_MODEL, FFN, P = (8, 2048, 128, 512, 8)
        BLK = 128
        Bx, Sx, D = x.shape
        T = Bx * Sx
        xf = x.reshape(T, D)
        xb = xf.reshape(T // BLK, BLK, D)
        s = jax.nn.sigmoid(alpha)

        def blk_fn(xx):
            t = jnp.max(xx[:, None, :] + Wt[None, :, :], axis=-1) + bt
            z = t[:, :, None]
            cvx = jnp.max(z * sl_cvx[None] + of_cvx[None], axis=-1)
            ccv = jnp.min(z * sl_ccv[None] + of_ccv[None], axis=-1)
            return s * cvx + (1.0 - s) * ccv
        trop = jax.lax.map(blk_fn, xb).reshape(T, FFN)
        classical = jax.nn.gelu(xf @ Wc + bc, approximate=False)
        g = jax.nn.sigmoid(xf @ Wg + bg)
        fused = g * trop + (1.0 - g) * classical
        out = fused @ Wd + bd
        return out.reshape(Bx, Sx, D)
    x = x + _L0_gnn_ref(_layernorm(x, axis=-1), adj, L0_gnn_W, L0_gnn_b)
    x = x + _L0_ffn_ref(_layernorm(x, axis=-1)[None], L0_ffn_W_in, L0_ffn_conv_w, L0_ffn_conv_b, L0_ffn_dt_bias, L0_ffn_A_log, L0_ffn_D, L0_ffn_norm_w, L0_ffn_W_out, L0_ffn_W_lin, L0_ffn_b_lin)[0]
    x = x + _L1_gnn_ref(_layernorm(x, axis=-1), adj, L1_gnn_W1, L1_gnn_b1, L1_gnn_W2, L1_gnn_b2, L1_gnn_W3, L1_gnn_b3, L1_gnn_a)
    x = x + _L1_ffn_ref(_layernorm(x, axis=-1)[None], L1_ffn_Wg, L1_ffn_bg, L1_ffn_W1, L1_ffn_b1, L1_ffn_W2, L1_ffn_b2)[0]
    x = x + _L2_gnn_ref(_layernorm(x, axis=-1), adj, L2_gnn_Wq, L2_gnn_Wk)
    x = x + _L2_ffn_ref(_layernorm(x, axis=-1)[None], L2_ffn_attention_mask, L2_ffn_wr, L2_ffn_br, L2_ffn_w1, L2_ffn_b1, L2_ffn_w2, L2_ffn_b2)[0]
    x = x + _L3_gnn_ref(_layernorm(x, axis=-1), adj, L3_gnn_W, L3_gnn_a)
    x = x + _L3_ffn_ref(_layernorm(x, axis=-1)[None], L3_ffn_Wt, L3_ffn_bt, L3_ffn_sl_cvx, L3_ffn_of_cvx, L3_ffn_sl_ccv, L3_ffn_of_ccv, L3_ffn_alpha, L3_ffn_Wc, L3_ffn_bc, L3_ffn_Wg, L3_ffn_bg, L3_ffn_Wd, L3_ffn_bd)[0]
    return x

_drawn_inputs = setup_inputs


def setup_inputs(seed=0):
    import zlib

    import numpy as np

    out = dict(_drawn_inputs(seed))
    spreads = {'L0_ffn_D': (1.0, 0.2),
     'L0_ffn_norm_w': (1.0, 0.2),
     'L0_ffn_b_lin': (0.0, 0.1),
     'L1_gnn_b1': (0.0, 0.726),
     'L1_gnn_b2': (0.0, 0.8),
     'L1_gnn_b3': (0.0, 0.1),
     'L1_ffn_bg': (0.0, 0.1),
     'L1_ffn_b1': (0.0, 0.556),
     'L1_ffn_b2': (0.0, 0.1),
     'L2_ffn_b1': (0.0, 0.8),
     'L2_ffn_b2': (0.0, 0.8),
     'L3_ffn_alpha': (0.0, 0.8),
     'L3_ffn_bc': (0.0, 2.0),
     'L3_ffn_bg': (2.0, 0.6),
     'L3_ffn_bd': (0.0, 0.326)}
    factors = {'L0_ffn_A_log': 4.447,
     'L2_gnn_Wq': 62.563,
     'L2_gnn_Wk': 49.444,
     'L2_ffn_wr': 8.0,
     'L2_ffn_w1': 8.0,
     'L2_ffn_w2': 8.0,
     'L3_ffn_Wt': 5.258,
     'L3_ffn_bt': 5.184,
     'L3_ffn_sl_cvx': 3.248,
     'L3_ffn_of_cvx': 5.691,
     'L3_ffn_sl_ccv': 3.021,
     'L3_ffn_of_ccv': 16.068,
     'L3_ffn_Wc': 2.882,
     'L3_ffn_Wg': 7.155}
    for name, (base, spread) in spreads.items():
        noise = np.random.default_rng([zlib.crc32(name.encode()), seed]).standard_normal(out[name].shape)
        drawn = base * np.exp(spread * noise) if base else spread * noise
        out[name] = jnp.asarray(drawn.astype(out[name].dtype))
    for name, factor in factors.items():
        out[name] = (out[name] * factor).astype(out[name].dtype)
    return out
```

```python
import numpy as np
import concourse.bass as bass
from concourse import mybir
from contextlib import ExitStack

F32 = mybir.dt.float32
BF16 = mybir.dt.bfloat16
I32 = mybir.dt.int32
ALU = mybir.AluOpType
ACT = mybir.ActivationFunctionType
AX = mybir.AxisListType.X

P = 128
N = 2048
D = 128
T = N // P
BLK = 512
NB = N // BLK
EPS = 1e-5
DEBUG = 0
LAYERS = 8

DIN, DST, KC, NH, HD = 256, 64, 4, 4, 64
XB = DIN + DST
E1, H1 = 8, 256
HT1 = E1 * H1 // P
H2 = 512
KSEL = N // 2 - 1
FF, PP = 512, 8
FT = FF // P
NEG = -1e30
FILL = -3.0e38


def build(nc, ins, out, dbg):
    with ExitStack() as ctx:
        def sb(name, shape, dt=F32):
            return ctx.enter_context(nc.sbuf_tensor(name, shape, dt))

        def sem(name):
            return ctx.enter_context(nc.semaphore(name))

        ps = ctx.enter_context(nc.psum_tensor("ps", [P, 8, BLK], F32))
        ps_wide = ps[:, :, :].rearrange("p (b k) n -> p b (k n)", b=2)

        x = sb("x", [P, T, D])
        xn = sb("xn", [P, T, D])
        xnT = sb("xnT", [P, 4 + N])
        mask = sb("mask", [P, T, N], BF16)
        ident = sb("ident", [P, P])
        identb = sb("identb", [P, P], BF16)
        ones = sb("ones", [P, P])
        upper = sb("upper", [P, P])
        negtri = sb("negtri", [P, P])
        tri = sb("tri", [P, P])
        tric = sb("tric", [P, P])
        selx = sb("selx", [96, 32], BF16)
        seld = sb("seld", [96, 16], BF16)
        rise = sb("rise", [P, D // 2, FT]); bias = sb("bias", [P, 2, FT])
        stats = sb("stats", [P, T, 6])
        mv = sb("mv", [P, T, 2])
        lnv = sb("lnv", [P, 4, T])
        deg = sb("deg", [P, T])
        XT = xnT[:, 4:4 + N]

        W = {}

        def weight(name, shape):
            W[name] = sb("w_" + name, shape)
            return W[name]

        weight("W0T", [P, D]); weight("b0", [P, D])
        weight("win", [P, 2 * DIN + 2 * DST + NH])
        weight("convb_row", [1, XB]); weight("convb_bc", [DST, 2])
        weight("dtb", [P, NH]); weight("alog", [P, NH]); weight("Dh", [P, NH])
        weight("nw", [P, 2]); weight("woutT", [P, DIN]); weight("wlin", [P, D]); weight("blin", [P, D])
        weight("W1n", [P, D]); weight("W2n", [P, D]); weight("WVu", [P, D + 4])
        weight("b12", [P, 2]); weight("A1", [P, 2]); weight("A2", [P, 2]); weight("vbias", [P, D + 4])
        weight("wg", [P, E1]); weight("bg", [P, E1]); weight("b1c", [P, HT1]); weight("b2r", [E1, D])
        weight("w1e", [P, E1 * H1])
        weight("wqT", [P, D]); weight("wkT", [P, D])
        weight("wr", [P, 1]); weight("br", [P, 1]); weight("w1m", [P, H2]); weight("b1m", [P, H2 // P])
        weight("w2m", [P, H2 // P, D]); weight("b2m", [P, D])
        weight("W3WT", [P, D]); weight("WVu3", [P, D + 2]); weight("a3", [P, 2])
        weight("Wt", [P, FT, D]); weight("bt", [P, FT])
        weight("slx", [P, FT, PP]); weight("ofx", [P, FT, PP]); weight("slc", [P, FT, PP]); weight("ofc", [P, FT, PP])
        weight("alpha", [P, FT]); weight("Wc", [P, FF]); weight("bc", [P, FT])
        weight("Wg", [P, FF]); weight("bgt", [P, FT]); weight("Wd", [P, FT, D]); weight("bd", [P, D])

        AR = 19300
        W2E_AT = AR - HT1 * D
        arena = sb("arena", [P, AR])
        at = [0]

        def lay(*shape, dt=F32, parts=P, fresh=False, to=None):
            if fresh:
                at[0] = 0
            if to is not None:
                at[0] = to
            size = int(np.prod(shape))
            words = size if dt == F32 else (size + 1) // 2
            v = arena[0:parts, at[0]:at[0] + words]
            at[0] += words
            assert at[0] <= AR, at[0]
            if dt != F32:
                v = v.bitcast(dt)[:, 0:size]
            names = "abcd"[:len(shape)]
            if len(shape) > 1:
                v = v.rearrange(f"p ({' '.join(names)}) -> p {' '.join(names)}", **dict(zip(names, shape)))
            return v

        x_loaded = sem("x_loaded"); cw_loaded = sem("cw_loaded"); w_loaded = sem("w_loaded")
        adj_in = [sem(f"adj_in{i}") for i in range(4)]
        mask_ready = sem("mask_ready"); consts = sem("consts")
        bn_chain = sem("bn_chain"); var_ready = sem("var_ready"); sqrt_ready = sem("sqrt_ready")
        xn_ready = sem("xn_ready"); xnT_ps = sem("xnT_ps"); xnT_ready = sem("xnT_ready")
        x_ready = sem("x_ready")
        dve_step = sem("dve_step"); act_step = sem("act_step"); pool_step = sem("pool_step")
        out_done = sem("out_done"); dbg_done = sem("dbg_done")

        steps = {"dve": 0, "act": 0, "pool": 0}

        def in_turn(eng, name, s, ins_):
            steps[name] += 1
            ins_.then_inc(s, 1)
            eng.wait_ge(s, steps[name])

        n_w = [0]
        block = ctx.enter_context(nc.Block())

        def bcast(v, n):
            return v.unsqueeze(len(v.shape)).broadcast_to(list(v.shape) + [n])

        stage_adj = lay(4, N, fresh=True).bitcast(I32)
        V0 = lay(T, D)
        XP0 = lay(T, 3 * D + 2, dt=BF16)
        R0 = lay(8, D)
        rdeg = lay(T)
        v0_ps = sem("v0_ps"); v0_ready = sem("v0_ready"); xp0_ready = sem("xp0_ready")
        agg_ps = sem("agg_ps"); agg_read = sem("agg_read")

        xs = lay(T, XB, fresh=True)
        sz = lay(T, DIN)
        CT = lay(N, parts=DST)
        BT = xn[0:DST, :, :].rearrange("p t d -> p (t d)")
        xdt = lay(2, DIN); xdd = lay(2, DIN)
        rowin = lay(2, NH, P)
        EM = lay(2, NH, P)
        Hst = lay(2, DIN, parts=DST)
        yscr = lay(2, DIN)
        wk = lay(KC, DIN + 2 * DST)
        cwb = sz[:, 0:6, :].rearrange("p c n -> p (c n)").rearrange("p (k n) -> p k n", k=KC)
        small = lay(12, T * NH)
        wol = lay(2, D)
        mamba_end = at[0]
        Aneg = lay(NH)
        DI = lay(NH, P)
        yT = lay(2, 2, P, to=0)
        wk_ready = sem("wk_ready"); wol_ps = sem("wol_ps"); wol_ready = sem("wol_ready")
        xb_ps = sem("xb_ps"); xs_ready = sem("xs_ready"); z_ps = sem("z_ps"); z_read = sem("z_read"); dt_read = sem("dt_read")
        bcT_ps = sem("bcT_ps"); bcT_ready = sem("bcT_ready")
        sp_exp = sem("sp_exp"); sp_ln = sem("sp_ln"); sp_e_ready = sem("sp_e_ready"); sp_u_ready = sem("sp_u_ready")
        dA_ready = sem("dA_ready"); acum_ps = sem("acum_ps"); acum_ready = sem("acum_ready"); decay_ready = sem("decay_ready")
        alog_exp = sem("alog_exp"); DI_ready = sem("DI_ready")
        rowin_ready = sem("rowin_ready"); row_ps = sem("row_ps"); E_ready = sem("E_ready"); G_ps = sem("G_ps")
        M_ready = sem("M_ready"); xdt_ready = sem("xdt_ready"); y_ps = sem("y_ps"); y_done = sem("y_done")
        h_ready = sem("h_ready"); sq_done = sem("sq_done"); yrms_var = sem("yrms_var"); yrms_sqrt = sem("yrms_sqrt")
        yT_ps = sem("yT_ps"); yT_ready = sem("yT_ready"); mo_ps = sem("mo_ps"); mo_read = sem("mo_read")

        def attention_memory(tag, heads, dh, ring, bias_cols):
            a = {}
            w1 = dh + 1
            a["heads"], a["dh"], a["w1"], a["ring"] = heads, dh, w1, ring
            a["VS"] = lay(T, D + bias_cols, fresh=True)
            a["Fv"] = lay(T, 2, w1)
            a["XP"] = [lay(T, 2, 3, w1, dt=BF16) for _ in range(heads)]
            a["row"] = [lay(N) for _ in range(heads)]
            a["M1"] = lay(ring, BLK, dt=BF16)
            a["M2"] = lay(ring, BLK, dt=BF16)
            a["R"] = lay(4, 2, w1)
            a["num"] = lay(4, w1)
            a["rd"] = lay(4)
            a["arg"] = lay(4, heads, T)
            a["ex"] = lay(4, heads, T)
            a["thr"] = lay(heads, T)
            a["smax"] = lay(heads)
            a["S"] = lay(heads)
            a["tt"] = lay(heads, T)
            a["cc"] = lay(heads, T)
            a["end"] = at[0]
            a["banks"] = 1 if 6 * w1 <= BLK else 2
            a["sets"] = 8 // (4 * a["banks"])
            for s in ("u_ps", "u_ready", "v_ps", "v_ready", "smax_ready", "S_ready", "arg_ready", "ex_ready",
                      "row_ps", "row_ready", "xp_ready", "m_ready", "m_used", "acc_ps", "acc_read"):
                a[s] = sem(f"{tag}_{s}")
            return a

        A1 = attention_memory("g1", 2, 64, 3, 4)
        assert A1["end"] <= W2E_AT, (A1["end"], W2E_AT)
        w2e = lay(HT1, D, to=W2E_AT)
        w2e_loaded = sem("w2e_loaded")
        A3 = attention_memory("g3", 1, 128, 5, 2)
        elu_m = lay(T, D, to=0)
        h3 = lay(T, D, to=T * (D + 2))
        elu_ready = sem("elu_ready"); elu_exp = sem("elu_exp")

        hT1 = lay(4, 2, BLK, fresh=True)
        gates = lay(T, E1 + 6)
        top8 = lay(T, 8)
        marked = lay(T, E1 + 6)
        emask = lay(T, E1)
        emT = lay(N, parts=E1)
        assert at[0] <= W2E_AT
        g_ps = sem("g_ps"); emask_ready = sem("emask_ready"); emT_ps = sem("emT_ps"); emT_ready = sem("emT_ready")
        h1_ps = sem("h1_ps"); h1_ready = sem("h1_ready"); o1_ps = sem("o1_ps"); o1_read = sem("o1_read")

        RE = 6
        Kt = lay(T, D, fresh=True)
        KnT = lay(N); QT = lay(N)
        Er = lay(RE, BLK)
        xn1 = lay(T, D + 1)
        qs = lay(8, T)
        sqj = lay(D)
        ab = lay(4, T)
        kq_ps = sem("kq_ps"); kq_read = sem("kq_read"); QT_ps = sem("QT_ps"); QT_ready = sem("QT_ready")
        norm_sq = sem("norm_sq"); norm_sqrt = sem("norm_sqrt"); kn_ready = sem("kn_ready")
        KnT_ps = sem("KnT_ps"); KnT_ready = sem("KnT_ready"); xn1_ready = sem("xn1_ready")
        sc_ps = sem("sc_ps"); sc_exp = sem("sc_exp"); p_ready = sem("p_ready"); p_used = sem("p_used")
        a2_ps = sem("a2_ps"); a2_read = sem("a2_read")

        wcol = lay(T, fresh=True)
        wrow = lay(N)
        junk = lay(N + P)
        rank = lay(4, T)
        sw = lay(T)
        hT2 = lay(2, H2 // P, BLK)
        w_ps = sem("w_ps"); wcol_ready = sem("wcol_ready"); wrow_ps = sem("wrow_ps"); wrow_ready = sem("wrow_ready")
        h2_ps = sem("h2_ps"); h2_ready = sem("h2_ready"); o2_ps = sem("o2_ps"); o2_read = sem("o2_read")

        GF = 32
        NG = D // GF
        xg = lay(NG, N, dt=BF16, parts=3 * GF, fresh=True)
        xp3 = lay(3, N, dt=BF16)
        res = lay(N)
        rise_m = lay(N + BLK * 2, to=NG * N // 2)
        rise0 = lay(N)
        rise1 = lay(2, N)
        oddc = lay(2, N)
        sa = lay(2, FT)
        AF = [lay(N, to=0), lay(N), lay(N), lay(N)]
        big = mask[:, :, :].rearrange("p t n -> p (t n)").bitcast(F32)
        acc = big[:, 0:FT * N].rearrange("p (f n) -> p f n", f=FT)
        CL = big[:, FT * N:FT * N + N]; G = big[:, FT * N + N:FT * N + 2 * N]
        cvx = big[:, FT * N + 2 * N:FT * N + 3 * N]; ccv = big[:, FT * N + 3 * N:FT * N + 4 * N]
        xp3_ready = sem("xp3_ready"); xg_in = sem("xg_in"); sel_ready = sem("sel_ready"); rise_table = sem("rise_table")
        bias_ready = sem("bias_ready"); fill_done = sem("fill_done"); bd_added = sem("bd_added")
        diff_ps = sem("diff_ps"); odd_ps = sem("odd_ps"); even_ps = sem("even_ps"); pair_ps = sem("pair_ps")
        odd_copied = sem("odd_copied"); rise_pe = sem("rise_pe"); rise_pool = sem("rise_pool"); sum_ready = sem("sum_ready")
        single_step = sem("single_step"); pair_step = sem("pair_step"); sum_step = sem("sum_step")
        z_ready = sem("z_ready"); af_ready = sem("af_ready"); af_used = sem("af_used")
        cl_ps = sem("cl_ps"); cl_ready = sem("cl_ready"); gt_ready = sem("gt_ready")
        sa_ready = sem("sa_ready"); fused_ready = sem("fused_ready"); trop_mix = sem("trop_mix"); f_ps = sem("f_ps")

        ld = []

        def load(eng, dst, src):
            ld.append(1)
            eng.dma_start(dst, src).then_inc(w_loaded, 16)

        small_loads = [
            ("W0T", "W0T"), ("win", "win"), ("woutT", "woutT"), ("wlin", "wlin"), ("W1n", "W1n"), ("W2n", "W2n"),
            ("wg", "wg"), ("w1e", "w1e"), ("wqT", "wqT"), ("wkT", "wkT"), ("w1m", "w1m"), ("W3WT", "W3WT"),
            ("Wc", "Wc"), ("Wg", "Wg"), ("b2r", "b2r"), ("wr", "wr"), ("w2m", "w2m"), ("Wt", "Wt"), ("Wd", "Wd"),
            ("slx", "slx"), ("ofx", "ofx"), ("slc", "slc"), ("ofc", "ofc"), ("bt", "bt"), ("alpha", "alpha"),
            ("bc", "bc"), ("bgt", "bgt"), ("b1m", "b1m"), ("b1c", "b1c"), ("nw", "nw"), ("convb_bc", "convb_bc"),
            ("b12", "b12"), ("a3", "a3"), ("convb_row", "convb_row")]
        row_loads = ["b0", "dtb", "alog", "Dh", "blin", "bg", "br", "b2m", "bd"]
        N_W = len(small_loads) + len(row_loads) + 1 + 4 + 1 + 1

        def dump(sp, q):
            if DEBUG and q < LAYERS:
                sp.wait_ge(x_ready, q + 1)
                sp.dma_start(dbg[q].rearrange("(t p) d -> p t d", p=P), x[:, :, :]).then_inc(dbg_done, 16)
                sp.wait_ge(dbg_done, 16 * (q + 1))

        @block.sync
        def _(sp):
            sp.dma_start(x[:, :, :], ins["x"].rearrange("(t p) d -> p t d", p=P)).then_inc(x_loaded, 16)
            for name, src in small_loads:
                load(sp, W[name][:], ins[src])
            for name in row_loads:
                load(sp, W[name][:], ins[name].partition_broadcast(P))
            load(sp, W["vbias"][:, 0:D], ins["b3"].partition_broadcast(P))
            load(sp, W["WVu"][:, 0:D], ins["W3T"])
            load(sp, W["WVu3"][:, 0:D], ins["W3W"])
            sp.wait_ge(consts, 1)
            for h in range(2):
                load(sp, W["A1"][64 * h:64 * h + 64, h:h + 1], ins["a"][h, 0:64].unsqueeze(1))
                load(sp, W["A2"][64 * h:64 * h + 64, h:h + 1], ins["a"][h, 64:128].unsqueeze(1))
            assert len(ld) == N_W, (len(ld), N_W)
            for jt in range(4, T):
                sp.wait_ge(mask_ready, jt - 3)
                sp.dma_start(stage_adj[:, jt % 4, :], ins["adjT"][jt * P:(jt + 1) * P, :]).then_inc(adj_in[jt % 4], 16)
            if LAYERS > 1:
                sp.wait_ge(x_ready, 1)
                sp.dma_start(cwb, ins["conv_w"].partition_broadcast(P)).then_inc(cw_loaded, 16)
            dump(sp, 0)
            if LAYERS > 2:
                sp.wait_ge(x_ready, 2)
                sp.dma_start(w2e, ins["w2e"]).then_inc(w2e_loaded, 16)
            for q in range(1, 7):
                dump(sp, q)
            if LAYERS > 7:
                sp.wait_ge(xp3_ready, 1)
                for g in range(NG):
                    for k in range(3):
                        sp.dma_start(xg[k:3 * (GF - 1) + k + 1:3, g, :], xp3[g * GF:(g + 1) * GF, k, :]).then_inc(xg_in, 16)
            if LAYERS < 8:
                sp.wait_ge(x_ready, LAYERS)
                sp.dma_start(out.rearrange("(t p) d -> p t d", p=P), x[:, :, :]).then_inc(out_done, 16)
                sp.wait_ge(out_done, 16)
            else:
                for t in range(T):
                    sp.wait_ge(x_ready, 7 + t + 1)
                    sp.dma_start(out[t * P:(t + 1) * P, :], x[:, t, :]).then_inc(out_done, 16)
                sp.wait_ge(out_done, 16 * T)

        @block.gpsimd
        def _(pool):
            def pin(i):
                in_turn(pool, "pool", pool_step, i)
            pin(pool.memset(W["A1"][:], 0.0))
            pool.memset(W["A2"][:], 0.0).then_inc(consts, 1)
            pin(pool.memset(ident[:], 0.0))
            pin(pool.affine_select(out=ident[:], in_=ident[:], compare_op=ALU.not_equal, fill=1.0, base=0,
                                   pattern=[[-1, P]], channel_multiplier=1))
            pin(pool.tensor_copy(identb[:], ident[:]))
            pin(pool.memset(ones[:], 1.0))
            pin(pool.affine_select(out=upper[:], in_=ones[:], compare_op=ALU.is_ge, fill=0.0, base=0,
                                   pattern=[[1, P]], channel_multiplier=-1))
            pin(pool.affine_select(out=tri[:], in_=ones[:], compare_op=ALU.is_gt, fill=0.0, base=0,
                                   pattern=[[-1, P]], channel_multiplier=1))
            pin(pool.affine_select(out=tric[:], in_=ones[:], compare_op=ALU.is_ge, fill=0.0, base=0,
                                   pattern=[[1, P]], channel_multiplier=-1))
            pin(pool.memset(negtri[:], 0.0))
            pin(pool.affine_select(out=negtri[:], in_=negtri[:], compare_op=ALU.is_ge, fill=NEG, base=0,
                                   pattern=[[-1, P]], channel_multiplier=1))
            pin(pool.memset(selx[:], 1.0))
            pin(pool.affine_select(out=selx[:], in_=selx[:], compare_op=ALU.is_ge, fill=0.0, base=0,
                                   pattern=[[-3, GF]], channel_multiplier=1))
            pin(pool.affine_select(out=selx[:], in_=selx[:], compare_op=ALU.is_ge, fill=0.0, base=2,
                                   pattern=[[3, GF]], channel_multiplier=-1))
            pool.tensor_tensor(seld[:], selx[:, 0:GF:2], selx[:, 1:GF:2], ALU.subtract).then_inc(sel_ready, 1)
            pool.memset(xnT[:, 0:4], 0.0).then_inc(consts, 1)

            if LAYERS > 1:
                pool.wait_ge(x_ready, 1)
                pin(pool.memset(Hst[:, 0, :], 0.0))
                pool.wait_ge(decay_ready, 2)
                pool.wait_ge(xs_ready, T)
                for c in range(T):
                    if c >= 2:
                        pool.wait_ge(y_ps, c - 1)
                    dtv = small[:, 0, c * NH:(c + 1) * NH]
                    dcv = small[:, 6, c * NH:(c + 1) * NH]
                    v = xdt[:, c % 2, :].rearrange("p (h q) -> p h q", h=NH)
                    pin(pool.tensor_tensor(v, xs[:, c, 0:DIN].rearrange("p (h q) -> p h q", h=NH), bcast(dtv, HD), ALU.mult))
                    pool.tensor_tensor(xdd[:, c % 2, :].rearrange("p (h q) -> p h q", h=NH), v, bcast(dcv, HD),
                                       ALU.mult).then_inc(xdt_ready, 1)

            def max_over_tokens(a):
                pool.wait_ge(a["smax_ready"], 1)
                pool.partition_all_reduce(a["S"], a["smax"], P, bass.bass_isa.ReduceOp.max).then_inc(a["S_ready"], 1)
            if LAYERS > 2:
                max_over_tokens(A1)
            if LAYERS > 6:
                max_over_tokens(A3)

            def tropical():
                def pair(j, slot):
                    pool.wait_ge(rise_pool, j * 2 + 1)
                    pool.tensor_tensor(rise0, rise0, oddc[:, slot, :], ALU.add).then_inc(sum_ready, 1)
                    pool.wait_ge(rise_pool, j * 2 + 2)
                    pool.tensor_tensor(rise1[:, slot, :], rise1[:, slot, :], oddc[:, slot, :], ALU.add).then_inc(sum_ready, 1)
                with pool.Fori(0, D // 4) as i:
                    for s in range(2):
                        pair(i * 2 + s, s)
                for f in range(FT):
                    pool.wait_ge(trop_mix, f + 1)
                    pool.wait_ge(gt_ready, NB * (f + 1))
                    pin(pool.tensor_tensor(cvx, cvx, CL, ALU.subtract))
                    pin(pool.tensor_tensor(cvx, cvx, G, ALU.mult))
                    pool.tensor_tensor(acc[:, f, :], cvx, CL, ALU.add).then_inc(fused_ready, 1)
            if LAYERS > 7:
                tropical()

        @block.tensor
        def _(pe):
            mm, tr = pe.matmul, pe.transpose

            def norm_transposes(q):
                for t in range(T):
                    pe.wait_ge(xn_ready, T * q + t + 1)
                    i = tr(ps[:, t // 4, (t % 4) * P:(t % 4 + 1) * P], xn[:, t, :], ident[:])
                    if t % 4 == 3:
                        i.then_inc(xnT_ps, 1)

            def tok(t):
                return XT[:, t * P:(t + 1) * P]

            pe.wait_ge(consts, 2)
            pe.wait_ge(w_loaded, 16 * N_W)
            norm_transposes(0)
            pe.wait_ge(xnT_ready, NB)
            for t in range(T):
                if t >= 4:
                    pe.wait_ge(v0_ready, t - 3)
                mm(ps[:, 4 + t % 4, 0:D], tok(t), W["W0T"][:], start=True, stop=True).then_inc(v0_ps, 1)
            pe.wait_ge(xp0_ready, 1)
            for half in range(2):
                if half:
                    pe.wait_ge(agg_read, 8)
                for jt in range(T):
                    pe.wait_ge(mask_ready, jt + 1)
                    for i in range(8):
                        m = mm(ps[:, i, 0:3 * D + 1], mask[:, jt, (half * 8 + i) * P:(half * 8 + i + 1) * P],
                               XP0[:, jt, 0:3 * D + 1], start=(jt == 0), stop=(jt == T - 1))
                        if jt == T - 1:
                            m.then_inc(agg_ps, 1)

            def mamba():
                norm_transposes(1)
                for k in range(2):
                    i = mm(ps[:, 4, k * P:(k + 1) * P], W["woutT"][:, k * P:(k + 1) * P], W["wlin"][:],
                           start=True, stop=True, skip_group_check=True)
                i.then_inc(wol_ps, 1)
                pe.wait_ge(xnT_ready, 2 * NB)
                pe.wait_ge(wk_ready, 1)
                pe.wait_ge(wol_ready, 1)
                for c in range(T):
                    if c >= 2:
                        pe.wait_ge(xs_ready, c - 1)
                    for k in range(KC):
                        mm(ps[:, c % 2, 0:XB], xnT[:, 1 + c * P + k:1 + c * P + k + P], wk[:, k, 0:XB], start=(k == 0), stop=False)
                    mm(ps[:, c % 2, 0:XB], ones[0:1, :], W["convb_row"][:], start=False, stop=True).then_inc(xb_ps, 1)
                    if c >= 2:
                        pe.wait_ge(z_read, c - 1)
                        pe.wait_ge(dt_read, c - 1)
                    mm(ps[:, 2 + c % 2, 0:DIN + NH], tok(c), W["win"][:, 0:DIN + NH], start=True, stop=True).then_inc(z_ps, 1)
                for g in range(2):
                    for b in range(NB):
                        n = g * NB + b
                        if n >= 4:
                            pe.wait_ge(bcT_ready, n - 3)
                        for k in range(KC):
                            i = mm(ps[0:DST, 4 + n % 4, :], wk[:, k, DIN + g * DST:DIN + (g + 1) * DST],
                                   xnT[:, 1 + b * BLK + k:1 + b * BLK + k + BLK], start=(k == 0), stop=(k == KC - 1))
                        i.then_inc(bcT_ps, 1)
                pe.wait_ge(dA_ready, 1)
                pe.wait_ge(xs_ready, T)
                dA = small[:, 1, :]
                mm(ps[:, 0, 0:T * NH], upper[:], dA, start=True, stop=True, skip_group_check=True)
                mm(ps[:, 0, T * NH:2 * T * NH], ones[:], dA, start=True, stop=True, skip_group_check=True).then_inc(acum_ps, 1)
                pe.wait_ge(acum_ready, 1)
                pe.wait_ge(bcT_ready, 2 * NB)
                pe.wait_ge(DI_ready, 1)
                def rows(c):
                    pe.wait_ge(rowin_ready, c + 1)
                    if c >= 2:
                        pe.wait_ge(M_ready, c - 1)
                    for h in range(NH):
                        i = tr(ps[:, c % 2, h * P:(h + 1) * P], rowin[:, c % 2, h, :], ident[:])
                    i.then_inc(row_ps, 1)
                    mm(ps[:, 2 + c % 2, 0:P], BT[:, c * P:(c + 1) * P], CT[:, c * P:(c + 1) * P],
                       start=True, stop=True).then_inc(G_ps, 1)
                rows(0)
                for c in range(T):
                    if c + 1 < T:
                        rows(c + 1)
                    pe.wait_ge(M_ready, c + 1)
                    pe.wait_ge(xdt_ready, c + 1)
                    if c:
                        pe.wait_ge(h_ready, c)
                        pe.wait_ge(y_done, c)
                    for h in range(NH):
                        mm(ps[:, 4, h * HD:(h + 1) * HD], EM[:, c % 2, h, :], xdt[:, c % 2, h * HD:(h + 1) * HD],
                           start=True, stop=False, skip_group_check=True)
                        mm(ps[:, 4, h * HD:(h + 1) * HD], DI[:, h, :], xs[:, c, h * HD:(h + 1) * HD],
                           start=False, stop=True, skip_group_check=True)
                    mm(ps[:, 5, 0:DIN], CT[:, c * P:(c + 1) * P], Hst[:, c % 2, :], start=True, stop=True)
                    mm(ps[0:DST, 6, 0:DIN], xs[:, c, DIN:XB], xdd[:, c % 2, :], start=True, stop=True).then_inc(y_ps, 1)
                pe.wait_ge(y_done, T)
                for c in range(T + 1):
                    if c < T:
                        if c >= 2:
                            pe.wait_ge(yT_ready, c - 1)
                        for k in range(2):
                            i = tr(ps[:, c % 2, k * P:(k + 1) * P], sz[:, c, k * P:(k + 1) * P], ident[:])
                        i.then_inc(yT_ps, 1)
                    if c >= 1:
                        e = c - 1
                        pe.wait_ge(yT_ready, e + 1)
                        if e >= 2:
                            pe.wait_ge(mo_read, e - 1)
                        for k in range(2):
                            i = mm(ps[:, 2 + e % 2, 0:D], yT[:, e % 2, k, :], wol[:, k, :], start=(k == 0), stop=(k == 1))
                        i.then_inc(mo_ps, 1)
            if LAYERS > 1:
                mamba()

            def attention(a, q, wv, nv):
                heads, w1, ring = a["heads"], a["w1"], a["ring"]
                pe.wait_ge(x_ready, q)
                if q == 2:
                    for k, (w, av) in enumerate((("W1n", "A1"), ("W2n", "A2"))):
                        mm(ps[:, 4, 2 * k:2 * k + 2], W[w][:], W[av][:], start=True, stop=True, skip_group_check=True)
                        i = mm(ps[:, 4, 4 + 2 * k:6 + 2 * k], W["b12"][:, k:k + 1].broadcast_to([P, P]), W[av][:],
                               start=True, stop=True, skip_group_check=True)
                else:
                    i = mm(ps[:, 4, 0:2], W["W3WT"][:], W["a3"][:], start=True, stop=True)
                i.then_inc(a["u_ps"], 1)
                norm_transposes(q)
                pe.wait_ge(xnT_ready, NB * (q + 1))
                pe.wait_ge(a["u_ready"], 1)
                for t in range(T):
                    if t >= 4:
                        pe.wait_ge(a["v_ready"], t - 3)
                    mm(ps[:, 4 + t % 4, 0:nv], tok(t), wv[:], start=True, stop=True).then_inc(a["v_ps"], 1)
                pe.wait_ge(a["v_ready"], T)
                for h in range(heads):
                    if h:
                        pe.wait_ge(a["row_ready"], NB * h)
                    for t in range(T):
                        i = tr(ps[:, t // 4, (t % 4) * P:(t % 4 + 1) * P],
                               a["VS"][:, t, D + h:D + h + 1].broadcast_to([P, P]), ident[:])
                        if t % 4 == 3:
                            i.then_inc(a["row_ps"], 1)
                pe.wait_ge(a["row_ready"], NB * heads)
                n = 0
                for k in range(heads * NB):
                    h = k // NB
                    if k >= a["sets"]:
                        pe.wait_ge(a["acc_read"], k - a["sets"] + 1)
                    if k % NB == 0:
                        pe.wait_ge(a["xp_ready"], h + 1)
                    for jt in range(T):
                        pe.wait_ge(a["m_ready"], n + 1)
                        for i in range(4):
                            for s, M in enumerate((a["M1"], a["M2"])):
                                bank = (k % a["sets"]) * 4 * a["banks"] + i * a["banks"] + (s if a["banks"] == 2 else 0)
                                col = s * 3 * w1 if a["banks"] == 1 else 0
                                m = mm(ps[:, bank, col:col + 3 * w1], M[:, n % ring, i * P:(i + 1) * P],
                                       a["XP"][h][:, jt, s, :, :].rearrange("p k c -> p (k c)"),
                                       start=(jt == 0 and (s == 0 or a["banks"] == 2)), stop=(jt == T - 1), skip_group_check=True)
                        m.then_inc(a["m_used"], 1)
                        n += 1
            if LAYERS > 2:
                attention(A1, 2, W["WVu"], D + 4)

            def experts():
                norm_transposes(3)
                pe.wait_ge(xnT_ready, NB * 4)
                for t in range(T):
                    i = mm(ps[:, 4, t * E1:(t + 1) * E1], tok(t), W["wg"][:], start=True, stop=True, skip_group_check=True)
                i.then_inc(g_ps, 1)
                pe.wait_ge(emask_ready, 1)
                for t in range(T):
                    i = tr(ps[0:E1, t // 4, (t % 4) * P:(t % 4 + 1) * P], emask[:, t, :], ident[:])
                    if t % 4 == 3:
                        i.then_inc(emT_ps, 1)
                pe.wait_ge(emT_ready, NB)
                pe.wait_ge(w2e_loaded, 16)
                n_up = n_dn = 0
                units = [(b, e) for b in range(NB) for e in range(E1)]

                def up(u):
                    b, e = units[u]
                    for k in range(2):
                        n = 2 * u + k
                        if n >= 4:
                            pe.wait_ge(h1_ready, n - 3)
                        mm(ps[:, n % 4, :], W["w1e"][:, (2 * e + k) * P:(2 * e + k + 1) * P],
                           XT[:, b * BLK:(b + 1) * BLK], start=True, stop=True).then_inc(h1_ps, 1)

                def down(u):
                    b, e = units[u]
                    pe.wait_ge(h1_ready, 2 * u + 2)
                    if e == 0:
                        if b >= 2:
                            pe.wait_ge(o1_read, (b - 1) * (E1 + 1) - E1)
                        for i in range(4):
                            t = 4 * b + i
                            m = mm(ps[:, 6 + b % 2, i * D:(i + 1) * D], emT[:, t * P:(t + 1) * P], W["b2r"][:],
                                   start=True, stop=True, skip_group_check=True)
                        m.then_inc(o1_ps, 1)
                    prior = u + b + 1 if e else u + b + 1
                    if u >= 2:
                        pe.wait_ge(o1_read, (u - 2) + (u - 2) // E1 + 2)
                    for i in range(4):
                        for k in range(2):
                            m = mm(ps[:, 4 + u % 2, i * D:(i + 1) * D], hT1[:, u % 4, k, i * P:(i + 1) * P],
                                   w2e[:, 2 * e + k, :], start=(k == 0), stop=(k == 1), skip_group_check=True)
                    m.then_inc(o1_ps, 1)
                up(0)
                for u in range(len(units)):
                    if u + 1 < len(units):
                        up(u + 1)
                    down(u)
            if LAYERS > 3:
                experts()

            def cosine():
                norm_transposes(4)
                pe.wait_ge(xnT_ready, NB * 5)
                for t in range(T):
                    if t >= 4:
                        pe.wait_ge(kq_read, t - 3)
                    mm(ps[:, 4 + t % 4, 0:D], tok(t), W["wkT"][:], start=True, stop=True, skip_group_check=True)
                    mm(ps[:, 4 + t % 4, D:2 * D], tok(t), W["wqT"][:], start=True, stop=True,
                       skip_group_check=True).then_inc(kq_ps, 1)
                for b in range(NB):
                    mm(ps[:, b, :], W["wqT"][:], XT[:, b * BLK:(b + 1) * BLK], start=True, stop=True).then_inc(QT_ps, 1)
                pe.wait_ge(QT_ready, NB)
                for t in range(T):
                    pe.wait_ge(kn_ready, 1)
                    i = tr(ps[:, t // 4, (t % 4) * P:(t % 4 + 1) * P], Kt[:, t, :], ident[:])
                    if t % 4 == 3:
                        i.then_inc(KnT_ps, 1)
                pe.wait_ge(KnT_ready, NB)
                pe.wait_ge(xn1_ready, 1)
                pe.wait_ge(kq_read, T)
                items = [(b, jt) for b in range(NB) for jt in range(T)]

                def score(n):
                    b, jt = items[n]
                    if n >= 2:
                        pe.wait_ge(sc_exp, n - 1)
                    mm(ps[:, n % 2, :], QT[:, jt * P:(jt + 1) * P], KnT[:, b * BLK:(b + 1) * BLK],
                       start=True, stop=True).then_inc(sc_ps, 1)

                def apply(n):
                    b, jt = items[n]
                    pe.wait_ge(p_ready, n + 1)
                    if jt == 0 and b:
                        pe.wait_ge(a2_read, b)
                    for i in range(4):
                        m = mm(ps[:, 2 + i, 0:D + 1], Er[:, n % RE, i * P:(i + 1) * P], xn1[:, jt, :],
                               start=(jt == 0), stop=(jt == T - 1))
                    m.then_inc(p_used, 1)
                score(0)
                score(1)
                for n in range(len(items)):
                    if n + 2 < len(items):
                        score(n + 2)
                    apply(n)
            if LAYERS > 4:
                cosine()

            def depths():
                norm_transposes(5)
                pe.wait_ge(xnT_ready, NB * 6)
                for t in range(T):
                    i = mm(ps[:, 4, t:t + 1], tok(t), W["wr"][:], start=True, stop=True, skip_group_check=True)
                i.then_inc(w_ps, 1)
                pe.wait_ge(wcol_ready, 1)
                for t in range(T):
                    i = tr(ps[:, t // 4, (t % 4) * P:(t % 4 + 1) * P], wcol[:, t:t + 1].broadcast_to([P, P]), ident[:])
                    if t % 4 == 3:
                        i.then_inc(wrow_ps, 1)
                pe.wait_ge(wrow_ready, NB)
                HTILES = H2 // P

                def up(b):
                    for k in range(HTILES):
                        n = b * HTILES + k
                        if n >= 4:
                            pe.wait_ge(h2_ready, n - 3)
                        mm(ps[:, n % 4, :], W["w1m"][:, k * P:(k + 1) * P], XT[:, b * BLK:(b + 1) * BLK],
                           start=True, stop=True).then_inc(h2_ps, 1)

                def down(b):
                    pe.wait_ge(h2_ready, (b + 1) * HTILES)
                    for i in range(4):
                        t = 4 * b + i
                        if t >= 4:
                            pe.wait_ge(o2_read, t - 3)
                        for k in range(HTILES):
                            m = mm(ps[:, 4 + t % 4, 0:D], hT2[:, b % 2, k, i * P:(i + 1) * P], W["w2m"][:, k, :],
                                   start=(k == 0), stop=(k == HTILES - 1))
                        m.then_inc(o2_ps, 1)
                up(0)
                for b in range(NB):
                    if b + 1 < NB:
                        up(b + 1)
                    down(b)
            if LAYERS > 5:
                depths()
            if LAYERS > 6:
                attention(A3, 6, W["WVu3"], D + 2)

            def tropical():
                norm_transposes(7)
                pe.wait_ge(xg_in, 16 * 3 * NG)
                pe.wait_ge(sel_ready, 1)

                def spread(bank, sel, g, half, stop=True):
                    for b in range(2):
                        c = half * 2 + b
                        m = mm(ps[:, bank + b, :], sel.broadcast_to([3 * GF, P]), xg[:, g, c * BLK:(c + 1) * BLK],
                               start=True, stop=stop)
                    return m

                def add(bank, src):
                    for b in range(2):
                        m = mm(ps[:, bank + b, :], ident[:], src[:, b * BLK:(b + 1) * BLK], start=False, stop=True)
                    return m

                def pair(j, i, g, first=False):
                    even, odd, diff = selx[:, bass.ds(i * 2, 1)], selx[:, bass.ds(i * 2 + 1, 1)], seld[:, bass.ds(i, 1)]
                    if not first:
                        pe.wait_ge(pair_step, j * 3 - 1)
                    spread(4, odd, g, 0).then_inc(odd_ps, 1)
                    if not first:
                        pe.wait_ge(pair_step, j * 3)
                    spread(6, odd, g, 1).then_inc(odd_ps, 1)
                    if not first:
                        pe.wait_ge(rise_pool, j * 2)
                    spread(0, diff, g, 0).then_inc(diff_ps, 1)
                    spread(2, diff, g, 1).then_inc(diff_ps, 1)
                    pe.wait_ge(odd_copied, j * 2 + 1)
                    spread(4, even, g, 0).then_inc(even_ps, 1)
                    pe.wait_ge(odd_copied, j * 2 + 2)
                    spread(6, odd, g, 0, stop=False)
                    pe.wait_ge(rise_pe, j * 3 + 1)
                    add(6, rise_m[:, 0:N // 2]).then_inc(pair_ps, 1)
                    pe.wait_ge(single_step, j * 2 + 1)
                    spread(4, odd, g, 1, stop=False)
                    pe.wait_ge(rise_pe, j * 3 + 2)
                    add(4, rise_m[:, N // 2:N]).then_inc(pair_ps, 1)
                    pe.wait_ge(pair_step, j * 3 + 1)
                    spread(6, odd, g, 1, stop=False)
                    pe.wait_ge(rise_pe, j * 3 + 3)
                    add(6, rise_m[:, N:]).then_inc(pair_ps, 1)
                for g in range(NG):
                    if g == 0:
                        pair(0, 0, 0, first=True)
                    with pe.Fori(int(g == 0), GF // 2) as i:
                        pair(i + g * (GF // 2), i, g)
                for f in range(FT):
                    for g, w in enumerate(("Wc", "Wg")):
                        if f:
                            pe.wait_ge(cl_ready if g == 0 else gt_ready, NB * f)
                        elif g == 0:
                            pe.wait_ge(pair_step, 3 * D // 2)
                            pe.wait_ge(rise_pool, D)
                        for b in range(NB):
                            mm(ps[:, 4 * g + b, :], W[w][:, f * P:(f + 1) * P], XT[:, b * BLK:(b + 1) * BLK],
                               start=True, stop=True).then_inc(cl_ps, 1)
                pe.wait_ge(fused_ready, FT)
                pe.wait_ge(cl_ready, NB * FT)
                pe.wait_ge(gt_ready, NB * FT)
                for t in range(T):
                    if t >= 8:
                        pe.wait_ge(x_ready, 7 + t - 7)
                    for f in range(FT):
                        m = mm(ps[:, t % 8, 0:D], acc[:, f, t * P:(t + 1) * P], W["Wd"][:, f, :], start=(f == 0), stop=(f == FT - 1))
                    m.then_inc(f_ps, 1)
            if LAYERS > 7:
                tropical()

        @block.scalar
        def _(act):
            A = act.activation

            def ain(i):
                in_turn(act, "act", act_step, i)

            for jt in range(4):
                act.dma_start(stage_adj[:, jt, :], ins["adjT"][jt * P:(jt + 1) * P, :]).then_inc(adj_in[jt], 16)

            def norm(q):
                act.wait_ge(var_ready, q + 1)
                A(lnv[:, 1, :], lnv[:, 0, :], ACT.Sqrt).then_inc(sqrt_ready, 1)
                for b in range(NB):
                    act.wait_ge(xnT_ps, NB * q + b + 1)
                    A(XT[:, b * BLK:(b + 1) * BLK], ps[:, b, :], ACT.Copy).then_inc(xnT_ready, 1)
            norm(0)

            def mamba():
                norm(1)
                act.wait_ge(wol_ps, 1)
                for k in range(2):
                    i = A(wol[:, k, :], ps[:, 4, k * P:(k + 1) * P], ACT.Copy, scale=W["nw"][:, k:k + 1])
                i.then_inc(wol_ready, 1)
                for c in range(T):
                    act.wait_ge(xb_ps, c + 1)
                    A(xs[:, c, :], ps[:, c % 2, 0:XB], ACT.Silu).then_inc(xs_ready, 1)
                    act.wait_ge(z_ps, c + 1)
                    A(small[:, 0, c * NH:(c + 1) * NH], ps[:, 2 + c % 2, DIN:DIN + NH], ACT.Copy).then_inc(dt_read, 1)
                    A(sz[:, c, :], ps[:, 2 + c % 2, 0:DIN], ACT.Silu).then_inc(z_read, 1)
                for g, dst in enumerate((BT, CT)):
                    for b in range(NB):
                        n = g * NB + b
                        act.wait_ge(bcT_ps, n + 1)
                        A(dst[:, b * BLK:(b + 1) * BLK], ps[0:DST, 4 + n % 4, :], ACT.Silu,
                          bias=W["convb_bc"][:, g:g + 1]).then_inc(bcT_ready, 1)
                A(Aneg, W["alog"][:], ACT.Exp).then_inc(alog_exp, 1)
                act.wait_ge(sp_e_ready, 1)
                A(small[:, 3, :], small[:, 2, :], ACT.Exp).then_inc(sp_exp, 1)
                act.wait_ge(sp_u_ready, 1)
                A(small[:, 5, :], small[:, 4, :], ACT.Ln).then_inc(sp_ln, 1)
                act.wait_ge(acum_ready, 1)
                A(small[:, 6:8, :], small[:, 6:8, :], ACT.Exp).then_inc(decay_ready, 1)
                A(small[:, 8, :], small[:, 9, :], ACT.Exp).then_inc(decay_ready, 1)
                for c in range(T):
                    act.wait_ge(row_ps, c + 1)
                    if c >= 2:
                        act.wait_ge(y_ps, c - 1)
                    for h in range(NH):
                        i = A(EM[:, c % 2, h, :], ps[:, c % 2, h * P:(h + 1) * P], ACT.Exp,
                              bias=small[:, 10, c * NH + h:c * NH + h + 1])
                    i.then_inc(E_ready, 1)
                act.wait_ge(y_done, T)
                for c in range(T):
                    ain(A(yscr[:, 0, :], sz[:, c, :], ACT.Square, accum_out=small[:, 11, c:c + 1]))
                A(small[:, 11, T:2 * T], small[:, 11, 0:T], ACT.Copy).then_inc(sq_done, 1)
                act.wait_ge(yrms_var, 1)
                A(small[:, 11, 2 * T:3 * T], small[:, 11, T:2 * T], ACT.Sqrt).then_inc(yrms_sqrt, 1)
                for c in range(T):
                    act.wait_ge(yT_ps, c + 1)
                    if c >= 2:
                        act.wait_ge(mo_ps, c - 1)
                    A(yT[:, c % 2, :, :].rearrange("p k n -> p (k n)"), ps[:, c % 2, 0:2 * P], ACT.Copy).then_inc(yT_ready, 1)
            if LAYERS > 1:
                mamba()

            def attention(a, q):
                norm(q)
                act.wait_ge(a["arg_ready"], 1)
                A(a["ex"].rearrange("p k h t -> p (k h t)"), a["arg"].rearrange("p k h t -> p (k h t)"), ACT.Exp).then_inc(a["ex_ready"], 1)
                for h in range(a["heads"]):
                    for b in range(NB):
                        act.wait_ge(a["row_ps"], h * NB + b + 1)
                        A(a["row"][h][:, b * BLK:(b + 1) * BLK], ps[:, b, :], ACT.Copy).then_inc(a["row_ready"], 1)
            if LAYERS > 2:
                attention(A1, 2)

            def experts():
                norm(3)
                for b in range(NB):
                    act.wait_ge(emT_ps, b + 1)
                    A(emT[:, b * BLK:(b + 1) * BLK], ps[0:E1, b, :], ACT.Copy).then_inc(emT_ready, 1)
                for u in range(NB * E1):
                    e = u % E1
                    if u >= 4:
                        act.wait_ge(o1_ps, (u - 4) + (u - 4) // E1 + 2)
                    for k in range(2):
                        n = 2 * u + k
                        act.wait_ge(h1_ps, n + 1)
                        A(hT1[:, u % 4, k, :], ps[:, n % 4, :], ACT.Gelu, bias=W["b1c"][:, 2 * e + k:2 * e + k + 1]).then_inc(h1_ready, 1)
            if LAYERS > 3:
                experts()

            def cosine():
                norm(4)
                for b in range(NB):
                    act.wait_ge(QT_ps, b + 1)
                    A(QT[:, b * BLK:(b + 1) * BLK], ps[:, b, :], ACT.Copy).then_inc(QT_ready, 1)
                act.wait_ge(norm_sq, 1)
                A(qs[:, 2:4, :], qs[:, 0:2, :], ACT.Sqrt).then_inc(norm_sqrt, 1)
                for b in range(NB):
                    act.wait_ge(KnT_ps, b + 1)
                    A(KnT[:, b * BLK:(b + 1) * BLK], ps[:, b, :], ACT.Copy).then_inc(KnT_ready, 1)
                for n in range(NB * T):
                    jt = n % T
                    act.wait_ge(sc_ps, n + 1)
                    if n >= RE:
                        act.wait_ge(p_used, n - RE + 1)
                    A(Er[:, n % RE, :], ps[:, n % 2, :], ACT.Exp, scale=qs[:, 5, jt:jt + 1]).then_inc(sc_exp, 1)
            if LAYERS > 4:
                cosine()

            def depths():
                norm(5)
                for b in range(NB):
                    act.wait_ge(wrow_ps, b + 1)
                    A(wrow[:, b * BLK:(b + 1) * BLK], ps[:, b, :], ACT.Copy).then_inc(wrow_ready, 1)
                for n in range(NB * (H2 // P)):
                    b, k = divmod(n, H2 // P)
                    act.wait_ge(h2_ps, n + 1)
                    if b >= 2 and k == 0:
                        act.wait_ge(o2_ps, 4 * (b - 1))
                    A(hT2[:, b % 2, k, :], ps[:, n % 4, :], ACT.Gelu_apprx_tanh, bias=W["b1m"][:, k:k + 1]).then_inc(h2_ready, 1)
            if LAYERS > 5:
                depths()
            if LAYERS > 6:
                attention(A3, 6)
                act.wait_ge(elu_ready, 1)
                A(elu_m, elu_m, ACT.Exp).then_inc(elu_exp, 1)

            def tropical():
                norm(7)
                A(sa[:, 0, :], W["alpha"][:], ACT.Sigmoid).then_inc(sa_ready, 1)

                act.wait_ge(rise_table, 1)

                def pair(j, slot, before=2):
                    A(bias[:, slot, :], rise[:, bass.ds(j, 1), :].rearrange("p o k -> p (o k)"), ACT.Copy).then_inc(bias_ready, 1)
                    if before > 1:
                        act.wait_ge(sum_ready, j * 2 - 2)
                    for n in range(2):
                        h = slice(n * N // 2, (n + 1) * N // 2)
                        act.wait_ge(odd_ps, j * 2 + (n + 1))
                        A(oddc[:, slot, h], ps_wide[:, 1, h], ACT.Copy).then_inc(odd_copied, 1)
                    act.wait_ge(bias_ready, j + 1)
                    for n, (f, half) in enumerate(((2, 0), (2, 1), (3, 1))):
                        if n < 2:
                            act.wait_ge(diff_ps, j * 2 + (n + 1))
                        A(rise_m[:, n * N // 2:(n + 1) * N // 2], ps_wide[:, 0, half * N // 2:(half + 1) * N // 2], ACT.Relu,
                          bias=bias[:, slot, f:f + 1]).then_inc(rise_pe, 1)
                    if before:
                        act.wait_ge(sum_step, j * 2 - 1)
                    A(rise0, ps_wide[:, 0, :], ACT.Relu, bias=bias[:, slot, 0:1]).then_inc(rise_pool, 1)
                    A(rise1[:, slot, :], ps_wide[:, 0, :], ACT.Relu, bias=bias[:, slot, 1:2]).then_inc(rise_pool, 1)
                pair(0, 0, before=0)
                pair(1, 1, before=1)
                with act.Fori(1, D // 4) as i:
                    for s in range(2):
                        pair(i * 2 + s, s)
                n = 0
                for f in range(FT):
                    if f:
                        act.wait_ge(fused_ready, f)
                    for b in range(NB):
                        act.wait_ge(cl_ps, 8 * f + b + 1)
                        A(CL[:, b * BLK:(b + 1) * BLK], ps[:, b, :], ACT.Gelu, bias=W["bc"][:, f:f + 1]).then_inc(cl_ready, 1)
                    for b in range(NB):
                        act.wait_ge(cl_ps, 8 * f + NB + b + 1)
                        A(G[:, b * BLK:(b + 1) * BLK], ps[:, 4 + b, :], ACT.Sigmoid, bias=W["bgt"][:, f:f + 1]).then_inc(gt_ready, 1)
                    act.wait_ge(z_ready, f + 1)
                    for sl, of in (("slx", "ofx"), ("slc", "ofc")):
                        for p in range(PP):
                            if n >= 4:
                                act.wait_ge(af_used, n - 3)
                            A(AF[n % 4], acc[:, f, :], ACT.Identity, bias=W[of][:, f, p:p + 1],
                              scale=W[sl][:, f, p:p + 1]).then_inc(af_ready, 1)
                            n += 1
            if LAYERS > 7:
                tropical()

        @block.vector
        def _(dve):
            V = nc.vector

            def din(i):
                in_turn(dve, "dve", dve_step, i)

            def newton_rsqrt(v, s, r, tmp):
                din(V.reciprocal(r, s))
                din(V.tensor_tensor(tmp, v, r, ALU.mult))
                din(V.tensor_tensor(tmp, tmp, s, ALU.add))
                din(V.tensor_scalar(tmp, tmp, 0.5, None, ALU.mult))
                din(V.reciprocal(r, tmp))

            def norm(q):
                if DEBUG and q:
                    dve.wait_ge(dbg_done, 16 * q)
                for t in range(T):
                    i = V.bn_stats(stats[:, t, :], x[:, t, :])
                din(i)
                for t in range(T):
                    i = V.bn_aggr(mv[:, t, :], stats[:, t, :])
                din(i)
                V.tensor_scalar(lnv[:, 0, :], mv[:, :, 1], EPS, None, ALU.add).then_inc(var_ready, 1)
                dve.wait_ge(sqrt_ready, q + 1)
                newton_rsqrt(lnv[:, 0, :], lnv[:, 1, :], lnv[:, 2, :], lnv[:, 3, :])
                for t in range(T):
                    V.tensor_scalar(xn[:, t, :], x[:, t, :], mv[:, t, 0:1], lnv[:, 2, t:t + 1], ALU.subtract, ALU.mult).then_inc(xn_ready, 1)

            def split3(hi, mid, lo, src):
                din(V.tensor_copy(hi, src))
                din(V.tensor_tensor(src, src, hi, ALU.subtract))
                din(V.tensor_copy(mid, src))
                din(V.tensor_tensor(lo, src, mid, ALU.subtract))

            dve.wait_ge(x_loaded, 16)
            norm(0)
            dve.wait_ge(w_loaded, 16 * N_W)
            for t in range(T):
                dve.wait_ge(v0_ps, t + 1)
                V.tensor_copy(V0[:, t, :], ps[:, 4 + t % 4, 0:D]).then_inc(v0_ready, 1)
            dve.wait_ge(v0_ready, T)
            split3(XP0[:, :, 0:D], XP0[:, :, D:2 * D], XP0[:, :, 2 * D:3 * D], V0)
            V.memset(XP0[:, :, 3 * D:3 * D + 2], 1.0).then_inc(xp0_ready, 1)
            din(V.tensor_tensor(x[:, :, :], x[:, :, :], W["b0"][:].unsqueeze(1).broadcast_to([P, T, D]), ALU.add))
            for jt in range(T):
                dve.wait_ge(adj_in[jt % 4], 16 * (jt // 4 + 1))
                V.tensor_scalar(mask[:, jt, :], stage_adj[:, jt % 4, :], 1.0, None, ALU.is_equal).then_inc(mask_ready, 1)
            for t in range(T):
                dve.wait_ge(agg_ps, t + 1)
                pv = ps[:, t % 8, 0:3 * D].rearrange("p (k d) -> p d k", k=3)
                V.tensor_copy(deg[:, t:t + 1], ps[:, t % 8, 3 * D:3 * D + 1])
                din(V.tensor_reduce(R0[:, t % 8, :], pv, AX, ALU.add))
                din(V.reciprocal(rdeg[:, t:t + 1], deg[:, t:t + 1]))
                i = V.scalar_tensor_tensor(x[:, t, :], R0[:, t % 8, :], rdeg[:, t:t + 1], x[:, t, :], ALU.mult, ALU.add)
                i.then_inc(agg_read if t < T - 1 else x_ready, 1)
            dve.wait_ge(x_ready, 1)

            def mamba():
                norm(1)
                dve.wait_ge(cw_loaded, 16)
                V.tensor_tensor(wk, cwb, W["win"][:, DIN + NH:].unsqueeze(1).broadcast_to([P, KC, DIN + 2 * DST]), ALU.mult).then_inc(wk_ready, 1)
                for h in range(NH):
                    i = V.tensor_scalar(DI[:, h, :], ident[:], W["Dh"][:, h:h + 1], None, ALU.mult)
                i.then_inc(DI_ready, 1)
                dve.wait_ge(dt_read, T)
                v = [small[:, k, :] for k in range(12)]

                def h4(u):
                    return u.rearrange("p (c h) -> p c h", h=NH)
                din(V.tensor_tensor(h4(v[0]), h4(v[0]), W["dtb"][:].unsqueeze(1).broadcast_to([P, T, NH]), ALU.add))
                din(V.tensor_scalar(v[1], v[0], -1.0, None, ALU.mult))
                V.tensor_tensor(v[2], v[0], v[1], ALU.min).then_inc(sp_e_ready, 1)
                dve.wait_ge(sp_exp, 1)
                V.tensor_scalar(v[4], v[3], 1.0, None, ALU.add).then_inc(sp_u_ready, 1)
                dve.wait_ge(sp_u_ready, 1)
                din(V.tensor_scalar(v[6], v[4], -1.0, None, ALU.add))
                din(V.tensor_tensor(v[3], v[3], v[6], ALU.subtract))
                din(V.reciprocal(v[7], v[4]))
                din(V.tensor_tensor(v[3], v[3], v[7], ALU.mult))
                dve.wait_ge(sp_ln, 1)
                din(V.tensor_tensor(v[5], v[5], v[3], ALU.add))
                din(V.scalar_tensor_tensor(v[0], v[0], 0.0, v[5], ALU.max, ALU.add))
                dve.wait_ge(alog_exp, 1)
                din(V.tensor_tensor(h4(v[1]), h4(v[0]), Aneg.unsqueeze(1).broadcast_to([P, T, NH]), ALU.mult))
                V.tensor_scalar(v[1], v[1], -1.0, None, ALU.mult).then_inc(dA_ready, 1)
                dve.wait_ge(dA_ready, 1)
                dve.wait_ge(acum_ps, 1)
                din(V.tensor_copy(v[9], ps[:, 0, 0:T * NH]))
                V.tensor_copy(v[7], ps[:, 0, T * NH:2 * T * NH])
                din(V.tensor_scalar(v[10], v[9], -1.0, None, ALU.mult))
                V.tensor_tensor(v[6], v[7], v[9], ALU.subtract).then_inc(acum_ready, 1)
                dve.wait_ge(decay_ready, 2)

                def rowin_of(c):
                    if c >= 2:
                        dve.wait_ge(row_ps, c - 1)
                    for h in range(NH):
                        i = V.tensor_scalar(rowin[:, c % 2, h, :], negtri[:], small[:, 9, c * NH + h:c * NH + h + 1], None, ALU.add)
                    i.then_inc(rowin_ready, 1)
                rowin_of(0)

                def weigh(c):
                    dve.wait_ge(E_ready, c + 1)
                    dve.wait_ge(G_ps, c + 1)
                    V.tensor_tensor(EM[:, c % 2, :, :], EM[:, c % 2, :, :],
                                    ps[:, 2 + c % 2, 0:P].unsqueeze(1).broadcast_to([P, NH, P]), ALU.mult).then_inc(M_ready, 1)
                for c in range(T):
                    if c + 1 < T:
                        rowin_of(c + 1)
                    weigh(c)
                    cd = small[0:DST, 7, c * NH:(c + 1) * NH]
                    ea = small[:, 8, c * NH:(c + 1) * NH]
                    hq = "p (h q) -> p h q"
                    dve.wait_ge(y_ps, c + 1)
                    if c + 1 < T:
                        Hn = Hst[:, (c + 1) % 2, :]
                        din(V.tensor_tensor(Hn.rearrange(hq, h=NH), Hst[:, c % 2, :].rearrange(hq, h=NH), bcast(cd, HD), ALU.mult))
                        V.tensor_tensor(Hn, Hn, ps[0:DST, 6, 0:DIN], ALU.add).then_inc(h_ready, 1)
                    din(V.tensor_tensor(yscr[:, 1, :].rearrange(hq, h=NH), ps[:, 5, 0:DIN].rearrange(hq, h=NH), bcast(ea, HD), ALU.mult))
                    din(V.tensor_tensor(yscr[:, 1, :], yscr[:, 1, :], ps[:, 4, 0:DIN], ALU.add))
                    V.tensor_tensor(sz[:, c, :], sz[:, c, :], yscr[:, 1, :], ALU.mult).then_inc(y_done, 1)
                dve.wait_ge(sq_done, 1)
                k = small[:, 11, :]
                V.tensor_scalar(k[:, T:2 * T], k[:, T:2 * T], 1.0 / DIN, EPS, ALU.mult, ALU.add).then_inc(yrms_var, 1)
                dve.wait_ge(yrms_sqrt, 1)
                newton_rsqrt(k[:, T:2 * T], k[:, 2 * T:3 * T], k[:, 3 * T:4 * T], k[:, 0:T])
                din(V.tensor_tensor(x[:, :, :], x[:, :, :], W["blin"][:].unsqueeze(1).broadcast_to([P, T, D]), ALU.add))
                for c in range(T):
                    dve.wait_ge(mo_ps, c + 1)
                    V.scalar_tensor_tensor(x[:, c, :], ps[:, 2 + c % 2, 0:D], k[:, 3 * T + c:3 * T + c + 1], x[:, c, :],
                                           ALU.mult, ALU.add).then_inc(mo_read if c < T - 1 else x_ready, 1)
                dve.wait_ge(x_ready, 2)
            if LAYERS > 1:
                mamba()

            def attention(a, q, nv):
                heads, dh, w1, ring, VS = a["heads"], a["dh"], a["w1"], a["ring"], a["VS"]
                dve.wait_ge(a["u_ps"], 1)
                if q == 2:
                    V.tensor_copy(W["WVu"][:, D:D + 4], ps[:, 4, 0:4])
                    i = V.tensor_copy(W["vbias"][:, D:D + 4], ps[:, 4, 4:8])
                else:
                    i = V.tensor_copy(W["WVu3"][:, D:D + 2], ps[:, 4, 0:2])
                i.then_inc(a["u_ready"], 1)
                norm(q)
                for t in range(T):
                    dve.wait_ge(a["v_ps"], t + 1)
                    if q == 2:
                        V.tensor_tensor(VS[:, t, :], ps[:, 4 + t % 4, 0:nv], W["vbias"][:], ALU.add).then_inc(a["v_ready"], 1)
                    else:
                        V.tensor_copy(VS[:, t, :], ps[:, 4 + t % 4, 0:nv]).then_inc(a["v_ready"], 1)
                dve.wait_ge(a["v_ready"], T)
                s1 = VS[:, :, D:D + heads].rearrange("p t h -> p h t")
                s2 = VS[:, :, D + heads:D + 2 * heads].rearrange("p t h -> p h t")
                V.tensor_reduce(a["smax"], s2, AX, ALU.max).then_inc(a["smax_ready"], 1)
                din(V.tensor_scalar(a["thr"], s2, -1.0, None, ALU.mult))
                dve.wait_ge(a["S_ready"], 1)
                Sb = bcast(a["S"], T)
                arg = a["arg"]
                din(V.tensor_tensor(arg[:, 0, :, :], s2, Sb, ALU.subtract))
                din(V.tensor_tensor(a["tt"], s1, Sb, ALU.add))
                din(V.tensor_scalar(arg[:, 1, :, :], arg[:, 0, :, :], 0.2, None, ALU.mult))
                din(V.scalar_tensor_tensor(a["cc"], a["tt"], 0.2, a["tt"], ALU.mult, ALU.max))
                din(V.tensor_tensor(arg[:, 2, :, :], a["tt"], a["cc"], ALU.subtract))
                V.scalar_tensor_tensor(arg[:, 3, :, :], a["tt"], 0.2, a["cc"], ALU.mult, ALU.subtract).then_inc(a["arg_ready"], 1)
                dve.wait_ge(a["ex_ready"], 1)
                ex = a["ex"]

                def values(h):
                    Fv, XP = a["Fv"], a["XP"][h]
                    for k in range(2):
                        V.tensor_tensor(Fv[:, :, k, 0:dh], VS[:, :, h * dh:(h + 1) * dh], bcast(ex[:, k, h, :], dh), ALU.mult)
                        i = V.tensor_copy(Fv[:, :, k, dh:w1], ex[:, k, h, :].unsqueeze(2))
                    din(i)
                    din(V.tensor_copy(XP[:, :, :, 0, :], Fv))
                    din(V.tensor_tensor(Fv, Fv, XP[:, :, :, 0, :], ALU.subtract))
                    din(V.tensor_copy(XP[:, :, :, 1, :], Fv))
                    V.tensor_tensor(XP[:, :, :, 2, :], Fv, XP[:, :, :, 1, :], ALU.subtract).then_inc(a["xp_ready"], 1)
                    dve.wait_ge(a["xp_ready"], h + 1)
                values(0)

                def masks(k, jt):
                    h, b = divmod(k, NB)
                    n = k * T + jt
                    if jt == 0:
                        dve.wait_ge(a["row_ready"], NB * h + b + 1)
                    if n >= ring:
                        dve.wait_ge(a["m_used"], n - ring + 1)
                    mk = mask[:, jt, b * BLK:(b + 1) * BLK]
                    din(V.scalar_tensor_tensor(a["M1"][:, n % ring, :], a["row"][h][:, b * BLK:(b + 1) * BLK],
                                               a["thr"][:, h, jt:jt + 1], mk, ALU.is_ge, ALU.mult))
                    V.tensor_tensor(a["M2"][:, n % ring, :], mk, a["M1"][:, n % ring, :], ALU.subtract).then_inc(a["m_ready"], 1)

                def evacuate(k):
                    h, b = divmod(k, NB)
                    dve.wait_ge(a["m_used"], (k + 1) * T)
                    base = (k % a["sets"]) * 4 * a["banks"]
                    for i in range(4):
                        if a["banks"] == 1:
                            m = V.tensor_reduce(a["R"][:, i, :, :], ps[:, base + i, 0:6 * w1].rearrange("p (s k c) -> p s c k", s=2, k=3), AX, ALU.add)
                        else:
                            for s in range(2):
                                m = V.tensor_reduce(a["R"][:, i, s, :], ps[:, base + 2 * i + s, 0:3 * w1].rearrange("p (k c) -> p c k", k=3), AX, ALU.add)
                    m.then_inc(a["acc_read"], 1)
                    dve.wait_ge(a["acc_read"], k + 1)
                    for s in range(2):
                        m = V.tensor_tensor(a["R"][:, :, s, :], a["R"][:, :, s, :], bcast(ex[:, 2 + s, h, 4 * b:4 * b + 4], w1), ALU.mult)
                    din(m)
                    din(V.tensor_tensor(a["num"], a["R"][:, :, 0, :], a["R"][:, :, 1, :], ALU.add))
                    din(V.reciprocal(a["rd"], a["num"][:, :, dh]))
                    if q == 6:
                        m = V.tensor_tensor(h3[:, 4 * b:4 * b + 4, :], a["num"][:, :, 0:dh], bcast(a["rd"], dh), ALU.mult)
                        din(m)
                    else:
                        din(V.tensor_tensor(a["num"][:, :, 0:dh], a["num"][:, :, 0:dh], bcast(a["rd"], dh), ALU.mult))
                        xv = x[:, 4 * b:4 * b + 4, h * dh:(h + 1) * dh]
                        m = V.tensor_tensor(xv, xv, a["num"][:, :, 0:dh], ALU.add)
                        if k == heads * NB - 1:
                            m.then_inc(x_ready, 1)
                            dve.wait_ge(x_ready, q + 1)
                for k in range(heads * NB):
                    for jt in range(T):
                        masks(k, jt)
                        if jt == ring - 1 and k:
                            evacuate(k - 1)
                    if k == 0 and heads > 1:
                        values(1)
                evacuate(heads * NB - 1)
            if LAYERS > 2:
                attention(A1, 2, D + 4)

            def experts():
                norm(3)
                dve.wait_ge(g_ps, 1)
                V.memset(gates[:, :, E1:], FILL)
                V.memset(top8, FILL)
                din(V.tensor_tensor(gates[:, :, 0:E1], ps[:, 4, 0:T * E1].rearrange("p (t e) -> p t e", e=E1),
                                    W["bg"][:].unsqueeze(1).broadcast_to([P, T, E1]), ALU.add))
                for t in range(T):
                    i = V.max(emask[:, t, :], gates[:, t, 0:E1])
                din(i)
                din(V.tensor_copy(top8[:, :, 0:2], emask[:, :, 0:2]))
                for t in range(T):
                    i = V.match_replace(out=marked[:, t, :], in_to_replace=top8[:, t, :], in_values=gates[:, t, :], imm_value=-FILL)
                din(i)
                V.tensor_scalar(emask, marked[:, :, 0:E1], -FILL, None, ALU.is_equal).then_inc(emask_ready, 1)
                dve.wait_ge(emask_ready, 1)
                n = 0
                for u in range(NB * E1):
                    b, e = divmod(u, E1)
                    xb = x[:, 4 * b:4 * b + 4, :]
                    if e == 0:
                        dve.wait_ge(o1_ps, n + 1)
                        n += 1
                        V.tensor_tensor(xb, xb, ps[:, 6 + b % 2, :].rearrange("p (i d) -> p i d", i=4), ALU.add).then_inc(o1_read, 1)
                        dve.wait_ge(o1_read, n)
                    dve.wait_ge(o1_ps, n + 1)
                    n += 1
                    for i in range(4):
                        m = V.scalar_tensor_tensor(x[:, 4 * b + i, :], ps[:, 4 + u % 2, i * D:(i + 1) * D],
                                                   emask[:, 4 * b + i, e:e + 1], x[:, 4 * b + i, :], ALU.mult, ALU.add)
                    m.then_inc(o1_read if u < NB * E1 - 1 else x_ready, 1)
                    dve.wait_ge(*((o1_read, n) if u < NB * E1 - 1 else (x_ready, 4)))
            if LAYERS > 3:
                experts()

            def cosine():
                norm(4)
                for t in range(T):
                    dve.wait_ge(kq_ps, t + 1)
                    V.tensor_copy(Kt[:, t, :], ps[:, 4 + t % 4, 0:D])
                    din(V.tensor_copy(Er[:, 0, 0:D], ps[:, 4 + t % 4, D:2 * D]))
                    V.scalar_tensor_tensor(sqj, Er[:, 0, 0:D], 1.0, Er[:, 0, 0:D], ALU.mult, ALU.mult, accum_out=qs[:, 1, t:t + 1])
                    din(V.scalar_tensor_tensor(Er[:, 1, 0:D], Kt[:, t, :], 1.0, Kt[:, t, :], ALU.mult, ALU.mult, accum_out=qs[:, 0, t:t + 1]))
                    V.tensor_copy(ab[:, 3, t:t + 1], qs[:, 0, t:t + 1]).then_inc(kq_read, 1)
                din(V.tensor_scalar(qs[:, 6:8, :], qs[:, 0:2, :], 1e-30, None, ALU.max))
                V.tensor_copy(qs[:, 0:2, :], qs[:, 6:8, :]).then_inc(norm_sq, 1)
                dve.wait_ge(norm_sqrt, 1)
                din(V.reciprocal(qs[:, 4:6, :], qs[:, 2:4, :]))
                din(V.tensor_tensor(qs[:, 6:8, :], qs[:, 0:2, :], qs[:, 4:6, :], ALU.mult))
                din(V.tensor_tensor(qs[:, 6:8, :], qs[:, 6:8, :], qs[:, 2:4, :], ALU.add))
                din(V.tensor_scalar(qs[:, 6:8, :], qs[:, 6:8, :], 0.5, 1e-4, ALU.mult, ALU.max))
                din(V.reciprocal(qs[:, 4:6, :], qs[:, 6:8, :]))
                V.tensor_tensor(Kt, Kt, bcast(qs[:, 4, :], D), ALU.mult).then_inc(kn_ready, 1)
                V.memset(xn1[:, :, D:D + 1], 1.0)
                V.tensor_copy(xn1[:, :, 0:D], xn[:, :, :]).then_inc(xn1_ready, 1)
                din(V.tensor_scalar(ab[:, 0, :], deg[:], 0.0, 0.5, ALU.is_gt, ALU.mult))
                din(V.tensor_scalar(ab[:, 1, :], ab[:, 0, :], -1.0, 1.0, ALU.mult, ALU.add))
                for t in range(T):
                    i = V.scalar_tensor_tensor(x[:, t, :], xn[:, t, :], ab[:, 1, t:t + 1], x[:, t, :], ALU.mult, ALU.add)
                din(i)

                def evacuate(b):
                    dve.wait_ge(p_used, T * (b + 1))
                    for i in range(4):
                        m = V.reciprocal(ab[:, 2, 4 * b + i:4 * b + i + 1], ps[:, 2 + i, D:D + 1])
                    din(m)
                    din(V.tensor_tensor(ab[:, 2, 4 * b:4 * b + 4], ab[:, 2, 4 * b:4 * b + 4], ab[:, 0, 4 * b:4 * b + 4], ALU.mult))
                    for i in range(4):
                        t = 4 * b + i
                        m = V.scalar_tensor_tensor(x[:, t, :], ps[:, 2 + i, 0:D], ab[:, 2, t:t + 1], x[:, t, :], ALU.mult, ALU.add)
                    m.then_inc(a2_read if b < NB - 1 else x_ready, 1)
                for n in range(NB * T):
                    b, jt = divmod(n, T)
                    dve.wait_ge(sc_exp, n + 1)
                    V.tensor_tensor(Er[:, n % RE, :], Er[:, n % RE, :], mask[:, jt, b * BLK:(b + 1) * BLK], ALU.mult).then_inc(p_ready, 1)
                    if jt == 1 and b:
                        evacuate(b - 1)
                evacuate(NB - 1)
                dve.wait_ge(x_ready, 5)
            if LAYERS > 4:
                cosine()

            def depths():
                norm(5)
                dve.wait_ge(w_ps, 1)
                V.tensor_scalar(wcol, ps[:, 4, 0:T], W["br"][:], None, ALU.add).then_inc(wcol_ready, 1)
                din(V.tensor_tensor(x[:, :, :], x[:, :, :], xn[:, :, :], ALU.add))
                dve.wait_ge(wrow_ready, NB)
                din(V.memset(rank, 0.0))
                dve.wait_ge(wcol_ready, 1)
                for t in range(T):
                    w = wcol[:, t:t + 1]
                    a0, a1 = t * P, (t + 1) * P
                    if t:
                        V.tensor_scalar(junk[:, 0:a0], wrow[:, 0:a0], w, None, ALU.is_ge, ALU.add, accum_out=rank[:, 0, t:t + 1])
                    if t < T - 1:
                        V.tensor_scalar(junk[:, a1:N], wrow[:, a1:N], w, None, ALU.is_gt, ALU.add, accum_out=rank[:, 1, t:t + 1])
                    V.scalar_tensor_tensor(junk[:, a0:a1], wrow[:, a0:a1], w, tri[:], ALU.is_ge, ALU.mult, accum_out=rank[:, 2, t:t + 1])
                    din(V.scalar_tensor_tensor(junk[:, N:N + P], wrow[:, a0:a1], w, tric[:], ALU.is_gt, ALU.mult, accum_out=rank[:, 3, t:t + 1]))
                din(V.tensor_tensor(rank[:, 0:2, :], rank[:, 0:2, :], rank[:, 2:4, :], ALU.add))
                din(V.tensor_tensor(rank[:, 0, :], rank[:, 0, :], rank[:, 1, :], ALU.add))
                din(V.scalar_tensor_tensor(sw, rank[:, 0, :], float(KSEL), wcol, ALU.is_lt, ALU.mult))
                for t in range(T):
                    dve.wait_ge(o2_ps, t + 1)
                    din(V.tensor_tensor(junk[:, 0:D], ps[:, 4 + t % 4, 0:D], W["b2m"][:], ALU.add))
                    V.scalar_tensor_tensor(x[:, t, :], junk[:, 0:D], sw[:, t:t + 1], x[:, t, :], ALU.mult,
                                           ALU.add).then_inc(o2_read if t < T - 1 else x_ready, 1)
                    if t < T - 1:
                        dve.wait_ge(o2_read, t + 1)
                dve.wait_ge(x_ready, 6)
            if LAYERS > 5:
                depths()

            def elu():
                V.tensor_scalar(elu_m, h3, 0.0, None, ALU.min).then_inc(elu_ready, 1)
                din(V.scalar_tensor_tensor(x[:, :, :], h3, 0.0, x[:, :, :], ALU.max, ALU.add))
                dve.wait_ge(elu_exp, 1)
                V.scalar_tensor_tensor(x[:, :, :], elu_m, -1.0, x[:, :, :], ALU.add, ALU.add).then_inc(x_ready, 1)
                dve.wait_ge(x_ready, 7)
            if LAYERS > 6:
                attention(A3, 6, D + 2)
                elu()

            def tropical():
                norm(7)
                for f in range(FT):
                    V.memset(acc[:, f, :], FILL).then_inc(fill_done, 1)
                dve.wait_ge(xn_ready, 8 * T)
                V.tensor_tensor(x[:, :, :], x[:, :, :], W["bd"][:].unsqueeze(1).broadcast_to([P, T, D]),
                                ALU.add).then_inc(bd_added, 1)
                dve.wait_ge(fill_done, FT)
                dve.wait_ge(xnT_ready, 8 * NB)
                din(V.tensor_copy(xp3[:, 0, :], XT))
                din(V.tensor_tensor(res, XT, xp3[:, 0, :], ALU.subtract))
                din(V.tensor_copy(xp3[:, 1, :], res))
                V.tensor_tensor(rise[:].rearrange("p j f -> p f j"), W["Wt"][:, :, 0:D:2], W["Wt"][:, :, 1:D:2],
                                ALU.subtract).then_inc(rise_table, 1)
                V.tensor_tensor(xp3[:, 2, :], res, xp3[:, 1, :], ALU.subtract).then_inc(xp3_ready, 1)
                lo, hi = slice(0, N // 2), slice(N // 2, N)

                def step(f, cols, src, feature):
                    return V.scalar_tensor_tensor(acc[:, f, cols], src, W["Wt"][:, f, bass.ds(feature, 1)],
                                                  acc[:, f, cols], ALU.add, ALU.max)

                def last_sum(j, slot, f, second=False):
                    dve.wait_ge(sum_ready, j * 2 + (f + 1))
                    if second:
                        dve.wait_ge(sum_step, j * 2 + (f - 1))
                    step(f, slice(0, N), rise1[:, slot, :] if f else rise0, j * 2 + 1).then_inc(sum_step, 1)

                def pair(j, slot, before=2):
                    dve.wait_ge(even_ps, j + 1)
                    if before:
                        dve.wait_ge(single_step, j * 2)
                    step(3, lo, ps_wide[:, 1, lo], j * 2).then_inc(single_step, 1)
                    if before:
                        last_sum(j - 1, 1 - slot, 0, second=before > 1)
                    dve.wait_ge(pair_ps, j * 3 + 1)
                    if before:
                        dve.wait_ge(pair_step, j * 3 - 2)
                    step(2, lo, ps_wide[:, 1, hi], j * 2 + 1).then_inc(pair_step, 1)
                    dve.wait_ge(single_step, j * 2 + 1)
                    step(3, lo, oddc[:, slot, lo], j * 2 + 1).then_inc(single_step, 1)
                    dve.wait_ge(pair_ps, j * 3 + 2)
                    if before:
                        dve.wait_ge(pair_step, j * 3 - 1)
                    step(2, hi, ps_wide[:, 1, lo], j * 2 + 1).then_inc(pair_step, 1)
                    dve.wait_ge(pair_ps, j * 3 + 3)
                    if before:
                        dve.wait_ge(pair_step, j * 3)
                    step(3, hi, ps_wide[:, 1, hi], j * 2 + 1).then_inc(pair_step, 1)
                    if before:
                        last_sum(j - 1, 1 - slot, 1, second=before > 1)
                pair(0, 0, before=0)
                pair(1, 1, before=1)
                with dve.Fori(1, D // 4) as i:
                    for s in range(2):
                        pair(i * 2 + s, s)
                for f in range(2):
                    last_sum(D // 2 - 1, 1, f, second=True)
                dve.wait_ge(sum_step, D)
                dve.wait_ge(pair_step, 3 * D // 2)
                dve.wait_ge(single_step, D)
                dve.wait_ge(sa_ready, 1)
                din(V.tensor_scalar(sa[:, 1, :], sa[:, 0, :], -1.0, 1.0, ALU.mult, ALU.add))
                n = 0
                for f in range(FT):
                    V.tensor_scalar(acc[:, f, :], acc[:, f, :], W["bt"][:, f:f + 1], None, ALU.add).then_inc(z_ready, 1)
                for f in range(FT):
                    for dst, op in ((cvx, ALU.max), (ccv, ALU.min)):
                        if f and op == ALU.max:
                            dve.wait_ge(fused_ready, f)
                        for p in range(1, PP):
                            dve.wait_ge(af_ready, n + 2 if p == 1 else n + 1)
                            if p == 1:
                                V.tensor_tensor(dst, AF[n % 4], AF[(n + 1) % 4], op).then_inc(af_used, 2)
                                n += 2
                            else:
                                V.tensor_tensor(dst, dst, AF[n % 4], op).then_inc(af_used, 1)
                                n += 1
                            dve.wait_ge(af_used, n)
                    din(V.tensor_scalar(cvx, cvx, sa[:, 0, f:f + 1], None, ALU.mult))
                    V.scalar_tensor_tensor(cvx, ccv, sa[:, 1, f:f + 1], cvx, ALU.mult, ALU.add).then_inc(trop_mix, 1)
                for t in range(T):
                    dve.wait_ge(f_ps, t + 1)
                    V.tensor_tensor(x[:, t, :], x[:, t, :], ps[:, t % 8, 0:D], ALU.add).then_inc(x_ready, 1)
            if LAYERS > 7:
                tropical()


def layout(i):
    def tiles(w):
        return w.reshape(-1, P, w.shape[-1]).transpose(1, 0, 2)

    def cols(v):
        return v.reshape(-1, P).T
    win = i["L0_ffn_W_in"]
    cb = i["L0_ffn_conv_b"]
    order = np.concatenate([win[:, 0:DIN], win[:, 2 * DIN + 2 * DST:], win[:, DIN:2 * DIN + 2 * DST]], axis=1)
    return {
        "x": i["x"], "adjT": i["adj"].T,
        "W0T": i["L0_gnn_W"].T, "b0": i["L0_gnn_b"],
        "win": order, "conv_w": i["L0_ffn_conv_w"].T,
        "convb_row": cb[None, 0:XB], "convb_bc": cb[DIN:].reshape(2, DST).T,
        "dtb": i["L0_ffn_dt_bias"], "alog": i["L0_ffn_A_log"], "Dh": i["L0_ffn_D"], "nw": cols(i["L0_ffn_norm_w"]),
        "woutT": i["L0_ffn_W_out"].T, "wlin": i["L0_ffn_W_lin"], "blin": i["L0_ffn_b_lin"],
        "W1n": i["L1_gnn_W1"], "W2n": i["L1_gnn_W2"], "W3T": i["L1_gnn_W3"].T,
        "b12": np.stack([i["L1_gnn_b1"], i["L1_gnn_b2"]], axis=1), "b3": i["L1_gnn_b3"], "a": i["L1_gnn_a"],
        "wg": i["L1_ffn_Wg"], "bg": i["L1_ffn_bg"],
        "w1e": i["L1_ffn_W1"].transpose(1, 0, 2).reshape(D, E1 * H1), "b1c": cols(i["L1_ffn_b1"].reshape(-1)),
        "w2e": tiles(i["L1_ffn_W2"].reshape(E1 * H1, D)), "b2r": i["L1_ffn_b2"],
        "wqT": i["L2_gnn_Wq"].T, "wkT": i["L2_gnn_Wk"].T,
        "wr": i["L2_ffn_wr"], "br": i["L2_ffn_br"], "w1m": i["L2_ffn_w1"], "b1m": cols(i["L2_ffn_b1"]),
        "w2m": tiles(i["L2_ffn_w2"]), "b2m": i["L2_ffn_b2"],
        "W3W": i["L3_gnn_W"], "W3WT": i["L3_gnn_W"].T, "a3": i["L3_gnn_a"].reshape(2, D).T,
        "Wt": tiles(i["L3_ffn_Wt"]), "bt": cols(i["L3_ffn_bt"]),
        "slx": tiles(i["L3_ffn_sl_cvx"]), "ofx": tiles(i["L3_ffn_of_cvx"]),
        "slc": tiles(i["L3_ffn_sl_ccv"]), "ofc": tiles(i["L3_ffn_of_ccv"]),
        "alpha": cols(i["L3_ffn_alpha"]), "Wc": i["L3_ffn_Wc"], "bc": cols(i["L3_ffn_bc"]),
        "Wg": i["L3_ffn_Wg"], "bgt": cols(i["L3_ffn_bg"]), "Wd": tiles(i["L3_ffn_Wd"]), "bd": i["L3_ffn_bd"],
    }


def kernel(**inputs):
    import concourse.bacc as bacc
    from concourse.bass_utils import run_bass_kernel_spmd

    nc = bacc.Bacc("TRN2", target_bir_lowering=False, num_devices=1)
    arrays, aps = {}, {}
    for name, a in layout({k: np.asarray(v) for k, v in inputs.items()}).items():
        a = np.ascontiguousarray(a)
        arrays[f"in_{name}"] = a
        aps[name] = nc.dram_tensor(f"in_{name}", a.shape, mybir.dt.from_np(a.dtype), kind="ExternalInput").ap()
    out = nc.dram_tensor("out_dram", (N, D), F32, kind="ExternalOutput").ap()
    dbg = nc.dram_tensor("dbg_dram", (8, N, D), F32, kind="ExternalOutput").ap() if DEBUG else None
    build(nc, aps, out, dbg)
    r = run_bass_kernel_spmd(nc, [arrays], core_ids=[0])
    return r.results[0]["out_dram"]
```

```python
import numpy as np
import concourse.bass as bass
from concourse import mybir
from contextlib import ExitStack

F32 = mybir.dt.float32
BF16 = mybir.dt.bfloat16
I32 = mybir.dt.int32
ALU = mybir.AluOpType
ACT = mybir.ActivationFunctionType
AX = mybir.AxisListType.X

P = 128
N = 2048
D = 128
T = N // P
BLK = 512
NB = N // BLK
TB = T // NB
EPS = 1e-5
DEBUG = 0
LAYERS = 8

DIN, DST, KC, NH, HD = 256, 64, 4, 4, 64
XB = DIN + DST
E1, H1 = 8, 256
HT1 = E1 * H1 // P
H2 = 512
KSEL = N // 2 - 1
FF, PP = 512, 8
FT = FF // P
NEG = -1e30
FILL = -3.0e38


def build(nc, ins, out, dbg):
    with ExitStack() as ctx:
        def sb(name, shape, dt=F32):
            return ctx.enter_context(nc.sbuf_tensor(name, shape, dt))

        def sem(name):
            return ctx.enter_context(nc.semaphore(name))

        ps = ctx.enter_context(nc.psum_tensor("ps", [P, 8, BLK], F32))
        ps_wide = ps[:, :, :].rearrange("p (b k) n -> p b (k n)", b=2)

        x = sb("x", [P, T, D])
        xn = sb("xn", [P, T, D])
        xnT = sb("xnT", [P, 4 + N])
        mask = sb("mask", [P, T, N], BF16)
        ident = sb("ident", [P, P])
        identb = sb("identb", [P, P], BF16)
        ones = sb("ones", [P, P])
        upper = sb("upper", [P, P])
        negtri = sb("negtri", [P, P])
        tri = sb("tri", [P, P])
        tric = sb("tric", [P, P])
        selx = sb("selx", [96, 32], BF16)
        seld = sb("seld", [96, 16], BF16)
        sa = sb("sa", [P, 2, FT])
        offs = sb("offs", [P, 2, FT, PP])
        dslope = sb("dslope", [P, 2, FT, PP // 2]); doffs = sb("doffs", [P, 2, FT, PP // 2])
        rise = sb("rise", [P, D // 2, FT]); bias = sb("bias", [P, 2, FT])
        stats = sb("stats", [P, T, 6])
        mv = sb("mv", [P, T, 2])
        lnv = sb("lnv", [P, 4, T])
        deg = sb("deg", [P, T])
        XT = xnT[:, 4:4 + N]

        W = {}

        def weight(name, shape):
            W[name] = sb("w_" + name, shape)
            return W[name]

        weight("W0T", [P, D]); weight("b0", [P, D])
        weight("win", [P, 2 * DIN + 2 * DST + NH])
        weight("convw", [P, 3, KC]); weight("convb", [P, 3])
        weight("dtb", [P, NH]); weight("alog", [P, NH]); weight("Dh", [P, NH])
        weight("nw", [P, 2]); weight("woutT", [P, DIN]); weight("wlin", [P, D]); weight("blin", [P, D])
        weight("W1n", [P, D]); weight("W2n", [P, D]); weight("WVu", [P, D + 4])
        weight("b12", [P, 2]); weight("A1", [P, 2]); weight("A2", [P, 2]); weight("vbias", [P, D + 4])
        weight("wg", [P, E1]); weight("bg", [P, E1]); weight("b1c", [P, HT1]); weight("b2r", [E1, D])
        weight("w1e", [P, E1 * H1])
        weight("wqT", [P, D]); weight("wkT", [P, D])
        weight("wr", [P, 1]); weight("br", [P, 1]); weight("w1m", [P, H2]); weight("b1m", [P, H2 // P])
        weight("w2m", [P, H2 // P, D]); weight("b2m", [P, D])
        weight("W3WT", [P, D]); weight("WVu3", [P, D + 2]); weight("a3", [P, 2])
        weight("Wt", [P, FT, D]); weight("bt", [P, FT])
        weight("slx", [P, FT, PP]); weight("ofx", [P, FT, PP]); weight("slc", [P, FT, PP]); weight("ofc", [P, FT, PP])
        weight("alpha", [P, FT]); weight("Wc", [P, FF]); weight("bc", [P, FT])
        weight("Wg", [P, FF]); weight("bgt", [P, FT]); weight("Wd", [P, FT, D]); weight("bd", [P, D])

        AR = 19300
        W2E_AT = AR - HT1 * D
        arena = sb("arena", [P, AR])
        at = [0]

        def lay(*shape, dt=F32, parts=P, fresh=False, to=None):
            if fresh:
                at[0] = 0
            if to is not None:
                at[0] = to
            size = int(np.prod(shape))
            words = size if dt == F32 else (size + 1) // 2
            v = arena[0:parts, at[0]:at[0] + words]
            at[0] += words
            assert at[0] <= AR, at[0]
            if dt != F32:
                v = v.bitcast(dt)[:, 0:size]
            names = "abcd"[:len(shape)]
            if len(shape) > 1:
                v = v.rearrange(f"p ({' '.join(names)}) -> p {' '.join(names)}", **dict(zip(names, shape)))
            return v

        x_loaded = sem("x_loaded"); w_loaded = sem("w_loaded"); w0_loaded = sem("w0_loaded")
        adj_in = [sem(f"adj_in{i}") for i in range(4)]
        mask_ready = sem("mask_ready"); consts = sem("consts")
        var_ready = sem("var_ready"); sqrt_ready = sem("sqrt_ready")
        xn_ready = sem("xn_ready"); xn_act = sem("xn_act"); shift_ready = sem("shift_ready"); xnT_ps = sem("xnT_ps"); xnT_ready = sem("xnT_ready")
        x_ready = sem("x_ready")
        dve_step = sem("dve_step"); act_step = sem("act_step"); pool_step = sem("pool_step")
        out_done = sem("out_done"); dbg_done = sem("dbg_done")

        steps = {"dve": 0, "act": 0, "pool": 0}

        def in_turn(eng, name, s, ins_):
            steps[name] += 1
            ins_.then_inc(s, 1)
            eng.wait_ge(s, steps[name])

        n_w = [0]
        block = ctx.enter_context(nc.Block())

        def bcast(v, n):
            return v.unsqueeze(len(v.shape)).broadcast_to(list(v.shape) + [n])

        stage_adj = lay(4, N, fresh=True).bitcast(I32)
        V0 = lay(T, D)
        XP0 = lay(T, 3 * D + 2, dt=BF16)
        R0 = lay(8, D)
        rdeg = lay(T)
        v0_of_ps = ps[:, 4:8, :].rearrange("p b (t d) -> p (b t) d", t=TB)
        v0_rounded = sem("v0_rounded")
        v0_ps = sem("v0_ps"); v0_ready = sem("v0_ready"); xp0_ready = sem("xp0_ready")
        agg_ps = sem("agg_ps"); agg_read = sem("agg_read")

        xs = lay(T, XB, fresh=True)
        XS_END = at[0]
        sz = lay(T, DIN)
        lay(2 * (KC - 1))
        CT = lay(N, parts=DST)
        conv_bc = xn[:, :, :].rearrange("p t d -> p (t d)")
        BT = conv_bc[0:DST, :]
        xdt = lay(2, DIN); xdd = lay(2, DIN)
        ROWIN_AT = at[0]
        rowin = lay(2, NH, P)
        EM = lay(2, NH, P)
        Hst = lay(2, DIN, parts=DST)
        yscr = lay(2, DIN)
        small = lay(12, T * NH)
        wol = lay(2, D)
        Aneg = lay(NH)
        DI = lay(NH, P)
        MAMBA_END = at[0]
        raw = lay(2, KC - 1 + N, to=XS_END)
        conv_x = [lay(N, to=ROWIN_AT), lay(N, to=MAMBA_END)]
        conv = conv_x + [conv_bc]
        CONV_ORDER = (2, 0, 1)
        RZ = 5
        yT = lay(2, 2, P, to=0)
        wol_ps = sem("wol_ps"); wol_ready = sem("wol_ready");
        raw_ps = sem("raw_ps"); raw_read = sem("raw_read"); conv_done = sem("conv_done"); silu_done = sem("silu_done")
        ct_in = sem("ct_in"); xs_ps = sem("xs_ps"); xs_ready = sem("xs_ready"); z_ps = sem("z_ps"); z_read = sem("z_read")
        dt_ps = sem("dt_ps"); dt_read = sem("dt_read")
        sp_exp = sem("sp_exp"); sp_ln = sem("sp_ln"); sp_e_ready = sem("sp_e_ready"); sp_u_ready = sem("sp_u_ready")
        dA_ready = sem("dA_ready"); acum_ps = sem("acum_ps"); acum_ready = sem("acum_ready"); decay_ready = sem("decay_ready")
        alog_exp = sem("alog_exp"); DI_ready = sem("DI_ready")
        rowin_ready = sem("rowin_ready"); row_ps = sem("row_ps"); E_ready = sem("E_ready"); G_ps = sem("G_ps")
        M_ready = sem("M_ready"); xdt_ready = sem("xdt_ready"); y_ps = sem("y_ps"); y_done = sem("y_done")
        h_ready = sem("h_ready"); s_ps = sem("s_ps"); sq_done = sem("sq_done"); yrms_var = sem("yrms_var"); yrms_sqrt = sem("yrms_sqrt")
        yT_ps = sem("yT_ps"); yT_ready = sem("yT_ready"); mo_ps = sem("mo_ps"); mo_read = sem("mo_read")

        once = {s: sem(s) for s in ("u_ps", "u_ready", "smax_ready", "S_ready", "arg_ready", "ex_ready")}

        def attention_memory(tag, heads, dh, ring, bias_cols):
            a = {}
            w1 = dh + 1
            a["heads"], a["dh"], a["w1"], a["ring"] = heads, dh, w1, ring
            a["VS"] = lay(T, D + bias_cols, fresh=True)
            a["Fv"] = lay(T, 2, w1)
            a["XP"] = [lay(T, 2, 3, w1, dt=BF16) for _ in range(heads)]
            a["row"] = [lay(N) for _ in range(heads)]
            a["M1"] = lay(ring, BLK, dt=BF16)
            a["M2"] = xn[:, :, :].rearrange("p t d -> p (t d)").bitcast(BF16)[:, 0:ring * BLK].rearrange("p (r n) -> p r n", r=ring)
            a["R"] = lay(4, 2, w1)
            a["num"] = lay(4, w1)
            a["rd"] = lay(4)
            a["arg"] = lay(4, heads, T)
            a["ex"] = lay(4, heads, T)
            a["thr"] = lay(heads, T)
            a["smax"] = lay(heads)
            a["S"] = lay(heads)
            a["tt"] = lay(heads, T)
            a["cc"] = lay(heads, T)
            a["end"] = at[0]
            a["banks"] = 1 if 6 * w1 <= BLK else 2
            a["sets"] = 8 // (4 * a["banks"])
            a["turn"] = 1 if tag == "g1" else 2
            a.update(once)
            for s in ("v_ps", "v_ready", "row_ps", "row_ready", "xp_ready", "m1_ready", "m2_pool", "m2_dve", "m_used", "acc_read"):
                a[s] = sem(f"{tag}_{s}")
            return a

        A1 = attention_memory("g1", 2, 64, 6, 4)
        assert A1["end"] <= W2E_AT, (A1["end"], W2E_AT)
        w2e = lay(HT1, D, to=W2E_AT)
        w2e_loaded = sem("w2e_loaded")
        A3 = attention_memory("g3", 1, 128, 8, 2)
        elu_m = lay(T, D, to=0)
        h3 = lay(T, D, to=T * (D + 2))
        elu_ready = sem("elu_ready"); elu_exp = sem("elu_exp")

        hT1 = lay(4, 2, BLK, fresh=True)
        gates = lay(T, E1 + 6)
        top8 = lay(T, 8)
        marked = lay(T, E1 + 6)
        emask = lay(T, E1)
        emT = lay(N, parts=E1)
        assert at[0] <= W2E_AT
        g_ps = sem("g_ps"); emask_ready = sem("emask_ready"); emT_ps = sem("emT_ps"); emT_ready = sem("emT_ready")
        h1_ps = sem("h1_ps"); h1_ready = sem("h1_ready"); o1_ps = sem("o1_ps"); o1_read = sem("o1_read")

        RE = 6
        Kt = lay(T, D, fresh=True)
        KnT = lay(N); QT = lay(N)
        Er = lay(RE, BLK)
        xn1 = lay(T, D + 1)
        qs = lay(8, T)
        sqj = lay(D)
        ab = lay(4, T)
        kq_ps = sem("kq_ps"); kq_read = sem("kq_read"); QT_ps = sem("QT_ps"); QT_ready = sem("QT_ready")
        norm_sq = sem("norm_sq"); norm_sqrt = sem("norm_sqrt"); kn_ready = sem("kn_ready")
        KnT_ps = sem("KnT_ps"); KnT_ready = sem("KnT_ready"); xn1_ready = sem("xn1_ready")
        sc_ps = sem("sc_ps"); sc_exp = sem("sc_exp"); p_ready = sem("p_ready"); p_used = sem("p_used")
        a2_read = sem("a2_read")

        wcol = lay(T, fresh=True)
        wrow = lay(N)
        junk = lay(N + P)
        rank = lay(4, T)
        sw = lay(T)
        hT2 = lay(2, H2 // P, BLK)
        w_ps = sem("w_ps"); wcol_ready = sem("wcol_ready"); wrow_ps = sem("wrow_ps"); wrow_ready = sem("wrow_ready")
        h2_ps = sem("h2_ps"); h2_ready = sem("h2_ready"); o2_ps = sem("o2_ps"); o2_read = sem("o2_read")

        GF = 32
        NG = D // GF
        xg = lay(NG, N, dt=BF16, parts=3 * GF, fresh=True)
        xp3 = lay(3, N, dt=BF16)
        res = lay(N)
        rise_m = lay(N + BLK * 2, to=NG * N // 2)
        rise0 = lay(N)
        rise1 = lay(2, N)
        oddc = lay(2, N)
        line_a = [lay(N, to=0), lay(N), lay(N)]
        line_b = [lay(N), lay(N), lay(N)]
        cvx = lay(N); ccv = lay(N); line = lay(N)
        big = mask[:, :, :].rearrange("p t n -> p (t n)").bitcast(F32)
        acc = big[:, 0:FT * N].rearrange("p (f n) -> p f n", f=FT)
        CL, G = ([big[:, FT * N + (2 * k + g) * N:FT * N + (2 * k + g + 1) * N] for k in range(2)] for g in range(2))
        xp3_ready = sem("xp3_ready"); xg_in = sem("xg_in"); sel_ready = sem("sel_ready"); rise_table = sem("rise_table")
        bias_ready = sem("bias_ready"); fill_done = sem("fill_done"); bd_added = sem("bd_added")
        diff_ps = sem("diff_ps"); odd_ps = sem("odd_ps"); even_ps = sem("even_ps"); pair_ps = sem("pair_ps")
        odd_copied = sem("odd_copied"); rise_pe = sem("rise_pe"); rise_pool = sem("rise_pool"); sum_ready = sem("sum_ready")
        single_step = sem("single_step"); pair_step = sem("pair_step"); sum_step = sem("sum_step")
        lines_table = sem("lines_table"); line_ready = sem("line_ready")
        pair_line = sem("pair_line"); pair_used = sem("pair_used")
        c_ps = sem("c_ps"); c_read = sem("c_read"); fused_ready = sem("fused_ready"); f_ps = sem("f_ps")
        x_summed = sem("x_summed"); sa_ready = sem("sa_ready")

        ld = []

        def load(eng, dst, src):
            ld.append(1)
            eng.dma_start(dst, src).then_inc(w_loaded, 16)

        small_loads = [
            ("win", "win"), ("woutT", "woutT"), ("wlin", "wlin"), ("W1n", "W1n"), ("W2n", "W2n"),
            ("wg", "wg"), ("w1e", "w1e"), ("wqT", "wqT"), ("wkT", "wkT"), ("w1m", "w1m"), ("W3WT", "W3WT"),
            ("Wc", "Wc"), ("Wg", "Wg"), ("b2r", "b2r"), ("wr", "wr"), ("w2m", "w2m"), ("Wt", "Wt"), ("Wd", "Wd"),
            ("slx", "slx"), ("ofx", "ofx"), ("slc", "slc"), ("ofc", "ofc"), ("bt", "bt"), ("alpha", "alpha"),
            ("bc", "bc"), ("bgt", "bgt"), ("b1m", "b1m"), ("b1c", "b1c"), ("nw", "nw"), ("convb", "convb"),
            ("b12", "b12"), ("a3", "a3"), ("convw", "convw")]
        row_loads = ["dtb", "alog", "Dh", "blin", "bg", "br", "b2m", "bd"]
        N_W = len(small_loads) + len(row_loads) + 1 + 4 + 1 + 1

        def dump(sp, q):
            if DEBUG and q < LAYERS:
                sp.wait_ge(x_ready, q + 1)
                sp.dma_start(dbg[q].rearrange("(t p) d -> p t d", p=P), x[:, :, :]).then_inc(dbg_done, 16)
                sp.wait_ge(dbg_done, 16 * (q + 1))

        @block.sync
        def _(sp):
            sp.dma_start(x[:, :, :], ins["x"].rearrange("(t p) d -> p t d", p=P)).then_inc(x_loaded, 16)
            sp.dma_start(W["W0T"][:], ins["W0T"]).then_inc(w0_loaded, 16)
            sp.dma_start(W["b0"][:], ins["b0"].partition_broadcast(P)).then_inc(w0_loaded, 16)
            for jt in range(4, T):
                sp.wait_ge(mask_ready, jt - 3)
                sp.dma_start(stage_adj[:, jt % 4, :], ins["adjT"][jt * P:(jt + 1) * P, :]).then_inc(adj_in[jt % 4], 16)
            for name, src in small_loads:
                load(sp, W[name][:], ins[src])
            for name in row_loads:
                load(sp, W[name][:], ins[name].partition_broadcast(P))
            load(sp, W["vbias"][:, 0:D], ins["b3"].partition_broadcast(P))
            load(sp, W["WVu"][:, 0:D], ins["W3T"])
            load(sp, W["WVu3"][:, 0:D], ins["W3W"])
            sp.wait_ge(consts, 1)
            for h in range(2):
                load(sp, W["A1"][64 * h:64 * h + 64, h:h + 1], ins["a"][h, 0:64].unsqueeze(1))
                load(sp, W["A2"][64 * h:64 * h + 64, h:h + 1], ins["a"][h, 64:128].unsqueeze(1))
            assert len(ld) == N_W, (len(ld), N_W)
            if LAYERS > 1:
                sp.wait_ge(silu_done, 1)
                sp.dma_start(CT, conv_bc[DST:2 * DST, :]).then_inc(ct_in, 16)
            dump(sp, 0)
            if LAYERS > 2:
                sp.wait_ge(x_ready, 2)
                sp.dma_start(w2e, ins["w2e"]).then_inc(w2e_loaded, 16)
            for q in range(1, 7):
                dump(sp, q)
            if LAYERS > 7:
                sp.wait_ge(xp3_ready, 1)
                for g in range(NG):
                    for k in range(3):
                        sp.dma_start(xg[k:3 * (GF - 1) + k + 1:3, g, :], xp3[g * GF:(g + 1) * GF, k, :]).then_inc(xg_in, 16)
            if LAYERS < 8:
                sp.wait_ge(x_ready, LAYERS)
                sp.dma_start(out.rearrange("(t p) d -> p t d", p=P), x[:, :, :]).then_inc(out_done, 16)
                sp.wait_ge(out_done, 16)
            else:
                for b in range(NB):
                    sp.wait_ge(x_ready, 7 + b + 1)
                    sp.dma_start(out[b * BLK:(b + 1) * BLK, :].rearrange("(t p) d -> p t d", p=P),
                                 x[:, b * TB:(b + 1) * TB, :]).then_inc(out_done, 16)
                sp.wait_ge(out_done, 16 * NB)

        @block.gpsimd
        def _(pool):
            def pin(i):
                in_turn(pool, "pool", pool_step, i)
            pin(pool.memset(W["A1"][:], 0.0))
            pool.memset(W["A2"][:], 0.0).then_inc(consts, 1)
            pin(pool.memset(ident[:], 0.0))
            pin(pool.affine_select(out=ident[:], in_=ident[:], compare_op=ALU.not_equal, fill=1.0, base=0,
                                   pattern=[[-1, P]], channel_multiplier=1))
            pin(pool.tensor_copy(identb[:], ident[:]))
            pin(pool.memset(ones[:], 1.0))
            pin(pool.affine_select(out=upper[:], in_=ones[:], compare_op=ALU.is_ge, fill=0.0, base=0,
                                   pattern=[[1, P]], channel_multiplier=-1))
            pin(pool.affine_select(out=tri[:], in_=ones[:], compare_op=ALU.is_gt, fill=0.0, base=0,
                                   pattern=[[-1, P]], channel_multiplier=1))
            pin(pool.affine_select(out=tric[:], in_=ones[:], compare_op=ALU.is_ge, fill=0.0, base=0,
                                   pattern=[[1, P]], channel_multiplier=-1))
            pin(pool.memset(negtri[:], 0.0))
            pin(pool.affine_select(out=negtri[:], in_=negtri[:], compare_op=ALU.is_ge, fill=NEG, base=0,
                                   pattern=[[-1, P]], channel_multiplier=1))
            pin(pool.memset(selx[:], 1.0))
            pin(pool.affine_select(out=selx[:], in_=selx[:], compare_op=ALU.is_ge, fill=0.0, base=0,
                                   pattern=[[-3, GF]], channel_multiplier=1))
            pin(pool.affine_select(out=selx[:], in_=selx[:], compare_op=ALU.is_ge, fill=0.0, base=2,
                                   pattern=[[3, GF]], channel_multiplier=-1))
            pool.tensor_tensor(seld[:], selx[:, 0:GF:2], selx[:, 1:GF:2], ALU.subtract).then_inc(sel_ready, 1)
            pool.memset(xnT[:, 0:4], 0.0).then_inc(consts, 1)

            if LAYERS > 1:
                pool.wait_ge(x_ready, 1)
                for k in range(2):
                    i = pool.memset(raw[:, k, 0:KC - 1], 0.0)
                i.then_inc(consts, 1)
                pin(pool.memset(Hst[:, 0, :], 0.0))
                pool.wait_ge(decay_ready, 2)
                pool.wait_ge(xs_ps, T)

                def rowin_of(c):
                    if c >= 2:
                        pool.wait_ge(row_ps, c - 1)
                    pool.tensor_tensor(rowin[:, c % 2, :, :], negtri[:].unsqueeze(1).broadcast_to([P, NH, P]),
                                       bcast(small[:, 9, c * NH:(c + 1) * NH], P), ALU.add).then_inc(rowin_ready, 1)
                rowin_of(0)
                rowin_of(1)
                for c in range(T):
                    if c >= 2:
                        pool.wait_ge(y_ps, c - 1)
                    pool.wait_ge(xs_ready, c + 1)
                    dtv = small[:, 0, c * NH:(c + 1) * NH]
                    dcv = small[:, 6, c * NH:(c + 1) * NH]
                    v = xdt[:, c % 2, :].rearrange("p (h q) -> p h q", h=NH)
                    pin(pool.tensor_tensor(v, xs[:, c, 0:DIN].rearrange("p (h q) -> p h q", h=NH), bcast(dtv, HD), ALU.mult))
                    pool.tensor_tensor(xdd[:, c % 2, :].rearrange("p (h q) -> p h q", h=NH), v, bcast(dcv, HD),
                                       ALU.mult).then_inc(xdt_ready, 1)
                    if c + 2 < T:
                        rowin_of(c + 2)

            def attention(a):
                max_over_tokens(a)
                for n in range(a["heads"] * NB * T):
                    if n % 3 < 2:
                        b, jt, r = n // T % NB, n % T, n % a["ring"]
                        pool.wait_ge(a["m1_ready"], n + 1)
                        pool.tensor_tensor(a["M2"][:, r, :], mask[:, jt, b * BLK:(b + 1) * BLK], a["M1"][:, r, :],
                                           ALU.subtract).then_inc(a["m2_pool"], 1)

            def max_over_tokens(a):
                pool.wait_ge(a["smax_ready"], a["turn"])
                pool.partition_all_reduce(a["S"], a["smax"], P, bass.bass_isa.ReduceOp.max).then_inc(a["S_ready"], 1)
            if LAYERS > 2:
                attention(A1)
            if LAYERS > 6:
                attention(A3)

            def tropical():
                def pair(j, slot):
                    pool.wait_ge(rise_pool, j * 2 + 1)
                    pool.tensor_tensor(rise0, rise0, oddc[:, slot, :], ALU.add).then_inc(sum_ready, 1)
                    pool.wait_ge(rise_pool, j * 2 + 2)
                    pool.tensor_tensor(rise1[:, slot, :], rise1[:, slot, :], oddc[:, slot, :], ALU.add).then_inc(sum_ready, 1)
                with pool.Fori(0, D // 4) as i:
                    for s in range(2):
                        pair(i * 2 + s, s)
                for n in range(6 * FT):
                    k = n % 3
                    pool.wait_ge(line_ready, 2 * n + 2)
                    pool.tensor_tensor(line_a[k], line_b[k], line_a[k],
                                       ALU.add if n % 6 < 3 else ALU.subtract).then_inc(pair_line, 1)
            if LAYERS > 7:
                tropical()

        @block.tensor
        def _(pe):
            mm, tr = pe.matmul, pe.transpose

            def norm_transposes(q):
                for t in range(T):
                    if t % 3 < 2:
                        pe.wait_ge(xn_ready, 11 * q + t - t // 3 + 1)
                    else:
                        pe.wait_ge(xn_act, 5 * q + t // 3 + 1)
                    i = tr(ps[:, t // 4, (t % 4) * P:(t % 4 + 1) * P], xn[:, t, :], ident[:])
                    if t % 4 == 3:
                        i.then_inc(xnT_ps, 1)

            def tok(t):
                return XT[:, t * P:(t + 1) * P]

            pe.wait_ge(consts, 2)
            norm_transposes(0)
            pe.wait_ge(w0_loaded, 32)
            for t in range(T):
                pe.wait_ge(xnT_ready, t // TB + 1)
                i = mm(ps[:, 4 + t // TB, t % TB * D:(t % TB + 1) * D], tok(t), W["W0T"][:], start=True, stop=True)
            i.then_inc(v0_ps, 1)
            pe.wait_ge(xp0_ready, 1)

            def gather(half, i, jt):
                m = mm(ps[:, i, 0:3 * D + 1], mask[:, jt, (half * 8 + i) * P:(half * 8 + i + 1) * P],
                       XP0[:, jt, 0:3 * D + 1], start=(jt == 0), stop=(jt == T - 1))
                if jt == T - 1:
                    m.then_inc(agg_ps, 1)
            for jt in range(T):
                pe.wait_ge(mask_ready, jt + 1)
                for i in range(8):
                    gather(0, i, jt)
            for i in range(8):
                pe.wait_ge(agg_read, i + 1)
                for jt in range(T):
                    gather(1, i, jt)

            def mamba():
                norm_transposes(1)
                pe.wait_ge(w_loaded, 16 * N_W)
                for k in range(2):
                    i = mm(ps[:, 4, k * P:(k + 1) * P], W["woutT"][:, k * P:(k + 1) * P], W["wlin"][:],
                           start=True, stop=True, skip_group_check=True)
                i.then_inc(wol_ps, 1)
                pe.wait_ge(xnT_ready, 2 * NB)
                for c in range(T):
                    i = mm(ps[:, 5, c * NH:(c + 1) * NH], tok(c), W["win"][:, DIN:DIN + NH],
                           start=True, stop=True, skip_group_check=True)
                i.then_inc(dt_ps, 1)
                for u, m in enumerate(CONV_ORDER):
                    if u == 1:
                        pe.wait_ge(wol_ready, 1)
                        pe.wait_ge(dt_read, 1)
                    for b in range(NB):
                        if u == 2:
                            pe.wait_ge(raw_read, b + 1)
                        mm(ps[:, 4 * (u % 2) + b, :], W["win"][:, DIN + NH + m * P:DIN + NH + (m + 1) * P],
                           XT[:, b * BLK:(b + 1) * BLK], start=True, stop=True).then_inc(raw_ps, 1)
                pe.wait_ge(dA_ready, 1)
                pe.wait_ge(raw_read, 3 * NB)
                dA = small[:, 1, :]
                mm(ps[:, 0, 0:T * NH], upper[:], dA, start=True, stop=True, skip_group_check=True)
                mm(ps[:, 0, T * NH:2 * T * NH], ones[:], dA, start=True, stop=True, skip_group_check=True).then_inc(acum_ps, 1)
                for c in range(T + RZ - 1):
                    if c < T:
                        if c >= RZ:
                            pe.wait_ge(z_read, c - RZ + 1)
                        mm(ps[:, 1 + c % RZ, 0:DIN], tok(c), W["win"][:, 0:DIN], start=True, stop=True).then_inc(z_ps, 1)
                    if c >= RZ - 1:
                        e = c - RZ + 1
                        pe.wait_ge(silu_done, 3)
                        if e >= 2:
                            pe.wait_ge(xs_ready, e - 1)
                        for k in range(2):
                            tr(ps[:, 6 + e % 2, k * P:(k + 1) * P], conv_x[k][:, e * P:(e + 1) * P], ident[:])
                        tr(ps[:, 6 + e % 2, DIN:XB], BT[:, e * P:(e + 1) * P], ident[0:DST, 0:DST]).then_inc(xs_ps, 1)
                pe.wait_ge(acum_ready, 1)
                pe.wait_ge(ct_in, 16)
                pe.wait_ge(DI_ready, 1)
                pe.wait_ge(z_read, T)
                pe.wait_ge(xs_ready, T)

                def rows(c):
                    pe.wait_ge(rowin_ready, c + 1)
                    if c >= 2:
                        pe.wait_ge(M_ready, c - 1)
                    for h in range(NH):
                        i = tr(ps[:, c % 2, h * P:(h + 1) * P], rowin[:, c % 2, h, :], ident[:])
                    i.then_inc(row_ps, 1)
                    mm(ps[:, 2 + c % 2, 0:P], BT[:, c * P:(c + 1) * P], CT[:, c * P:(c + 1) * P],
                       start=True, stop=True).then_inc(G_ps, 1)
                rows(0)
                for c in range(T):
                    if c + 1 < T:
                        rows(c + 1)
                    pe.wait_ge(xdt_ready, c + 1)
                    if c >= 2:
                        pe.wait_ge(h_ready, c - 1)
                    mm(ps[0:DST, 6 + c % 2, 0:DIN], xs[:, c, DIN:XB], xdd[:, c % 2, :], start=True, stop=True).then_inc(s_ps, 1)
                    pe.wait_ge(M_ready, c + 1)
                    if c >= 2:
                        pe.wait_ge(y_done, c - 1)
                    for h in range(NH):
                        mm(ps[:, 4 + c % 2, h * HD:(h + 1) * HD], EM[:, c % 2, h, :], xdt[:, c % 2, h * HD:(h + 1) * HD],
                           start=True, stop=False, skip_group_check=True)
                        mm(ps[:, 4 + c % 2, h * HD:(h + 1) * HD], DI[:, h, :], xs[:, c, h * HD:(h + 1) * HD],
                           start=False, stop=True, skip_group_check=True)
                    if c:
                        pe.wait_ge(h_ready, c)
                    mm(ps[:, 4 + c % 2, DIN:2 * DIN], CT[:, c * P:(c + 1) * P], Hst[:, c % 2, :],
                       start=True, stop=True, skip_group_check=True).then_inc(y_ps, 1)
                pe.wait_ge(y_done, T)
                for c in range(T + 1):
                    if c < T:
                        if c >= 2:
                            pe.wait_ge(yT_ready, c - 1)
                        for k in range(2):
                            i = tr(ps[:, c % 2, k * P:(k + 1) * P], sz[:, c, k * P:(k + 1) * P], ident[:])
                        i.then_inc(yT_ps, 1)
                    if c >= 1:
                        e = c - 1
                        pe.wait_ge(yT_ready, e + 1)
                        if e >= 2:
                            pe.wait_ge(mo_read, e - 1)
                        for k in range(2):
                            i = mm(ps[:, 2 + e % 2, 0:D], yT[:, e % 2, k, :], wol[:, k, :], start=(k == 0), stop=(k == 1))
                        i.then_inc(mo_ps, 1)
            if LAYERS > 1:
                mamba()

            def attention(a, q, wv, nv):
                heads, w1, ring = a["heads"], a["w1"], a["ring"]
                pe.wait_ge(x_ready, q)
                if q == 2:
                    for k, (w, av) in enumerate((("W1n", "A1"), ("W2n", "A2"))):
                        mm(ps[:, 4, 2 * k:2 * k + 2], W[w][:], W[av][:], start=True, stop=True, skip_group_check=True)
                        i = mm(ps[:, 4, 4 + 2 * k:6 + 2 * k], W["b12"][:, k:k + 1].broadcast_to([P, P]), W[av][:],
                               start=True, stop=True, skip_group_check=True)
                else:
                    i = mm(ps[:, 4, 0:2], W["W3WT"][:], W["a3"][:], start=True, stop=True)
                i.then_inc(a["u_ps"], 1)
                norm_transposes(q)
                pe.wait_ge(xnT_ready, NB * (q + 1))
                pe.wait_ge(a["u_ready"], a["turn"])
                for t in range(T):
                    if t >= 4:
                        pe.wait_ge(a["v_ready"], t - 3)
                    mm(ps[:, 4 + t % 4, 0:nv], tok(t), wv[:], start=True, stop=True).then_inc(a["v_ps"], 1)
                pe.wait_ge(a["v_ready"], T)
                for h in range(heads):
                    if h:
                        pe.wait_ge(a["row_ready"], NB * h)
                    for t in range(T):
                        i = tr(ps[:, t // 4, (t % 4) * P:(t % 4 + 1) * P],
                               a["VS"][:, t, D + h:D + h + 1].broadcast_to([P, P]), ident[:])
                        if t % 4 == 3:
                            i.then_inc(a["row_ps"], 1)
                pe.wait_ge(a["row_ready"], NB * heads)
                n = 0
                for k in range(heads * NB):
                    h = k // NB
                    if k >= a["sets"]:
                        pe.wait_ge(a["acc_read"], k - a["sets"] + 1)
                    if k % NB == 0:
                        pe.wait_ge(a["xp_ready"], h + 1)
                    for jt in range(T):
                        if n % 3 < 2:
                            pe.wait_ge(a["m2_pool"], n - n // 3 + 1)
                        else:
                            pe.wait_ge(a["m2_dve"], n // 3 + 1)
                        for i in range(4):
                            for s, M in enumerate((a["M1"], a["M2"])):
                                bank = (k % a["sets"]) * 4 * a["banks"] + i * a["banks"] + (s if a["banks"] == 2 else 0)
                                col = s * 3 * w1 if a["banks"] == 1 else 0
                                m = mm(ps[:, bank, col:col + 3 * w1], M[:, n % ring, i * P:(i + 1) * P],
                                       a["XP"][h][:, jt, s, :, :].rearrange("p k c -> p (k c)"),
                                       start=(jt == 0 and (s == 0 or a["banks"] == 2)), stop=(jt == T - 1), skip_group_check=True)
                        m.then_inc(a["m_used"], 1)
                        n += 1
            if LAYERS > 2:
                attention(A1, 2, W["WVu"], D + 4)

            def experts():
                norm_transposes(3)
                pe.wait_ge(xnT_ready, NB * 4)
                for t in range(T):
                    i = mm(ps[:, 4, t * E1:(t + 1) * E1], tok(t), W["wg"][:], start=True, stop=True, skip_group_check=True)
                i.then_inc(g_ps, 1)
                pe.wait_ge(emask_ready, 1)
                for t in range(T):
                    i = tr(ps[0:E1, t // 4, (t % 4) * P:(t % 4 + 1) * P], emask[:, t, :], ident[:])
                    if t % 4 == 3:
                        i.then_inc(emT_ps, 1)
                pe.wait_ge(emT_ready, NB)
                pe.wait_ge(w2e_loaded, 16)
                n_up = n_dn = 0
                units = [(b, e) for b in range(NB) for e in range(E1)]

                def up(u):
                    b, e = units[u]
                    for k in range(2):
                        n = 2 * u + k
                        if n >= 4:
                            pe.wait_ge(h1_ready, n - 3)
                        mm(ps[:, n % 4, :], W["w1e"][:, (2 * e + k) * P:(2 * e + k + 1) * P],
                           XT[:, b * BLK:(b + 1) * BLK], start=True, stop=True).then_inc(h1_ps, 1)

                def down(u):
                    b, e = units[u]
                    pe.wait_ge(h1_ready, 2 * u + 2)
                    if e == 0:
                        if b >= 2:
                            pe.wait_ge(o1_read, (b - 1) * (E1 + 1) - E1)
                        for i in range(4):
                            t = 4 * b + i
                            m = mm(ps[:, 6 + b % 2, i * D:(i + 1) * D], emT[:, t * P:(t + 1) * P], W["b2r"][:],
                                   start=True, stop=True, skip_group_check=True)
                        m.then_inc(o1_ps, 1)
                    prior = u + b + 1 if e else u + b + 1
                    if u >= 2:
                        pe.wait_ge(o1_read, (u - 2) + (u - 2) // E1 + 2)
                    for i in range(4):
                        for k in range(2):
                            m = mm(ps[:, 4 + u % 2, i * D:(i + 1) * D], hT1[:, u % 4, k, i * P:(i + 1) * P],
                                   w2e[:, 2 * e + k, :], start=(k == 0), stop=(k == 1), skip_group_check=True)
                    m.then_inc(o1_ps, 1)
                up(0)
                for u in range(len(units)):
                    if u + 1 < len(units):
                        up(u + 1)
                    down(u)
            if LAYERS > 3:
                experts()

            def cosine():
                norm_transposes(4)
                pe.wait_ge(xnT_ready, NB * 5)
                for t in range(T):
                    if t >= 4:
                        pe.wait_ge(kq_read, t - 3)
                    mm(ps[:, 4 + t % 4, 0:D], tok(t), W["wkT"][:], start=True, stop=True, skip_group_check=True)
                    mm(ps[:, 4 + t % 4, D:2 * D], tok(t), W["wqT"][:], start=True, stop=True,
                       skip_group_check=True).then_inc(kq_ps, 1)
                for b in range(NB):
                    mm(ps[:, b, :], W["wqT"][:], XT[:, b * BLK:(b + 1) * BLK], start=True, stop=True).then_inc(QT_ps, 1)
                pe.wait_ge(QT_ready, NB)
                for t in range(T):
                    pe.wait_ge(kn_ready, 1)
                    i = tr(ps[:, t // 4, (t % 4) * P:(t % 4 + 1) * P], Kt[:, t, :], ident[:])
                    if t % 4 == 3:
                        i.then_inc(KnT_ps, 1)
                pe.wait_ge(KnT_ready, NB)
                pe.wait_ge(xn1_ready, 1)
                pe.wait_ge(kq_read, T)
                items = [(b, jt) for b in range(NB) for jt in range(T)]

                def score(n):
                    b, jt = items[n]
                    if n >= 2:
                        pe.wait_ge(sc_exp, n - 1)
                    mm(ps[:, n % 2, :], QT[:, jt * P:(jt + 1) * P], KnT[:, b * BLK:(b + 1) * BLK],
                       start=True, stop=True).then_inc(sc_ps, 1)

                def apply(n):
                    b, jt = items[n]
                    pe.wait_ge(p_ready, n + 1)
                    if jt == 0 and b:
                        pe.wait_ge(a2_read, b)
                    for i in range(4):
                        m = mm(ps[:, 2 + i, 0:D + 1], Er[:, n % RE, i * P:(i + 1) * P], xn1[:, jt, :],
                               start=(jt == 0), stop=(jt == T - 1))
                    m.then_inc(p_used, 1)
                score(0)
                score(1)
                for n in range(len(items)):
                    if n + 2 < len(items):
                        score(n + 2)
                    apply(n)
            if LAYERS > 4:
                cosine()

            def depths():
                norm_transposes(5)
                pe.wait_ge(xnT_ready, NB * 6)
                for t in range(T):
                    i = mm(ps[:, 4, t:t + 1], tok(t), W["wr"][:], start=True, stop=True, skip_group_check=True)
                i.then_inc(w_ps, 1)
                pe.wait_ge(wcol_ready, 1)
                for t in range(T):
                    i = tr(ps[:, t // 4, (t % 4) * P:(t % 4 + 1) * P], wcol[:, t:t + 1].broadcast_to([P, P]), ident[:])
                    if t % 4 == 3:
                        i.then_inc(wrow_ps, 1)
                pe.wait_ge(wrow_ready, NB)
                HTILES = H2 // P

                def up(b):
                    for k in range(HTILES):
                        n = b * HTILES + k
                        if n >= 4:
                            pe.wait_ge(h2_ready, n - 3)
                        mm(ps[:, n % 4, :], W["w1m"][:, k * P:(k + 1) * P], XT[:, b * BLK:(b + 1) * BLK],
                           start=True, stop=True).then_inc(h2_ps, 1)

                def down(b):
                    pe.wait_ge(h2_ready, (b + 1) * HTILES)
                    for i in range(4):
                        t = 4 * b + i
                        if t >= 4:
                            pe.wait_ge(o2_read, t - 3)
                        for k in range(HTILES):
                            m = mm(ps[:, 4 + t % 4, 0:D], hT2[:, b % 2, k, i * P:(i + 1) * P], W["w2m"][:, k, :],
                                   start=(k == 0), stop=(k == HTILES - 1))
                        m.then_inc(o2_ps, 1)
                up(0)
                for b in range(NB):
                    if b + 1 < NB:
                        up(b + 1)
                    down(b)
            if LAYERS > 5:
                depths()
            if LAYERS > 6:
                attention(A3, 6, W["WVu3"], D + 2)

            def tropical():
                norm_transposes(7)
                pe.wait_ge(xg_in, 16 * 3 * NG)
                pe.wait_ge(sel_ready, 1)

                def spread(bank, sel, g, half, stop=True):
                    for b in range(2):
                        c = half * 2 + b
                        m = mm(ps[:, bank + b, :], sel.broadcast_to([3 * GF, P]), xg[:, g, c * BLK:(c + 1) * BLK],
                               start=True, stop=stop)
                    return m

                def add(bank, src):
                    for b in range(2):
                        m = mm(ps[:, bank + b, :], ident[:], src[:, b * BLK:(b + 1) * BLK], start=False, stop=True)
                    return m

                def pair(j, i, g, first=False):
                    even, odd, diff = selx[:, bass.ds(i * 2, 1)], selx[:, bass.ds(i * 2 + 1, 1)], seld[:, bass.ds(i, 1)]
                    if not first:
                        pe.wait_ge(pair_step, j * 3 - 1)
                    spread(4, odd, g, 0).then_inc(odd_ps, 1)
                    if not first:
                        pe.wait_ge(pair_step, j * 3)
                    spread(6, odd, g, 1).then_inc(odd_ps, 1)
                    if not first:
                        pe.wait_ge(rise_pool, j * 2)
                    spread(0, diff, g, 0).then_inc(diff_ps, 1)
                    spread(2, diff, g, 1).then_inc(diff_ps, 1)
                    pe.wait_ge(odd_copied, j * 2 + 1)
                    spread(4, even, g, 0).then_inc(even_ps, 1)
                    pe.wait_ge(odd_copied, j * 2 + 2)
                    spread(6, odd, g, 0, stop=False)
                    pe.wait_ge(rise_pe, j * 3 + 1)
                    add(6, rise_m[:, 0:N // 2]).then_inc(pair_ps, 1)
                    pe.wait_ge(single_step, j * 2 + 1)
                    spread(4, odd, g, 1, stop=False)
                    pe.wait_ge(rise_pe, j * 3 + 2)
                    add(4, rise_m[:, N // 2:N]).then_inc(pair_ps, 1)
                    pe.wait_ge(pair_step, j * 3 + 1)
                    spread(6, odd, g, 1, stop=False)
                    pe.wait_ge(rise_pe, j * 3 + 3)
                    add(6, rise_m[:, N:]).then_inc(pair_ps, 1)
                for g in range(NG):
                    if g == 0:
                        pair(0, 0, 0, first=True)
                    with pe.Fori(int(g == 0), GF // 2) as i:
                        pair(i + g * (GF // 2), i, g)
                def classical(h):
                    f, g = divmod(h, 2)
                    w = ("Wc", "Wg")[(f + g) % 2]
                    for b in range(NB):
                        if h:
                            pe.wait_ge(c_read, (h - 1) * NB + b + 1)
                        mm(ps[:, b, :], W[w][:, f * P:(f + 1) * P], XT[:, b * BLK:(b + 1) * BLK],
                           start=True, stop=True).then_inc(c_ps, 1)

                def down(n, parts):
                    for b in range(NB):
                        if n:
                            pe.wait_ge(x_summed, n)
                        for t in range(b * TB, (b + 1) * TB):
                            for k, (a, w) in enumerate(parts):
                                m = mm(ps[:, 4 + b, (t % TB) * D:(t % TB + 1) * D], a[:, t * P:(t + 1) * P], W["Wd"][:, w, :],
                                       start=(k == 0), stop=(k == len(parts) - 1))
                        m.then_inc(f_ps, 1)
                pe.wait_ge(rise_pool, D)
                classical(0)
                classical(1)
                pe.wait_ge(c_read, 2 * NB)
                pe.wait_ge(pair_step, 3 * D // 2)
                down(0, [(CL[0], 0)])
                ahead = 2
                for f in range(FT):
                    while ahead < min(2 * f + 6, 2 * FT):
                        classical(ahead)
                        ahead += 1
                    pe.wait_ge(fused_ready, f + 1)
                    if f + 1 < FT:
                        pe.wait_ge(c_read, 2 * (f + 2) * NB)
                        down(f + 1, [(acc[:, f, :], f), (CL[(f + 1) % 2], f + 1)])
                    else:
                        down(f + 1, [(acc[:, f, :], f)])
            if LAYERS > 7:
                tropical()

        @block.scalar
        def _(act):
            A = act.activation

            def ain(i):
                in_turn(act, "act", act_step, i)

            for jt in range(4):
                act.dma_start(stage_adj[:, jt, :], ins["adjT"][jt * P:(jt + 1) * P, :]).then_inc(adj_in[jt], 16)

            def norm(q):
                act.wait_ge(var_ready, q + 1)
                A(lnv[:, 1, :], lnv[:, 0, :], ACT.Sqrt).then_inc(sqrt_ready, 1)
                act.wait_ge(shift_ready, q + 1)
                for t in range(2, T, 3):
                    A(xn[:, t, :], x[:, t, :], ACT.Identity, bias=lnv[:, 3, t:t + 1], scale=lnv[:, 2, t:t + 1]).then_inc(xn_act, 1)
                for b in range(NB):
                    act.wait_ge(xnT_ps, NB * q + b + 1)
                    A(XT[:, b * BLK:(b + 1) * BLK], ps[:, b, :], ACT.Copy).then_inc(xnT_ready, 1)
            norm(0)
            act.wait_ge(v0_ps, 1)
            A(XP0[:, :, 0:D], v0_of_ps, ACT.Copy).then_inc(v0_rounded, 1)
            act.wait_ge(v0_ready, 1)
            A(XP0[:, :, D:2 * D], V0, ACT.Copy).then_inc(v0_rounded, 1)

            def mamba():
                norm(1)
                act.wait_ge(wol_ps, 1)
                for k in range(2):
                    i = A(wol[:, k, :], ps[:, 4, k * P:(k + 1) * P], ACT.Copy, scale=W["nw"][:, k:k + 1])
                i.then_inc(wol_ready, 1)
                def conv_input(u):
                    m = CONV_ORDER[u]
                    if u == 2:
                        act.wait_ge(conv_done, 1)
                    for b in range(NB):
                        act.wait_ge(raw_ps, u * NB + b + 1)
                        A(raw[:, u % 2, KC - 1 + b * BLK:KC - 1 + (b + 1) * BLK], ps[:, 4 * (u % 2) + b, :], ACT.Copy)
                        A(conv[m][:, b * BLK:(b + 1) * BLK], ps[:, 4 * (u % 2) + b, :], ACT.Identity,
                          bias=W["convb"][:, m:m + 1], scale=W["convw"][:, m, KC - 1:KC]).then_inc(raw_read, 1)
                conv_input(0)
                conv_input(1)
                A(Aneg, W["alog"][:], ACT.Exp).then_inc(alog_exp, 1)
                act.wait_ge(sp_e_ready, 1)
                A(small[:, 3, :], small[:, 2, :], ACT.Exp).then_inc(sp_exp, 1)
                act.wait_ge(sp_u_ready, 1)
                A(small[:, 5, :], small[:, 4, :], ACT.Ln).then_inc(sp_ln, 1)
                conv_input(2)
                for u, m in enumerate(CONV_ORDER):
                    act.wait_ge(conv_done, u + 1)
                    A(conv[m], conv[m], ACT.Silu).then_inc(silu_done, 1)
                for c in range(T):
                    act.wait_ge(z_ps, c + 1)
                    A(sz[:, c, :], ps[:, 1 + c % RZ, 0:DIN], ACT.Silu).then_inc(z_read, 1)
                act.wait_ge(acum_ready, 1)
                A(small[:, 6:8, :], small[:, 6:8, :], ACT.Exp).then_inc(decay_ready, 1)
                A(small[:, 8, :], small[:, 9, :], ACT.Exp).then_inc(decay_ready, 1)
                for c in range(T):
                    act.wait_ge(row_ps, c + 1)
                    if c >= 2:
                        act.wait_ge(y_ps, c - 1)
                    for h in range(NH):
                        i = A(EM[:, c % 2, h, :], ps[:, c % 2, h * P:(h + 1) * P], ACT.Exp,
                              bias=small[:, 10, c * NH + h:c * NH + h + 1])
                    i.then_inc(E_ready, 1)
                act.wait_ge(y_done, T)
                for c in range(T):
                    ain(A(yscr[:, 0, :], sz[:, c, :], ACT.Square, accum_out=small[:, 11, c:c + 1]))
                A(small[:, 11, T:2 * T], small[:, 11, 0:T], ACT.Copy).then_inc(sq_done, 1)
                act.wait_ge(yrms_var, 1)
                A(small[:, 11, 2 * T:3 * T], small[:, 11, T:2 * T], ACT.Sqrt).then_inc(yrms_sqrt, 1)
                for c in range(T):
                    act.wait_ge(yT_ps, c + 1)
                    if c >= 2:
                        act.wait_ge(mo_ps, c - 1)
                    A(yT[:, c % 2, :, :].rearrange("p k n -> p (k n)"), ps[:, c % 2, 0:2 * P], ACT.Copy).then_inc(yT_ready, 1)
            if LAYERS > 1:
                mamba()

            def attention(a, q):
                norm(q)
                act.wait_ge(a["arg_ready"], a["turn"])
                A(a["ex"].rearrange("p k h t -> p (k h t)"), a["arg"].rearrange("p k h t -> p (k h t)"), ACT.Exp).then_inc(a["ex_ready"], 1)
                for h in range(a["heads"]):
                    for b in range(NB):
                        act.wait_ge(a["row_ps"], h * NB + b + 1)
                        A(a["row"][h][:, b * BLK:(b + 1) * BLK], ps[:, b, :], ACT.Copy).then_inc(a["row_ready"], 1)
            if LAYERS > 2:
                attention(A1, 2)

            def experts():
                norm(3)
                for b in range(NB):
                    act.wait_ge(emT_ps, b + 1)
                    A(emT[:, b * BLK:(b + 1) * BLK], ps[0:E1, b, :], ACT.Copy).then_inc(emT_ready, 1)
                for u in range(NB * E1):
                    e = u % E1
                    if u >= 4:
                        act.wait_ge(o1_ps, (u - 4) + (u - 4) // E1 + 2)
                    for k in range(2):
                        n = 2 * u + k
                        act.wait_ge(h1_ps, n + 1)
                        A(hT1[:, u % 4, k, :], ps[:, n % 4, :], ACT.Gelu, bias=W["b1c"][:, 2 * e + k:2 * e + k + 1]).then_inc(h1_ready, 1)
            if LAYERS > 3:
                experts()

            def cosine():
                norm(4)
                for b in range(NB):
                    act.wait_ge(QT_ps, b + 1)
                    A(QT[:, b * BLK:(b + 1) * BLK], ps[:, b, :], ACT.Copy).then_inc(QT_ready, 1)
                act.wait_ge(norm_sq, 1)
                A(qs[:, 2:4, :], qs[:, 0:2, :], ACT.Sqrt).then_inc(norm_sqrt, 1)
                for b in range(NB):
                    act.wait_ge(KnT_ps, b + 1)
                    A(KnT[:, b * BLK:(b + 1) * BLK], ps[:, b, :], ACT.Copy).then_inc(KnT_ready, 1)
                for n in range(NB * T):
                    jt = n % T
                    act.wait_ge(sc_ps, n + 1)
                    if n >= RE:
                        act.wait_ge(p_used, n - RE + 1)
                    A(Er[:, n % RE, :], ps[:, n % 2, :], ACT.Exp, scale=qs[:, 5, jt:jt + 1]).then_inc(sc_exp, 1)
            if LAYERS > 4:
                cosine()

            def depths():
                norm(5)
                for b in range(NB):
                    act.wait_ge(wrow_ps, b + 1)
                    A(wrow[:, b * BLK:(b + 1) * BLK], ps[:, b, :], ACT.Copy).then_inc(wrow_ready, 1)
                for n in range(NB * (H2 // P)):
                    b, k = divmod(n, H2 // P)
                    act.wait_ge(h2_ps, n + 1)
                    if b >= 2 and k == 0:
                        act.wait_ge(o2_ps, 4 * (b - 1))
                    A(hT2[:, b % 2, k, :], ps[:, n % 4, :], ACT.Gelu_apprx_tanh, bias=W["b1m"][:, k:k + 1]).then_inc(h2_ready, 1)
            if LAYERS > 5:
                depths()
            if LAYERS > 6:
                attention(A3, 6)
                act.wait_ge(elu_ready, 1)
                A(elu_m, elu_m, ACT.Exp).then_inc(elu_exp, 1)

            def tropical():
                norm(7)
                A(sa[:, 0, :], W["alpha"][:], ACT.Sigmoid).then_inc(sa_ready, 1)

                act.wait_ge(rise_table, 1)

                def pair(j, slot, before=2):
                    A(bias[:, slot, :], rise[:, bass.ds(j, 1), :].rearrange("p o k -> p (o k)"), ACT.Copy).then_inc(bias_ready, 1)
                    if before > 1:
                        act.wait_ge(sum_ready, j * 2 - 2)
                    for n in range(2):
                        h = slice(n * N // 2, (n + 1) * N // 2)
                        act.wait_ge(odd_ps, j * 2 + (n + 1))
                        A(oddc[:, slot, h], ps_wide[:, 1, h], ACT.Copy).then_inc(odd_copied, 1)
                    act.wait_ge(bias_ready, j + 1)
                    for n, (f, half) in enumerate(((2, 0), (2, 1), (3, 1))):
                        if n < 2:
                            act.wait_ge(diff_ps, j * 2 + (n + 1))
                        A(rise_m[:, n * N // 2:(n + 1) * N // 2], ps_wide[:, 0, half * N // 2:(half + 1) * N // 2], ACT.Relu,
                          bias=bias[:, slot, f:f + 1]).then_inc(rise_pe, 1)
                    if before:
                        act.wait_ge(sum_step, j * 2 - 1)
                    A(rise0, ps_wide[:, 0, :], ACT.Relu, bias=bias[:, slot, 0:1]).then_inc(rise_pool, 1)
                    A(rise1[:, slot, :], ps_wide[:, 0, :], ACT.Relu, bias=bias[:, slot, 1:2]).then_inc(rise_pool, 1)
                pair(0, 0, before=0)
                pair(1, 1, before=1)
                with act.Fori(1, D // 4) as i:
                    for s in range(2):
                        pair(i * 2 + s, s)

                def classical(h):
                    f, g = divmod(h, 2)
                    dst, fn, b0 = ((CL, ACT.Gelu, "bc"), (G, ACT.Sigmoid, "bgt"))[(f + g) % 2]
                    for b in range(NB):
                        act.wait_ge(c_ps, h * NB + b + 1)
                        A(dst[f % 2][:, b * BLK:(b + 1) * BLK], ps[:, b, :], fn, bias=W[b0][:, f:f + 1]).then_inc(c_read, 1)
                classical(0)
                classical(1)
                act.wait_ge(lines_table, 4)
                act.wait_ge(sum_step, D)
                act.wait_ge(pair_step, 3 * D // 2)
                act.wait_ge(single_step, D)
                for f in range(FT):
                    for k in range(6):
                        n, side, q = 6 * f + k, k // 3, k % 3
                        of = (2 * q + 1, 2 * q)[side]
                        if k == 3 and f + 1 < FT:
                            if f:
                                act.wait_ge(fused_ready, f)
                                act.wait_ge(f_ps, NB * f)
                            classical(2 * f + 2)
                        if k == 4 and f + 1 < FT:
                            classical(2 * f + 3)
                        if n >= 3:
                            act.wait_ge(pair_used, n - 2)
                        A(line_a[n % 3], acc[:, f, :], ACT.Relu, bias=doffs[:, side, f, q:q + 1],
                          scale=dslope[:, side, f, q:q + 1]).then_inc(line_ready, 1)
                        A(line_b[n % 3], acc[:, f, :], ACT.Identity, bias=offs[:, side, f, of:of + 1],
                          scale=W[("slx", "slc")[side]][:, f, of:of + 1]).then_inc(line_ready, 1)
            if LAYERS > 7:
                tropical()

        @block.vector
        def _(dve):
            V = nc.vector

            def din(i):
                in_turn(dve, "dve", dve_step, i)

            def newton_rsqrt(v, s, r, tmp):
                din(V.reciprocal(r, s))
                din(V.tensor_tensor(tmp, v, r, ALU.mult))
                din(V.tensor_tensor(tmp, tmp, s, ALU.add))
                din(V.tensor_scalar(tmp, tmp, 0.5, None, ALU.mult))
                din(V.reciprocal(r, tmp))

            counted = set()

            def moments(tiles):
                for t in tiles:
                    i = V.bn_stats(stats[:, t, :], x[:, t, :])
                    counted.add(t)
                return i

            def norm(q):
                if DEBUG and q:
                    dve.wait_ge(dbg_done, 16 * q)
                din(moments([t for t in range(T) if t not in counted]))
                counted.clear()
                for t in range(T):
                    i = V.bn_aggr(mv[:, t, :], stats[:, t, :])
                din(i)
                V.tensor_scalar(lnv[:, 0, :], mv[:, :, 1], EPS, None, ALU.add).then_inc(var_ready, 1)
                dve.wait_ge(sqrt_ready, q + 1)
                newton_rsqrt(lnv[:, 0, :], lnv[:, 1, :], lnv[:, 2, :], lnv[:, 3, :])
                V.scalar_tensor_tensor(lnv[:, 3, :], mv[:, :, 0], -1.0, lnv[:, 2, :], ALU.mult, ALU.mult).then_inc(shift_ready, 1)
                for t in range(T):
                    if t % 3 < 2:
                        V.tensor_scalar(xn[:, t, :], x[:, t, :], mv[:, t, 0:1], lnv[:, 2, t:t + 1], ALU.subtract, ALU.mult).then_inc(xn_ready, 1)

            dve.wait_ge(x_loaded, 16)
            norm(0)

            def cast(jt):
                dve.wait_ge(adj_in[jt % 4], 16 * (jt // 4 + 1))
                V.tensor_scalar(mask[:, jt, :], stage_adj[:, jt % 4, :], 1.0, None, ALU.is_equal).then_inc(mask_ready, 1)
            for jt in range(4):
                cast(jt)
            dve.wait_ge(v0_rounded, 1)
            V.tensor_tensor(V0, v0_of_ps, XP0[:, :, 0:D], ALU.subtract).then_inc(v0_ready, 1)
            cast(4)
            cast(5)
            dve.wait_ge(v0_rounded, 2)
            din(V.tensor_tensor(XP0[:, :, 2 * D:3 * D], V0, XP0[:, :, D:2 * D], ALU.subtract))
            V.memset(XP0[:, :, 3 * D:3 * D + 2], 1.0).then_inc(xp0_ready, 1)
            for jt in range(6, T):
                cast(jt)
                if jt == 8:
                    dve.wait_ge(w0_loaded, 32)
                    din(V.tensor_tensor(x[:, :, :], x[:, :, :], W["b0"][:].unsqueeze(1).broadcast_to([P, T, D]), ALU.add))
            for t in range(T):
                if t:
                    dve.wait_ge(agg_read, t)
                    moments([t - 1])
                dve.wait_ge(agg_ps, t + 1)
                pv = ps[:, t % 8, 0:3 * D].rearrange("p (k d) -> p d k", k=3)
                V.tensor_copy(deg[:, t:t + 1], ps[:, t % 8, 3 * D:3 * D + 1])
                din(V.tensor_reduce(R0[:, t % 8, :], pv, AX, ALU.add))
                din(V.reciprocal(rdeg[:, t:t + 1], deg[:, t:t + 1]))
                i = V.scalar_tensor_tensor(x[:, t, :], R0[:, t % 8, :], rdeg[:, t:t + 1], x[:, t, :], ALU.mult, ALU.add)
                i.then_inc(agg_read if t < T - 1 else x_ready, 1)
            dve.wait_ge(x_ready, 1)
            dve.wait_ge(w_loaded, 16 * N_W)

            def mamba():
                norm(1)
                for h in range(NH):
                    i = V.tensor_scalar(DI[:, h, :], ident[:], W["Dh"][:, h:h + 1], None, ALU.mult)
                i.then_inc(DI_ready, 1)
                v = [small[:, k, :] for k in range(12)]

                def convolve(u):
                    m = CONV_ORDER[u]
                    dve.wait_ge(raw_read, (u + 1) * NB)
                    for k in range(KC - 1):
                        i = V.scalar_tensor_tensor(conv[m], raw[:, u % 2, k:k + N], W["convw"][:, m, k:k + 1], conv[m],
                                                   ALU.mult, ALU.add)
                        if k < KC - 2:
                            din(i)
                    i.then_inc(conv_done, 1)

                def h4(u):
                    return u.rearrange("p (c h) -> p c h", h=NH)
                dve.wait_ge(dt_ps, 1)
                V.tensor_tensor(h4(v[0]), h4(ps[:, 5, 0:T * NH]), W["dtb"][:].unsqueeze(1).broadcast_to([P, T, NH]), ALU.add).then_inc(dt_read, 1)
                dve.wait_ge(dt_read, 1)
                din(V.tensor_scalar(v[1], v[0], -1.0, None, ALU.mult))
                V.tensor_tensor(v[2], v[0], v[1], ALU.min).then_inc(sp_e_ready, 1)
                dve.wait_ge(consts, 3)
                convolve(0)
                dve.wait_ge(sp_exp, 1)
                V.tensor_scalar(v[4], v[3], 1.0, None, ALU.add).then_inc(sp_u_ready, 1)
                dve.wait_ge(sp_u_ready, 1)
                din(V.tensor_scalar(v[6], v[4], -1.0, None, ALU.add))
                din(V.tensor_tensor(v[3], v[3], v[6], ALU.subtract))
                din(V.reciprocal(v[7], v[4]))
                din(V.tensor_tensor(v[3], v[3], v[7], ALU.mult))
                convolve(1)
                dve.wait_ge(sp_ln, 1)
                din(V.tensor_tensor(v[5], v[5], v[3], ALU.add))
                din(V.scalar_tensor_tensor(v[0], v[0], 0.0, v[5], ALU.max, ALU.add))
                dve.wait_ge(alog_exp, 1)
                din(V.tensor_tensor(h4(v[1]), h4(v[0]), Aneg.unsqueeze(1).broadcast_to([P, T, NH]), ALU.mult))
                V.tensor_scalar(v[1], v[1], -1.0, None, ALU.mult).then_inc(dA_ready, 1)
                dve.wait_ge(dA_ready, 1)
                convolve(2)
                dve.wait_ge(acum_ps, 1)
                din(V.tensor_copy(v[9], ps[:, 0, 0:T * NH]))
                V.tensor_copy(v[7], ps[:, 0, T * NH:2 * T * NH])
                din(V.tensor_scalar(v[10], v[9], -1.0, None, ALU.mult))
                V.tensor_tensor(v[6], v[7], v[9], ALU.subtract).then_inc(acum_ready, 1)
                for c in range(T):
                    dve.wait_ge(xs_ps, c + 1)
                    V.tensor_copy(xs[:, c, :], ps[:, 6 + c % 2, 0:XB]).then_inc(xs_ready, 1)
                dve.wait_ge(decay_ready, 2)

                def weigh(c):
                    dve.wait_ge(E_ready, c + 1)
                    dve.wait_ge(G_ps, c + 1)
                    V.tensor_tensor(EM[:, c % 2, :, :], EM[:, c % 2, :, :],
                                    ps[:, 2 + c % 2, 0:P].unsqueeze(1).broadcast_to([P, NH, P]), ALU.mult).then_inc(M_ready, 1)
                weigh(0)
                hq = "p (h q) -> p h q"
                for c in range(T):
                    cd = small[0:DST, 7, c * NH:(c + 1) * NH]
                    ea = small[:, 8, c * NH:(c + 1) * NH]
                    if c + 1 < T:
                        Hn = Hst[:, (c + 1) % 2, :]
                        if c:
                            dve.wait_ge(h_ready, c)
                        din(V.tensor_tensor(Hn.rearrange(hq, h=NH), Hst[:, c % 2, :].rearrange(hq, h=NH), bcast(cd, HD), ALU.mult))
                        dve.wait_ge(s_ps, c + 1)
                        V.tensor_tensor(Hn, Hn, ps[0:DST, 6 + c % 2, 0:DIN], ALU.add).then_inc(h_ready, 1)
                        weigh(c + 1)
                    dve.wait_ge(y_ps, c + 1)
                    if c:
                        dve.wait_ge(y_done, c)
                    din(V.tensor_tensor(yscr[:, 1, :].rearrange(hq, h=NH), ps[:, 4 + c % 2, DIN:2 * DIN].rearrange(hq, h=NH), bcast(ea, HD), ALU.mult))
                    din(V.tensor_tensor(yscr[:, 1, :], yscr[:, 1, :], ps[:, 4 + c % 2, 0:DIN], ALU.add))
                    V.tensor_tensor(sz[:, c, :], sz[:, c, :], yscr[:, 1, :], ALU.mult).then_inc(y_done, 1)
                dve.wait_ge(sq_done, 1)
                k = small[:, 11, :]
                V.tensor_scalar(k[:, T:2 * T], k[:, T:2 * T], 1.0 / DIN, EPS, ALU.mult, ALU.add).then_inc(yrms_var, 1)
                dve.wait_ge(yrms_sqrt, 1)
                newton_rsqrt(k[:, T:2 * T], k[:, 2 * T:3 * T], k[:, 3 * T:4 * T], k[:, 0:T])
                din(V.tensor_tensor(x[:, :, :], x[:, :, :], W["blin"][:].unsqueeze(1).broadcast_to([P, T, D]), ALU.add))
                for c in range(T):
                    if c:
                        dve.wait_ge(mo_read, c)
                        moments([c - 1])
                    dve.wait_ge(mo_ps, c + 1)
                    V.scalar_tensor_tensor(x[:, c, :], ps[:, 2 + c % 2, 0:D], k[:, 3 * T + c:3 * T + c + 1], x[:, c, :],
                                           ALU.mult, ALU.add).then_inc(mo_read if c < T - 1 else x_ready, 1)
                dve.wait_ge(x_ready, 2)
            if LAYERS > 1:
                mamba()

            def attention(a, q, nv):
                heads, dh, w1, ring, VS = a["heads"], a["dh"], a["w1"], a["ring"], a["VS"]
                dve.wait_ge(a["u_ps"], a["turn"])
                if q == 2:
                    V.tensor_copy(W["WVu"][:, D:D + 4], ps[:, 4, 0:4])
                    i = V.tensor_copy(W["vbias"][:, D:D + 4], ps[:, 4, 4:8])
                else:
                    i = V.tensor_copy(W["WVu3"][:, D:D + 2], ps[:, 4, 0:2])
                i.then_inc(a["u_ready"], 1)
                norm(q)
                for t in range(T):
                    dve.wait_ge(a["v_ps"], t + 1)
                    if q == 2:
                        V.tensor_tensor(VS[:, t, :], ps[:, 4 + t % 4, 0:nv], W["vbias"][:], ALU.add).then_inc(a["v_ready"], 1)
                    else:
                        V.tensor_copy(VS[:, t, :], ps[:, 4 + t % 4, 0:nv]).then_inc(a["v_ready"], 1)
                dve.wait_ge(a["v_ready"], T)
                s1 = VS[:, :, D:D + heads].rearrange("p t h -> p h t")
                s2 = VS[:, :, D + heads:D + 2 * heads].rearrange("p t h -> p h t")
                V.tensor_reduce(a["smax"], s2, AX, ALU.max).then_inc(a["smax_ready"], 1)
                din(V.tensor_scalar(a["thr"], s2, -1.0, None, ALU.mult))
                dve.wait_ge(a["S_ready"], a["turn"])
                Sb = bcast(a["S"], T)
                arg = a["arg"]
                din(V.tensor_tensor(arg[:, 0, :, :], s2, Sb, ALU.subtract))
                din(V.tensor_tensor(a["tt"], s1, Sb, ALU.add))
                din(V.tensor_scalar(arg[:, 1, :, :], arg[:, 0, :, :], 0.2, None, ALU.mult))
                din(V.scalar_tensor_tensor(a["cc"], a["tt"], 0.2, a["tt"], ALU.mult, ALU.max))
                din(V.tensor_tensor(arg[:, 2, :, :], a["tt"], a["cc"], ALU.subtract))
                V.scalar_tensor_tensor(arg[:, 3, :, :], a["tt"], 0.2, a["cc"], ALU.mult, ALU.subtract).then_inc(a["arg_ready"], 1)
                dve.wait_ge(a["ex_ready"], a["turn"])
                ex = a["ex"]

                def values(h):
                    Fv, XP = a["Fv"], a["XP"][h]
                    for k in range(2):
                        V.tensor_tensor(Fv[:, :, k, 0:dh], VS[:, :, h * dh:(h + 1) * dh], bcast(ex[:, k, h, :], dh), ALU.mult)
                        i = V.tensor_copy(Fv[:, :, k, dh:w1], ex[:, k, h, :].unsqueeze(2))
                    din(i)
                    din(V.tensor_copy(XP[:, :, :, 0, :], Fv))
                    din(V.tensor_tensor(Fv, Fv, XP[:, :, :, 0, :], ALU.subtract))
                    din(V.tensor_copy(XP[:, :, :, 1, :], Fv))
                    V.tensor_tensor(XP[:, :, :, 2, :], Fv, XP[:, :, :, 1, :], ALU.subtract).then_inc(a["xp_ready"], 1)
                    dve.wait_ge(a["xp_ready"], h + 1)
                values(0)

                def masks(k, jt):
                    h, b = divmod(k, NB)
                    n = k * T + jt
                    if jt == 0:
                        dve.wait_ge(a["row_ready"], NB * h + b + 1)
                    if n >= ring:
                        dve.wait_ge(a["m_used"], n - ring + 1)
                    mk = mask[:, jt, b * BLK:(b + 1) * BLK]
                    V.scalar_tensor_tensor(a["M1"][:, n % ring, :], a["row"][h][:, b * BLK:(b + 1) * BLK],
                                           a["thr"][:, h, jt:jt + 1], mk, ALU.is_ge, ALU.mult).then_inc(a["m1_ready"], 1)
                    if n and n % 3 == 0:
                        other(n - 1)

                def other(n):
                    b, jt = n // T % NB, n % T
                    dve.wait_ge(a["m1_ready"], n + 1)
                    V.tensor_tensor(a["M2"][:, n % ring, :], mask[:, jt, b * BLK:(b + 1) * BLK], a["M1"][:, n % ring, :],
                                    ALU.subtract).then_inc(a["m2_dve"], 1)

                def evacuate(k):
                    h, b = divmod(k, NB)
                    dve.wait_ge(a["m_used"], (k + 1) * T)
                    base = (k % a["sets"]) * 4 * a["banks"]
                    for i in range(4):
                        if a["banks"] == 1:
                            m = V.tensor_reduce(a["R"][:, i, :, :], ps[:, base + i, 0:6 * w1].rearrange("p (s k c) -> p s c k", s=2, k=3), AX, ALU.add)
                        else:
                            for s in range(2):
                                m = V.tensor_reduce(a["R"][:, i, s, :], ps[:, base + 2 * i + s, 0:3 * w1].rearrange("p (k c) -> p c k", k=3), AX, ALU.add)
                    m.then_inc(a["acc_read"], 1)
                    dve.wait_ge(a["acc_read"], k + 1)
                    for s in range(2):
                        m = V.tensor_tensor(a["R"][:, :, s, :], a["R"][:, :, s, :], bcast(ex[:, 2 + s, h, 4 * b:4 * b + 4], w1), ALU.mult)
                    din(m)
                    din(V.tensor_tensor(a["num"], a["R"][:, :, 0, :], a["R"][:, :, 1, :], ALU.add))
                    din(V.reciprocal(a["rd"], a["num"][:, :, dh]))
                    if q == 6:
                        m = V.tensor_tensor(h3[:, 4 * b:4 * b + 4, :], a["num"][:, :, 0:dh], bcast(a["rd"], dh), ALU.mult)
                        din(m)
                    else:
                        din(V.tensor_tensor(a["num"][:, :, 0:dh], a["num"][:, :, 0:dh], bcast(a["rd"], dh), ALU.mult))
                        xv = x[:, 4 * b:4 * b + 4, h * dh:(h + 1) * dh]
                        m = V.tensor_tensor(xv, xv, a["num"][:, :, 0:dh], ALU.add)
                        if k == heads * NB - 1:
                            m.then_inc(x_ready, 1)
                            dve.wait_ge(x_ready, q + 1)
                for k in range(heads * NB):
                    for jt in range(T):
                        masks(k, jt)
                        if jt == ring - 1 and k:
                            evacuate(k - 1)
                    if k == 0 and heads > 1:
                        values(1)
                evacuate(heads * NB - 1)
            if LAYERS > 2:
                attention(A1, 2, D + 4)

            def experts():
                norm(3)
                dve.wait_ge(g_ps, 1)
                V.memset(gates[:, :, E1:], FILL)
                V.memset(top8, FILL)
                din(V.tensor_tensor(gates[:, :, 0:E1], ps[:, 4, 0:T * E1].rearrange("p (t e) -> p t e", e=E1),
                                    W["bg"][:].unsqueeze(1).broadcast_to([P, T, E1]), ALU.add))
                for t in range(T):
                    i = V.max(emask[:, t, :], gates[:, t, 0:E1])
                din(i)
                din(V.tensor_copy(top8[:, :, 0:2], emask[:, :, 0:2]))
                for t in range(T):
                    i = V.match_replace(out=marked[:, t, :], in_to_replace=top8[:, t, :], in_values=gates[:, t, :], imm_value=-FILL)
                din(i)
                V.tensor_scalar(emask, marked[:, :, 0:E1], -FILL, None, ALU.is_equal).then_inc(emask_ready, 1)
                dve.wait_ge(emask_ready, 1)
                n = 0
                for u in range(NB * E1):
                    b, e = divmod(u, E1)
                    xb = x[:, 4 * b:4 * b + 4, :]
                    if e == 0:
                        dve.wait_ge(o1_ps, n + 1)
                        n += 1
                        V.tensor_tensor(xb, xb, ps[:, 6 + b % 2, :].rearrange("p (i d) -> p i d", i=4), ALU.add).then_inc(o1_read, 1)
                        dve.wait_ge(o1_read, n)
                    dve.wait_ge(o1_ps, n + 1)
                    n += 1
                    for i in range(4):
                        m = V.scalar_tensor_tensor(x[:, 4 * b + i, :], ps[:, 4 + u % 2, i * D:(i + 1) * D],
                                                   emask[:, 4 * b + i, e:e + 1], x[:, 4 * b + i, :], ALU.mult, ALU.add)
                    m.then_inc(o1_read if u < NB * E1 - 1 else x_ready, 1)
                    dve.wait_ge(*((o1_read, n) if u < NB * E1 - 1 else (x_ready, 4)))
                    if e == E1 - 1 and b < NB - 1:
                        moments(range(4 * b, 4 * b + 4))
            if LAYERS > 3:
                experts()

            def cosine():
                norm(4)
                for t in range(T):
                    dve.wait_ge(kq_ps, t + 1)
                    V.tensor_copy(Kt[:, t, :], ps[:, 4 + t % 4, 0:D])
                    din(V.tensor_copy(Er[:, 0, 0:D], ps[:, 4 + t % 4, D:2 * D]))
                    V.scalar_tensor_tensor(sqj, Er[:, 0, 0:D], 1.0, Er[:, 0, 0:D], ALU.mult, ALU.mult, accum_out=qs[:, 1, t:t + 1])
                    din(V.scalar_tensor_tensor(Er[:, 1, 0:D], Kt[:, t, :], 1.0, Kt[:, t, :], ALU.mult, ALU.mult, accum_out=qs[:, 0, t:t + 1]))
                    V.tensor_copy(ab[:, 3, t:t + 1], qs[:, 0, t:t + 1]).then_inc(kq_read, 1)
                din(V.tensor_scalar(qs[:, 6:8, :], qs[:, 0:2, :], 1e-30, None, ALU.max))
                V.tensor_copy(qs[:, 0:2, :], qs[:, 6:8, :]).then_inc(norm_sq, 1)
                dve.wait_ge(norm_sqrt, 1)
                din(V.reciprocal(qs[:, 4:6, :], qs[:, 2:4, :]))
                din(V.tensor_tensor(qs[:, 6:8, :], qs[:, 0:2, :], qs[:, 4:6, :], ALU.mult))
                din(V.tensor_tensor(qs[:, 6:8, :], qs[:, 6:8, :], qs[:, 2:4, :], ALU.add))
                din(V.tensor_scalar(qs[:, 6:8, :], qs[:, 6:8, :], 0.5, 1e-4, ALU.mult, ALU.max))
                din(V.reciprocal(qs[:, 4:6, :], qs[:, 6:8, :]))
                V.tensor_tensor(Kt, Kt, bcast(qs[:, 4, :], D), ALU.mult).then_inc(kn_ready, 1)
                V.memset(xn1[:, :, D:D + 1], 1.0)
                V.tensor_copy(xn1[:, :, 0:D], xn[:, :, :]).then_inc(xn1_ready, 1)
                din(V.tensor_scalar(ab[:, 0, :], deg[:], 0.0, 0.5, ALU.is_gt, ALU.mult))
                din(V.tensor_scalar(ab[:, 1, :], ab[:, 0, :], -1.0, 1.0, ALU.mult, ALU.add))
                for t in range(T):
                    i = V.scalar_tensor_tensor(x[:, t, :], xn[:, t, :], ab[:, 1, t:t + 1], x[:, t, :], ALU.mult, ALU.add)
                din(i)

                def evacuate(b):
                    dve.wait_ge(p_used, T * (b + 1))
                    for i in range(4):
                        m = V.reciprocal(ab[:, 2, 4 * b + i:4 * b + i + 1], ps[:, 2 + i, D:D + 1])
                    din(m)
                    din(V.tensor_tensor(ab[:, 2, 4 * b:4 * b + 4], ab[:, 2, 4 * b:4 * b + 4], ab[:, 0, 4 * b:4 * b + 4], ALU.mult))
                    for i in range(4):
                        t = 4 * b + i
                        m = V.scalar_tensor_tensor(x[:, t, :], ps[:, 2 + i, 0:D], ab[:, 2, t:t + 1], x[:, t, :], ALU.mult, ALU.add)
                    m.then_inc(a2_read if b < NB - 1 else x_ready, 1)
                for n in range(NB * T):
                    b, jt = divmod(n, T)
                    dve.wait_ge(sc_exp, n + 1)
                    V.tensor_tensor(Er[:, n % RE, :], Er[:, n % RE, :], mask[:, jt, b * BLK:(b + 1) * BLK], ALU.mult).then_inc(p_ready, 1)
                    if jt == 1 and b:
                        evacuate(b - 1)
                    if jt == 2 and b:
                        dve.wait_ge(a2_read, b)
                        moments(range(4 * (b - 1), 4 * b))
                evacuate(NB - 1)
                dve.wait_ge(x_ready, 5)
            if LAYERS > 4:
                cosine()

            def depths():
                norm(5)
                dve.wait_ge(w_ps, 1)
                V.tensor_scalar(wcol, ps[:, 4, 0:T], W["br"][:], None, ALU.add).then_inc(wcol_ready, 1)
                din(V.tensor_tensor(x[:, :, :], x[:, :, :], xn[:, :, :], ALU.add))
                dve.wait_ge(wrow_ready, NB)
                din(V.memset(rank, 0.0))
                dve.wait_ge(wcol_ready, 1)
                for t in range(T):
                    w = wcol[:, t:t + 1]
                    a0, a1 = t * P, (t + 1) * P
                    if t:
                        V.tensor_scalar(junk[:, 0:a0], wrow[:, 0:a0], w, None, ALU.is_ge, ALU.add, accum_out=rank[:, 0, t:t + 1])
                    if t < T - 1:
                        V.tensor_scalar(junk[:, a1:N], wrow[:, a1:N], w, None, ALU.is_gt, ALU.add, accum_out=rank[:, 1, t:t + 1])
                    V.scalar_tensor_tensor(junk[:, a0:a1], wrow[:, a0:a1], w, tri[:], ALU.is_ge, ALU.mult, accum_out=rank[:, 2, t:t + 1])
                    din(V.scalar_tensor_tensor(junk[:, N:N + P], wrow[:, a0:a1], w, tric[:], ALU.is_gt, ALU.mult, accum_out=rank[:, 3, t:t + 1]))
                din(V.tensor_tensor(rank[:, 0:2, :], rank[:, 0:2, :], rank[:, 2:4, :], ALU.add))
                din(V.tensor_tensor(rank[:, 0, :], rank[:, 0, :], rank[:, 1, :], ALU.add))
                din(V.scalar_tensor_tensor(sw, rank[:, 0, :], float(KSEL), wcol, ALU.is_lt, ALU.mult))
                for t in range(T):
                    dve.wait_ge(o2_ps, t + 1)
                    din(V.tensor_tensor(junk[:, 0:D], ps[:, 4 + t % 4, 0:D], W["b2m"][:], ALU.add))
                    V.scalar_tensor_tensor(x[:, t, :], junk[:, 0:D], sw[:, t:t + 1], x[:, t, :], ALU.mult,
                                           ALU.add).then_inc(o2_read if t < T - 1 else x_ready, 1)
                    if t < T - 1:
                        dve.wait_ge(o2_read, t + 1)
                        moments([t])
                dve.wait_ge(x_ready, 6)
            if LAYERS > 5:
                depths()

            def elu():
                V.tensor_scalar(elu_m, h3, 0.0, None, ALU.min).then_inc(elu_ready, 1)
                din(V.scalar_tensor_tensor(x[:, :, :], h3, 0.0, x[:, :, :], ALU.max, ALU.add))
                dve.wait_ge(elu_exp, 1)
                V.scalar_tensor_tensor(x[:, :, :], elu_m, -1.0, x[:, :, :], ALU.add, ALU.add).then_inc(x_ready, 1)
                dve.wait_ge(x_ready, 7)
            if LAYERS > 6:
                attention(A3, 6, D + 2)
                elu()

            def tropical():
                norm(7)
                for f in range(FT):
                    V.memset(acc[:, f, :], FILL).then_inc(fill_done, 1)
                dve.wait_ge(xn_ready, 8 * 11)
                dve.wait_ge(xn_act, 8 * 5)
                V.tensor_tensor(x[:, :, :], x[:, :, :], W["bd"][:].unsqueeze(1).broadcast_to([P, T, D]),
                                ALU.add).then_inc(bd_added, 1)
                dve.wait_ge(fill_done, FT)
                dve.wait_ge(xnT_ready, 8 * NB)
                din(V.tensor_copy(xp3[:, 0, :], XT))
                din(V.tensor_tensor(res, XT, xp3[:, 0, :], ALU.subtract))
                din(V.tensor_copy(xp3[:, 1, :], res))
                V.tensor_tensor(rise[:].rearrange("p j f -> p f j"), W["Wt"][:, :, 0:D:2], W["Wt"][:, :, 1:D:2],
                                ALU.subtract).then_inc(rise_table, 1)
                V.tensor_tensor(xp3[:, 2, :], res, xp3[:, 1, :], ALU.subtract).then_inc(xp3_ready, 1)
                for side, sl in enumerate((W["slx"], W["slc"])):
                    i = V.tensor_tensor(offs[:, side], sl[:], bcast(W["bt"][:], PP), ALU.mult)
                din(i)
                for side, of in enumerate((W["ofx"], W["ofc"])):
                    i = V.tensor_tensor(offs[:, side], offs[:, side], of[:], ALU.add)
                din(i)
                for side, sl in enumerate((W["slx"], W["slc"])):
                    V.tensor_tensor(dslope[:, side], sl[:, :, 0:PP:2], sl[:, :, 1:PP:2], ALU.subtract).then_inc(lines_table, 1)
                V.tensor_tensor(doffs[:], offs[:, :, :, 0:PP:2], offs[:, :, :, 1:PP:2], ALU.subtract).then_inc(lines_table, 1)
                dve.wait_ge(sa_ready, 1)
                V.tensor_scalar(sa[:, 1, :], sa[:, 0, :], -1.0, 1.0, ALU.mult, ALU.add).then_inc(lines_table, 1)
                lo, hi = slice(0, N // 2), slice(N // 2, N)

                def step(f, cols, src, feature):
                    return V.scalar_tensor_tensor(acc[:, f, cols], src, W["Wt"][:, f, bass.ds(feature, 1)],
                                                  acc[:, f, cols], ALU.add, ALU.max)

                def last_sum(j, slot, f, second=False):
                    dve.wait_ge(sum_ready, j * 2 + (f + 1))
                    if second:
                        dve.wait_ge(sum_step, j * 2 + (f - 1))
                    step(f, slice(0, N), rise1[:, slot, :] if f else rise0, j * 2 + 1).then_inc(sum_step, 1)

                def pair(j, slot, before=2):
                    dve.wait_ge(even_ps, j + 1)
                    if before:
                        dve.wait_ge(single_step, j * 2)
                    step(3, lo, ps_wide[:, 1, lo], j * 2).then_inc(single_step, 1)
                    if before:
                        last_sum(j - 1, 1 - slot, 0, second=before > 1)
                    dve.wait_ge(pair_ps, j * 3 + 1)
                    if before:
                        dve.wait_ge(pair_step, j * 3 - 2)
                    step(2, lo, ps_wide[:, 1, hi], j * 2 + 1).then_inc(pair_step, 1)
                    dve.wait_ge(single_step, j * 2 + 1)
                    step(3, lo, oddc[:, slot, lo], j * 2 + 1).then_inc(single_step, 1)
                    dve.wait_ge(pair_ps, j * 3 + 2)
                    if before:
                        dve.wait_ge(pair_step, j * 3 - 1)
                    step(2, hi, ps_wide[:, 1, lo], j * 2 + 1).then_inc(pair_step, 1)
                    dve.wait_ge(pair_ps, j * 3 + 3)
                    if before:
                        dve.wait_ge(pair_step, j * 3)
                    step(3, hi, ps_wide[:, 1, hi], j * 2 + 1).then_inc(pair_step, 1)
                    if before:
                        last_sum(j - 1, 1 - slot, 1, second=before > 1)
                pair(0, 0, before=0)
                pair(1, 1, before=1)
                with dve.Fori(1, D // 4) as i:
                    for s in range(2):
                        pair(i * 2 + s, s)
                for f in range(2):
                    last_sum(D // 2 - 1, 1, f, second=True)
                dve.wait_ge(sum_step, D)
                dve.wait_ge(pair_step, 3 * D // 2)
                dve.wait_ge(single_step, D)
                used = 0

                def take(dst, op):
                    nonlocal used
                    dve.wait_ge(pair_line, used + 1)
                    V.tensor_tensor(dst, dst, line_a[used % 3], op).then_inc(pair_used, 1)
                    used += 1
                    dve.wait_ge(pair_used, used)

                def own_line(dst, side, f, p):
                    din(V.tensor_scalar(dst, acc[:, f, :], W[("slx", "slc")[side]][:, f, p:p + 1],
                                        offs[:, side, f, p:p + 1], ALU.mult, ALU.add))
                def add_out(f):
                    dve.wait_ge(f_ps, NB * (f + 1))
                    V.tensor_tensor(x[:, :, :], x[:, :, :], ps[:, 4:8, :].rearrange("p b (t d) -> p (b t) d", t=TB),
                                    ALU.add).then_inc(x_summed, 1)
                    dve.wait_ge(x_summed, f + 1)
                for f in range(FT):
                    if f:
                        dve.wait_ge(fused_ready, f)
                    for dst, side, op in ((cvx, 0, ALU.max), (ccv, 1, ALU.min)):
                        own_line(dst, side, f, PP - 2)
                        take(dst, op)
                        own_line(line, side, f, PP - 1)
                        din(V.tensor_tensor(dst, dst, line, op))
                        take(dst, op)
                        take(dst, op)
                    add_out(f)
                    dve.wait_ge(c_read, 2 * (f + 1) * NB)
                    din(V.scalar_tensor_tensor(ccv, ccv, sa[:, 1, f:f + 1], CL[f % 2], ALU.mult, ALU.subtract))
                    din(V.scalar_tensor_tensor(cvx, cvx, sa[:, 0, f:f + 1], ccv, ALU.mult, ALU.add))
                    V.tensor_tensor(acc[:, f, :], cvx, G[f % 2], ALU.mult).then_inc(fused_ready, 1)
                for b in range(NB):
                    dve.wait_ge(f_ps, NB * FT + b + 1)
                    V.tensor_tensor(x[:, b * TB:(b + 1) * TB, :], x[:, b * TB:(b + 1) * TB, :],
                                    ps[:, 4 + b, :].rearrange("p (t d) -> p t d", t=TB), ALU.add).then_inc(x_ready, 1)
            if LAYERS > 7:
                tropical()


def layout(i):
    def tiles(w):
        return w.reshape(-1, P, w.shape[-1]).transpose(1, 0, 2)

    def cols(v):
        return v.reshape(-1, P).T
    win = i["L0_ffn_W_in"]
    order = np.concatenate([win[:, 0:DIN], win[:, 2 * DIN + 2 * DST:], win[:, DIN:2 * DIN + 2 * DST]], axis=1)
    return {
        "x": i["x"], "adjT": i["adj"].T,
        "W0T": i["L0_gnn_W"].T, "b0": i["L0_gnn_b"],
        "win": order, "convw": tiles(i["L0_ffn_conv_w"]), "convb": cols(i["L0_ffn_conv_b"]),
        "dtb": i["L0_ffn_dt_bias"], "alog": i["L0_ffn_A_log"], "Dh": i["L0_ffn_D"], "nw": cols(i["L0_ffn_norm_w"]),
        "woutT": i["L0_ffn_W_out"].T, "wlin": i["L0_ffn_W_lin"], "blin": i["L0_ffn_b_lin"],
        "W1n": i["L1_gnn_W1"], "W2n": i["L1_gnn_W2"], "W3T": i["L1_gnn_W3"].T,
        "b12": np.stack([i["L1_gnn_b1"], i["L1_gnn_b2"]], axis=1), "b3": i["L1_gnn_b3"], "a": i["L1_gnn_a"],
        "wg": i["L1_ffn_Wg"], "bg": i["L1_ffn_bg"],
        "w1e": i["L1_ffn_W1"].transpose(1, 0, 2).reshape(D, E1 * H1), "b1c": cols(i["L1_ffn_b1"].reshape(-1)),
        "w2e": tiles(i["L1_ffn_W2"].reshape(E1 * H1, D)), "b2r": i["L1_ffn_b2"],
        "wqT": i["L2_gnn_Wq"].T, "wkT": i["L2_gnn_Wk"].T,
        "wr": i["L2_ffn_wr"], "br": i["L2_ffn_br"], "w1m": i["L2_ffn_w1"], "b1m": cols(i["L2_ffn_b1"]),
        "w2m": tiles(i["L2_ffn_w2"]), "b2m": i["L2_ffn_b2"],
        "W3W": i["L3_gnn_W"], "W3WT": i["L3_gnn_W"].T, "a3": i["L3_gnn_a"].reshape(2, D).T,
        "Wt": tiles(i["L3_ffn_Wt"]), "bt": cols(i["L3_ffn_bt"]),
        "slx": tiles(i["L3_ffn_sl_cvx"]), "ofx": tiles(i["L3_ffn_of_cvx"]),
        "slc": tiles(i["L3_ffn_sl_ccv"]), "ofc": tiles(i["L3_ffn_of_ccv"]),
        "alpha": cols(i["L3_ffn_alpha"]), "Wc": i["L3_ffn_Wc"], "bc": cols(i["L3_ffn_bc"]),
        "Wg": i["L3_ffn_Wg"], "bgt": cols(i["L3_ffn_bg"]), "Wd": tiles(i["L3_ffn_Wd"]), "bd": i["L3_ffn_bd"],
    }


def kernel(**inputs):
    import concourse.bacc as bacc
    from concourse.bass_utils import run_bass_kernel_spmd

    nc = bacc.Bacc("TRN2", target_bir_lowering=False, num_devices=1)
    arrays, aps = {}, {}
    for name, a in layout({k: np.asarray(v) for k, v in inputs.items()}).items():
        a = np.ascontiguousarray(a)
        arrays[f"in_{name}"] = a
        aps[name] = nc.dram_tensor(f"in_{name}", a.shape, mybir.dt.from_np(a.dtype), kind="ExternalInput").ap()
    out = nc.dram_tensor("out_dram", (N, D), F32, kind="ExternalOutput").ap()
    dbg = nc.dram_tensor("dbg_dram", (8, N, D), F32, kind="ExternalOutput").ap() if DEBUG else None
    build(nc, aps, out, dbg)
    r = run_bass_kernel_spmd(nc, [arrays], core_ids=[0])
    return r.results[0]["out_dram"]
```

```python
import numpy as np
import concourse.bass as bass
from concourse import mybir
from contextlib import ExitStack

F32 = mybir.dt.float32
BF16 = mybir.dt.bfloat16
I32 = mybir.dt.int32
ALU = mybir.AluOpType
ACT = mybir.ActivationFunctionType
AX = mybir.AxisListType.X

P = 128
N = 2048
D = 128
T = N // P
BLK = 512
NB = N // BLK
TB = T // NB
EPS = 1e-5

DIN, DST, KC, NH, HD = 256, 64, 4, 4, 64
XB = DIN + DST
E1, H1 = 8, 256
HT1 = E1 * H1 // P
H2 = 512
KSEL = N // 2 - 1
FF, PP = 512, 8
FT = FF // P
NEG = -1e30
FILL = -3.0e38


def build(nc, ins, out):
    with ExitStack() as ctx:
        def sb(name, shape, dt=F32):
            return ctx.enter_context(nc.sbuf_tensor(name, shape, dt))

        def sem(name):
            return ctx.enter_context(nc.semaphore(name))

        ps = ctx.enter_context(nc.psum_tensor("ps", [P, 8, BLK], F32))
        ps_wide = ps[:, :, :].rearrange("p (b k) n -> p b (k n)", b=2)

        x = sb("x", [P, T, D])
        xn = sb("xn", [P, T, D])
        XT = sb("XT", [P, N])[:, :]
        mask = sb("mask", [P, T, N], BF16)
        ident = sb("ident", [P, P])
        ones = sb("ones", [P, P])
        upper = sb("upper", [P, P])
        negtri = sb("negtri", [P, P])
        tri = sb("tri", [P, P])
        selx = sb("selx", [96, 32], BF16)
        seld = sb("seld", [96, 16], BF16)
        sa = sb("sa", [P, 2, FT])
        offs = sb("offs", [P, 2, FT, PP])
        dslope = sb("dslope", [P, 2, FT, PP // 2]); doffs = sb("doffs", [P, 2, FT, PP // 2])
        rise = sb("rise", [P, D // 2, FT]); bias = sb("bias", [P, 2, FT])
        stats = sb("stats", [P, T, 6])
        mv = sb("mv", [P, T, 2])
        lnv = sb("lnv", [P, 4, T])
        deg = sb("deg", [P, T])

        W = {}

        def weight(name, shape):
            W[name] = sb("w_" + name, shape)
            return W[name]

        weight("W0T", [P, D]); weight("b0", [P, D])
        weight("win", [P, 2 * DIN + 2 * DST + NH])
        weight("convw", [P, 3, KC]); weight("convb", [P, 3])
        weight("dtb", [P, NH]); weight("alog", [P, NH]); weight("Dh", [P, NH])
        weight("nw", [P, 2]); weight("woutT", [P, DIN]); weight("wlin", [P, D]); weight("blin", [P, D])
        weight("W1n", [P, D]); weight("W2n", [P, D]); weight("WVu", [P, D + 4])
        weight("b12", [P, 2]); weight("A1", [P, 2]); weight("A2", [P, 2]); weight("vbias", [P, D + 4])
        weight("wg", [P, E1]); weight("bg", [P, E1]); weight("b1c", [P, HT1]); weight("b2r", [E1, D])
        weight("w1e", [P, E1 * H1])
        weight("wqT", [P, D]); weight("wkT", [P, D])
        weight("limit", [P, T]); weight("wr", [P, 1]); weight("br", [P, 1]); weight("w1m", [P, H2]); weight("b1m", [P, H2 // P])
        weight("w2m", [P, H2 // P, D]); weight("b2m", [P, D])
        weight("W3WT", [P, D]); weight("WVu3", [P, D + 2]); weight("a3", [P, 2])
        weight("Wt", [P, FT, D]); weight("bt", [P, FT])
        weight("slx", [P, FT, PP]); weight("ofx", [P, FT, PP]); weight("slc", [P, FT, PP]); weight("ofc", [P, FT, PP])
        weight("alpha", [P, FT]); weight("Wc", [P, FF]); weight("bc", [P, FT])
        weight("Wg", [P, FF]); weight("bgt", [P, FT]); weight("Wd", [P, FT, D]); weight("bd", [P, D])

        AR = 19300
        W2E_AT = AR - HT1 * D
        arena = sb("arena", [P, AR])
        at = [0]

        def lay(*shape, dt=F32, parts=P, fresh=False, to=None):
            if fresh:
                at[0] = 0
            if to is not None:
                at[0] = to
            size = int(np.prod(shape))
            words = size if dt == F32 else (size + 1) // 2
            v = arena[0:parts, at[0]:at[0] + words]
            at[0] += words
            assert at[0] <= AR, at[0]
            if dt != F32:
                v = v.bitcast(dt)[:, 0:size]
            names = "abcd"[:len(shape)]
            if len(shape) > 1:
                v = v.rearrange(f"p ({' '.join(names)}) -> p {' '.join(names)}", **dict(zip(names, shape)))
            return v

        x_loaded = sem("x_loaded"); w_loaded = sem("w_loaded"); w0_loaded = sem("w0_loaded")
        adj_in = [sem(f"adj_in{i}") for i in range(4)]
        mask_ready = sem("mask_ready"); consts = sem("consts")
        var_ready = sem("var_ready"); sqrt_ready = sem("sqrt_ready")
        xn_ready = sem("xn_ready"); xn_act = sem("xn_act"); shift_ready = sem("shift_ready"); xnT_ps = sem("xnT_ps"); xnT_ready = sem("xnT_ready")
        x_ready = sem("x_ready")
        dve_step = sem("dve_step"); act_step = sem("act_step"); pool_step = sem("pool_step")
        out_done = sem("out_done")

        steps = {"dve": 0, "act": 0, "pool": 0}

        def in_turn(eng, name, s, ins_):
            steps[name] += 1
            ins_.then_inc(s, 1)
            eng.wait_ge(s, steps[name])
        block = ctx.enter_context(nc.Block())

        def bcast(v, n):
            return v.unsqueeze(len(v.shape)).broadcast_to(list(v.shape) + [n])

        stage_adj = lay(4, N, fresh=True).bitcast(I32)
        V0 = lay(T, D)
        XP0 = lay(T, 3 * D + 2, dt=BF16)
        R0 = lay(8, D)
        rdeg = lay(T)
        v0_of_ps = ps[:, 4:8, :].rearrange("p b (t d) -> p (b t) d", t=TB)
        v0_rounded = sem("v0_rounded")
        v0_ps = sem("v0_ps"); v0_ready = sem("v0_ready"); xp0_ready = sem("xp0_ready")
        agg_ps = sem("agg_ps"); agg_read = sem("agg_read")

        xs = lay(T, XB, fresh=True)
        XS_END = at[0]
        sz = lay(T, DIN)
        lay(2 * (KC - 1))
        CT = lay(N, parts=DST)
        conv_bc = xn[:, :, :].rearrange("p t d -> p (t d)")
        BT = conv_bc[0:DST, :]
        xdt = lay(2, DIN); xdd = lay(2, DIN)
        ROWIN_AT = at[0]
        rowin = lay(2, NH, P)
        EM = lay(2, NH, P)
        Hst = lay(2, DIN, parts=DST)
        yscr = lay(2, DIN)
        small = lay(12, T * NH)
        wol = lay(2, D)
        Aneg = lay(NH)
        DI = lay(NH, P)
        MAMBA_END = at[0]
        raw = lay(2, KC - 1 + N, to=XS_END)
        conv_x = [lay(N, to=ROWIN_AT), lay(N, to=MAMBA_END)]
        conv = conv_x + [conv_bc]
        CONV_ORDER = (2, 0, 1)
        RZ = 5
        yT = lay(3, 2, P, to=0)
        wol_ps = sem("wol_ps"); wol_ready = sem("wol_ready");
        raw_ps = sem("raw_ps"); raw_read = sem("raw_read"); conv_done = sem("conv_done"); silu_done = sem("silu_done")
        ct_in = sem("ct_in"); xs_ps = sem("xs_ps"); xs_ready = sem("xs_ready"); z_ps = sem("z_ps"); z_read = sem("z_read")
        dt_ps = sem("dt_ps"); dt_read = sem("dt_read")
        softplus_act = sem("softplus_act"); softplus_arg = sem("softplus_arg")
        dA_ready = sem("dA_ready"); acum_ps = sem("acum_ps"); acum_ready = sem("acum_ready"); decay_ready = sem("decay_ready")
        alog_exp = sem("alog_exp"); DI_ready = sem("DI_ready")
        rowin_ready = sem("rowin_ready"); row_ps = sem("row_ps"); E_ready = sem("E_ready"); G_ps = sem("G_ps")
        M_ready = sem("M_ready"); xdt_ready = sem("xdt_ready"); y_ps = sem("y_ps"); y_done = sem("y_done")
        h_ready = sem("h_ready"); s_ps = sem("s_ps"); sq_done = sem("sq_done"); yrms_var = sem("yrms_var"); yrms_sqrt = sem("yrms_sqrt")
        yT_ps = sem("yT_ps"); yT_ready = sem("yT_ready"); mo_ps = sem("mo_ps"); mo_read = sem("mo_read")

        SHARE = 4
        once = {s: sem(s) for s in ("u_ps", "u_ready", "smax_ready", "S_ready", "arg_ready", "ex_ready")}

        def attention_memory(tag, heads, dh, ring, bias_cols):
            a = {}
            w1 = dh + 1
            a["heads"], a["dh"], a["w1"], a["ring"] = heads, dh, w1, ring
            a["VS"] = lay(T, D + bias_cols, fresh=True)
            a["Fv"] = lay(T, 2, w1)
            a["XP"] = [lay(T, 2, 3, w1, dt=BF16) for _ in range(heads)]
            a["row"] = [lay(N) for _ in range(heads)]
            a["M1"] = lay(ring, BLK, dt=BF16)
            a["M2"] = xn[:, :, :].rearrange("p t d -> p (t d)").bitcast(BF16)[:, 0:ring * BLK].rearrange("p (r n) -> p r n", r=ring)
            a["R"] = lay(4, 2, w1)
            a["num"] = lay(4, w1)
            a["rd"] = lay(4)
            a["arg"] = lay(4, heads, T)
            a["ex"] = lay(4, heads, T)
            a["thr"] = lay(heads, T)
            a["smax"] = lay(heads)
            a["S"] = lay(heads)
            a["tt"] = lay(heads, T)
            a["cc"] = lay(heads, T)
            a["end"] = at[0]
            a["banks"] = 1 if 6 * w1 <= BLK else 2
            a["sets"] = 8 // (4 * a["banks"])
            a["turn"] = 1 if tag == "g1" else 2
            a.update(once)
            for s in ("v_ps", "v_ready", "row_ps", "row_ready", "xp_ready", "m1_ready", "m2_pool", "m2_dve", "m_used", "acc_read"):
                a[s] = sem(f"{tag}_{s}")
            return a

        A1 = attention_memory("g1", 2, 64, 6, 4)
        assert A1["end"] <= W2E_AT, (A1["end"], W2E_AT)
        w2e = lay(HT1, D, to=W2E_AT)
        w2e_loaded = sem("w2e_loaded")
        A3 = attention_memory("g3", 1, 128, 8, 2)
        elu_m = lay(T, D, to=0)
        h3 = lay(T, D, to=T * (D + 2))
        elu_ready = sem("elu_ready"); elu_exp = sem("elu_exp")

        hT1 = lay(4, 2, BLK, fresh=True)
        gates = lay(T, E1 + 6)
        top8 = lay(T, 8)
        marked = lay(T, E1 + 6)
        emask = lay(T, E1)
        emT = lay(N, parts=E1)
        assert at[0] <= W2E_AT
        g_ps = sem("g_ps"); emask_ready = sem("emask_ready"); emT_ps = sem("emT_ps"); emT_ready = sem("emT_ready")
        h1_ps = sem("h1_ps"); h1_ready = sem("h1_ready"); o1_ps = sem("o1_ps"); o1_read = sem("o1_read")

        RE = 6
        Kt = lay(T, D, fresh=True)
        KnT = lay(N); QT = lay(N)
        Er = lay(RE, BLK)
        xn1 = lay(T, D + 1)
        qs = lay(8, T)
        sqj = lay(D)
        ab = lay(4, T)
        kq_ps = sem("kq_ps"); kq_read = sem("kq_read"); QT_ps = sem("QT_ps"); QT_ready = sem("QT_ready")
        norm_sq = sem("norm_sq"); norm_sqrt = sem("norm_sqrt"); kn_ready = sem("kn_ready")
        KnT_ps = sem("KnT_ps"); KnT_ready = sem("KnT_ready"); xn1_ready = sem("xn1_ready")
        sc_ps = sem("sc_ps"); sc_exp = sem("sc_exp"); p_ready = sem("p_ready"); p_used = sem("p_used")
        a2_read = sem("a2_read")

        wcol = lay(T, fresh=True)
        wrow = lay(N)
        RC = 4
        cmp = lay(RC, N, dt=BF16)
        onesb = lay(2, dt=BF16)
        y2 = lay(2, TB, D)
        own = lay(T, P)
        rank = lay(2, T)
        sw = lay(T)
        hT2 = lay(2, H2 // P, BLK)
        cmp_ready = sem("cmp_ready"); cmp_used = sem("cmp_used")
        wrow_ps = sem("wrow_ps"); wrow_ready = sem("wrow_ready")
        h2_ps = sem("h2_ps"); h2_ready = sem("h2_ready"); o2_ps = sem("o2_ps"); o2_read = sem("o2_read")

        GF = 32
        NG = D // GF
        xg = lay(NG, N, dt=BF16, parts=3 * GF, fresh=True)
        xp3 = lay(3, N, dt=BF16)
        res = lay(N)
        rise1 = lay(2, N)
        oddc = lay(2, N)
        rise3 = lay(2, BLK)
        line_a = [lay(N, to=0), lay(N), lay(N)]
        line_b = [lay(N), lay(N), lay(N)]
        cvx = lay(N); ccv = lay(N); line = lay(N)
        big = mask[:, :, :].rearrange("p t n -> p (t n)").bitcast(F32)
        acc = big[:, 0:FT * N].rearrange("p (f n) -> p f n", f=FT)
        rise_m = big[:, FT * N:FT * N + 3 * N // 2]
        rise0 = (res, big[:, FT * N + 3 * N:FT * N + 4 * N])
        CL, G = ([big[:, FT * N + (2 * k + g) * N:FT * N + (2 * k + g + 1) * N] for k in range(2)] for g in range(2))
        xp3_ready = sem("xp3_ready"); xg_in = sem("xg_in"); rise_table = sem("rise_table")
        bias_ready = sem("bias_ready"); fill_done = sem("fill_done"); xg_first = sem("xg_first")
        diff_ps = sem("diff_ps"); odd_ps = sem("odd_ps"); even_ps = sem("even_ps"); pair_ps = sem("pair_ps")
        odd_copied = sem("odd_copied"); rise_pe = sem("rise_pe"); rise_pool = sem("rise_pool"); sum_ready = sem("sum_ready")
        single_step = sem("single_step"); pair_step = sem("pair_step"); sum_step = sem("sum_step")
        lines_table = sem("lines_table"); line_ready = sem("line_ready")
        pair_line = sem("pair_line"); pair_used = sem("pair_used")
        c_ps = sem("c_ps"); c_read = sem("c_read"); fused_ready = sem("fused_ready"); f_ps = sem("f_ps")
        x_summed = sem("x_summed"); sa_ready = sem("sa_ready")

        ld = []

        def load(eng, dst, src):
            ld.append(1)
            eng.dma_start(dst, src).then_inc(w_loaded, 16)

        small_loads = [
            ("win", "win"), ("woutT", "woutT"), ("wlin", "wlin"), ("W1n", "W1n"), ("W2n", "W2n"),
            ("wg", "wg"), ("w1e", "w1e"), ("wqT", "wqT"), ("wkT", "wkT"), ("w1m", "w1m"), ("W3WT", "W3WT"),
            ("Wc", "Wc"), ("Wg", "Wg"), ("b2r", "b2r"), ("wr", "wr"), ("limit", "limit"), ("w2m", "w2m"), ("Wt", "Wt"), ("Wd", "Wd"),
            ("slx", "slx"), ("ofx", "ofx"), ("slc", "slc"), ("ofc", "ofc"), ("bt", "bt"), ("alpha", "alpha"),
            ("bc", "bc"), ("bgt", "bgt"), ("b1m", "b1m"), ("b1c", "b1c"), ("nw", "nw"), ("convb", "convb"),
            ("b12", "b12"), ("a3", "a3"), ("convw", "convw")]
        row_loads = ["dtb", "alog", "Dh", "blin", "bg", "br", "b2m", "bd"]
        N_W = len(small_loads) + len(row_loads) + 1 + 4 + 1 + 1

        @block.sync
        def _(sp):
            sp.dma_start(x[:, :, :], ins["x"].rearrange("(t p) d -> p t d", p=P)).then_inc(x_loaded, 16)
            sp.dma_start(W["W0T"][:], ins["W0T"]).then_inc(w0_loaded, 16)
            sp.dma_start(W["b0"][:], ins["b0"].partition_broadcast(P)).then_inc(w0_loaded, 16)
            for jt in range(4, T):
                sp.wait_ge(mask_ready, jt - 3)
                sp.dma_start(stage_adj[:, jt % 4, :], ins["adjT"][jt * P:(jt + 1) * P, :]).then_inc(adj_in[jt % 4], 16)
            for name, src in small_loads:
                load(sp, W[name][:], ins[src])
            for name in row_loads:
                load(sp, W[name][:], ins[name].partition_broadcast(P))
            load(sp, W["vbias"][:, 0:D], ins["b3"].partition_broadcast(P))
            load(sp, W["WVu"][:, 0:D], ins["W3T"])
            load(sp, W["WVu3"][:, 0:D], ins["W3W"])
            sp.wait_ge(consts, 1)
            for h in range(2):
                load(sp, W["A1"][64 * h:64 * h + 64, h:h + 1], ins["a"][h, 0:64].unsqueeze(1))
                load(sp, W["A2"][64 * h:64 * h + 64, h:h + 1], ins["a"][h, 64:128].unsqueeze(1))
            assert len(ld) == N_W, (len(ld), N_W)
            sp.wait_ge(silu_done, 1)
            sp.dma_start(CT, conv_bc[DST:2 * DST, :]).then_inc(ct_in, 16)
            sp.wait_ge(x_ready, 2)
            sp.dma_start(w2e, ins["w2e"]).then_inc(w2e_loaded, 16)
            sp.wait_ge(xp3_ready, 1)
            for g in range(NG):
                for k in range(3):
                    sp.dma_start(xg[k:3 * (GF - 1) + k + 1:3, g, :], xp3[g * GF:(g + 1) * GF, k, :]).then_inc(xg_in if g else xg_first, 16)
            for b in range(NB):
                sp.wait_ge(x_ready, 7 + b + 1)
                sp.dma_start(out[b * BLK:(b + 1) * BLK, :].rearrange("(t p) d -> p t d", p=P),
                             x[:, b * TB:(b + 1) * TB, :]).then_inc(out_done, 16)
            sp.wait_ge(out_done, 16 * NB)

        @block.gpsimd
        def _(pool):
            def pin(i):
                in_turn(pool, "pool", pool_step, i)
            pin(pool.memset(W["A1"][:], 0.0))
            pool.memset(W["A2"][:], 0.0).then_inc(consts, 1)
            pin(pool.memset(ident[:], 0.0))
            pin(pool.affine_select(out=ident[:], in_=ident[:], compare_op=ALU.not_equal, fill=1.0, base=0,
                                   pattern=[[-1, P]], channel_multiplier=1))
            pin(pool.memset(ones[:], 1.0))
            pin(pool.affine_select(out=upper[:], in_=ones[:], compare_op=ALU.is_ge, fill=0.0, base=0,
                                   pattern=[[1, P]], channel_multiplier=-1))
            pin(pool.affine_select(out=tri[:], in_=ones[:], compare_op=ALU.is_gt, fill=0.0, base=0,
                                   pattern=[[-1, P]], channel_multiplier=1))
            pin(pool.memset(negtri[:], 0.0))
            pin(pool.affine_select(out=negtri[:], in_=negtri[:], compare_op=ALU.is_ge, fill=NEG, base=0,
                                   pattern=[[-1, P]], channel_multiplier=1))
            pin(pool.memset(selx[:], 1.0))
            pin(pool.affine_select(out=selx[:], in_=selx[:], compare_op=ALU.is_ge, fill=0.0, base=0,
                                   pattern=[[-3, GF]], channel_multiplier=1))
            pin(pool.affine_select(out=selx[:], in_=selx[:], compare_op=ALU.is_ge, fill=0.0, base=2,
                                   pattern=[[3, GF]], channel_multiplier=-1))
            pool.tensor_tensor(seld[:], selx[:, 0:GF:2], selx[:, 1:GF:2], ALU.subtract).then_inc(consts, 1)

            pool.wait_ge(x_ready, 1)
            for k in range(2):
                i = pool.memset(raw[:, k, 0:KC - 1], 0.0)
            i.then_inc(consts, 1)
            pin(pool.memset(Hst[:, 0, :], 0.0))
            pool.wait_ge(decay_ready, 2)
            pool.wait_ge(xs_ps, T)

            def rowin_of(c):
                if c >= 2:
                    pool.wait_ge(row_ps, c - 1)
                pool.tensor_tensor(rowin[:, c % 2, :, :], negtri[:].unsqueeze(1).broadcast_to([P, NH, P]),
                                   bcast(small[:, 9, c * NH:(c + 1) * NH], P), ALU.add).then_inc(rowin_ready, 1)
            rowin_of(0)
            rowin_of(1)
            for c in range(T):
                if c >= 2:
                    pool.wait_ge(y_ps, c - 1)
                pool.wait_ge(xs_ready, c + 1)
                dtv = small[:, 0, c * NH:(c + 1) * NH]
                dcv = small[:, 6, c * NH:(c + 1) * NH]
                v = xdt[:, c % 2, :].rearrange("p (h q) -> p h q", h=NH)
                pin(pool.tensor_tensor(v, xs[:, c, 0:DIN].rearrange("p (h q) -> p h q", h=NH), bcast(dtv, HD), ALU.mult))
                pool.tensor_tensor(xdd[:, c % 2, :].rearrange("p (h q) -> p h q", h=NH), v, bcast(dcv, HD),
                                   ALU.mult).then_inc(xdt_ready, 1)
                if c + 2 < T:
                    rowin_of(c + 2)

            def attention(a):
                max_over_tokens(a)
                for n in range(a["heads"] * NB * T):
                    if n % SHARE < SHARE - 1:
                        b, jt, r = n // T % NB, n % T, n % a["ring"]
                        pool.wait_ge(a["m1_ready"], n + 1)
                        pool.tensor_tensor(a["M2"][:, r, :], mask[:, jt, b * BLK:(b + 1) * BLK], a["M1"][:, r, :],
                                           ALU.subtract).then_inc(a["m2_pool"], 1)

            def max_over_tokens(a):
                pool.wait_ge(a["smax_ready"], a["turn"])
                pool.partition_all_reduce(a["S"], a["smax"], P, bass.bass_isa.ReduceOp.max).then_inc(a["S_ready"], 1)
            attention(A1)
            attention(A3)

            def tropical():
                pool.wait_ge(x_ready, 7)
                for f in range(FT):
                    pool.memset(acc[:, f, :], FILL).then_inc(fill_done, 1)

                def pair(j, slot):
                    pool.wait_ge(rise_pool, j * 3 + 1)
                    pool.tensor_tensor(rise0[slot], rise0[slot], oddc[:, slot, :], ALU.add).then_inc(sum_ready, 1)
                    pool.wait_ge(rise_pool, j * 3 + 2)
                    pool.tensor_tensor(rise3[:, slot, :], rise3[:, slot, :], oddc[:, slot, 0:BLK], ALU.add).then_inc(sum_ready, 1)
                    pool.wait_ge(rise_pool, j * 3 + 3)
                    pool.tensor_tensor(rise1[:, slot, :], rise1[:, slot, :], oddc[:, slot, :], ALU.add).then_inc(sum_ready, 1)
                with pool.Fori(0, D // 4) as i:
                    for s in range(2):
                        pair(i * 2 + s, s)
                for n in range(6 * FT):
                    k = n % 3
                    pool.wait_ge(line_ready, 2 * n + 2)
                    pool.tensor_tensor(line_a[k], line_b[k], line_a[k],
                                       ALU.add if n % 6 < 3 else ALU.subtract).then_inc(pair_line, 1)
            tropical()

        @block.tensor
        def _(pe):
            mm, tr = pe.matmul, pe.transpose

            def norm_transposes(q):
                for t in range(T):
                    if t % 3 < 2:
                        pe.wait_ge(xn_ready, 11 * q + t - t // 3 + 1)
                    else:
                        pe.wait_ge(xn_act, 5 * q + t // 3 + 1)
                    i = tr(ps[:, t // 4, (t % 4) * P:(t % 4 + 1) * P], xn[:, t, :], ident[:])
                    if t % 4 == 3:
                        i.then_inc(xnT_ps, 1)

            def tok(t):
                return XT[:, t * P:(t + 1) * P]

            pe.wait_ge(consts, 2)
            norm_transposes(0)
            pe.wait_ge(w0_loaded, 32)
            for t in range(T):
                pe.wait_ge(xnT_ready, t // TB + 1)
                i = mm(ps[:, 4 + t // TB, t % TB * D:(t % TB + 1) * D], tok(t), W["W0T"][:], start=True, stop=True)
            i.then_inc(v0_ps, 1)
            pe.wait_ge(xp0_ready, 1)

            def gather(half, i, jt):
                m = mm(ps[:, i, 0:3 * D + 1], mask[:, jt, (half * 8 + i) * P:(half * 8 + i + 1) * P],
                       XP0[:, jt, 0:3 * D + 1], start=(jt == 0), stop=(jt == T - 1))
                if jt == T - 1:
                    m.then_inc(agg_ps, 1)
            for jt in range(T):
                pe.wait_ge(mask_ready, jt + 1)
                for i in range(8):
                    gather(0, i, jt)
            for i in range(8):
                pe.wait_ge(agg_read, i + 1)
                for jt in range(T):
                    gather(1, i, jt)

            def mamba():
                norm_transposes(1)
                pe.wait_ge(w_loaded, 16 * N_W)
                for k in range(2):
                    i = mm(ps[:, 4, k * P:(k + 1) * P], W["woutT"][:, k * P:(k + 1) * P], W["wlin"][:],
                           start=True, stop=True, skip_group_check=True)
                i.then_inc(wol_ps, 1)
                pe.wait_ge(xnT_ready, 2 * NB)
                for c in range(T):
                    i = mm(ps[:, 5, c * NH:(c + 1) * NH], tok(c), W["win"][:, DIN:DIN + NH],
                           start=True, stop=True, skip_group_check=True)
                i.then_inc(dt_ps, 1)
                for u, m in enumerate(CONV_ORDER):
                    if u == 1:
                        pe.wait_ge(wol_ready, 1)
                        pe.wait_ge(dt_read, 1)
                    for b in range(NB):
                        if u == 2:
                            pe.wait_ge(raw_read, b + 1)
                        mm(ps[:, 4 * (u % 2) + b, :], W["win"][:, DIN + NH + m * P:DIN + NH + (m + 1) * P],
                           XT[:, b * BLK:(b + 1) * BLK], start=True, stop=True).then_inc(raw_ps, 1)
                pe.wait_ge(dA_ready, 1)
                pe.wait_ge(raw_read, 3 * NB)
                dA = small[:, 1, :]
                mm(ps[:, 0, 0:T * NH], upper[:], dA, start=True, stop=True, skip_group_check=True)
                mm(ps[:, 0, T * NH:2 * T * NH], ones[:], dA, start=True, stop=True, skip_group_check=True).then_inc(acum_ps, 1)
                for c in range(T + RZ - 1):
                    if c < T:
                        if c >= RZ:
                            pe.wait_ge(z_read, c - RZ + 1)
                        mm(ps[:, 1 + c % RZ, 0:DIN], tok(c), W["win"][:, 0:DIN], start=True, stop=True).then_inc(z_ps, 1)
                    if c >= RZ - 1:
                        e = c - RZ + 1
                        pe.wait_ge(silu_done, 3)
                        if e >= 2:
                            pe.wait_ge(xs_ready, e - 1)
                        for k in range(2):
                            tr(ps[:, 6 + e % 2, k * P:(k + 1) * P], conv_x[k][:, e * P:(e + 1) * P], ident[:])
                        tr(ps[:, 6 + e % 2, DIN:XB], BT[:, e * P:(e + 1) * P], ident[0:DST, 0:DST]).then_inc(xs_ps, 1)
                pe.wait_ge(acum_ready, 1)
                pe.wait_ge(ct_in, 16)
                pe.wait_ge(DI_ready, 1)
                pe.wait_ge(z_read, T)
                pe.wait_ge(xs_ready, T)

                def rows(c):
                    pe.wait_ge(rowin_ready, c + 1)
                    if c >= 2:
                        pe.wait_ge(M_ready, c - 1)
                    for h in range(NH):
                        i = tr(ps[:, c % 2, h * P:(h + 1) * P], rowin[:, c % 2, h, :], ident[:])
                    i.then_inc(row_ps, 1)
                    mm(ps[:, 2 + c % 2, 0:P], BT[:, c * P:(c + 1) * P], CT[:, c * P:(c + 1) * P],
                       start=True, stop=True).then_inc(G_ps, 1)
                rows(0)
                for c in range(T):
                    if c + 1 < T:
                        rows(c + 1)
                    pe.wait_ge(xdt_ready, c + 1)
                    if c >= 2:
                        pe.wait_ge(h_ready, c - 1)
                    mm(ps[0:DST, 6 + c % 2, 0:DIN], xs[:, c, DIN:XB], xdd[:, c % 2, :], start=True, stop=True).then_inc(s_ps, 1)
                    pe.wait_ge(M_ready, c + 1)
                    if c >= 2:
                        pe.wait_ge(y_done, c - 1)
                    for h in range(NH):
                        mm(ps[:, 4 + c % 2, h * HD:(h + 1) * HD], EM[:, c % 2, h, :], xdt[:, c % 2, h * HD:(h + 1) * HD],
                           start=True, stop=False, skip_group_check=True)
                        mm(ps[:, 4 + c % 2, h * HD:(h + 1) * HD], DI[:, h, :], xs[:, c, h * HD:(h + 1) * HD],
                           start=False, stop=True, skip_group_check=True)
                    if c:
                        pe.wait_ge(h_ready, c)
                    mm(ps[:, 4 + c % 2, DIN:2 * DIN], CT[:, c * P:(c + 1) * P], Hst[:, c % 2, :],
                       start=True, stop=True, skip_group_check=True).then_inc(y_ps, 1)
                pe.wait_ge(y_done, T)
                for c in range(T + 2):
                    if c < T:
                        if c >= 3:
                            pe.wait_ge(yT_ready, c - 2)
                        for k in range(2):
                            i = tr(ps[:, (0, 1, 4)[c % 3], k * P:(k + 1) * P], sz[:, c, k * P:(k + 1) * P], ident[:])
                        i.then_inc(yT_ps, 1)
                    if c >= 2:
                        e = c - 2
                        pe.wait_ge(yT_ready, e + 1)
                        if e >= 2:
                            pe.wait_ge(mo_read, e - 1)
                        for k in range(2):
                            i = mm(ps[:, 2 + e % 2, 0:D], yT[:, e % 3, k, :], wol[:, k, :], start=(k == 0), stop=(k == 1))
                        i.then_inc(mo_ps, 1)
            mamba()

            def attention(a, q, wv, nv):
                heads, w1, ring = a["heads"], a["w1"], a["ring"]
                pe.wait_ge(x_ready, q)
                if q == 2:
                    for k, (w, av) in enumerate((("W1n", "A1"), ("W2n", "A2"))):
                        mm(ps[:, 4, 2 * k:2 * k + 2], W[w][:], W[av][:], start=True, stop=True, skip_group_check=True)
                        i = mm(ps[:, 4, 4 + 2 * k:6 + 2 * k], W["b12"][:, k:k + 1].broadcast_to([P, P]), W[av][:],
                               start=True, stop=True, skip_group_check=True)
                else:
                    i = mm(ps[:, 4, 0:2], W["W3WT"][:], W["a3"][:], start=True, stop=True)
                i.then_inc(a["u_ps"], 1)
                norm_transposes(q)
                pe.wait_ge(xnT_ready, NB * (q + 1))
                pe.wait_ge(a["u_ready"], a["turn"])
                for t in range(T):
                    if t >= 4:
                        pe.wait_ge(a["v_ready"], t - 3)
                    mm(ps[:, 4 + t % 4, 0:nv], tok(t), wv[:], start=True, stop=True).then_inc(a["v_ps"], 1)
                pe.wait_ge(a["v_ready"], T)
                for h in range(heads):
                    if h:
                        pe.wait_ge(a["row_ready"], NB * h)
                    for t in range(T):
                        i = tr(ps[:, t // 4, (t % 4) * P:(t % 4 + 1) * P],
                               a["VS"][:, t, D + h:D + h + 1].broadcast_to([P, P]), ident[:])
                        if t % 4 == 3:
                            i.then_inc(a["row_ps"], 1)
                pe.wait_ge(a["row_ready"], NB * heads)
                n = 0
                for k in range(heads * NB):
                    h = k // NB
                    if k >= a["sets"]:
                        pe.wait_ge(a["acc_read"], k - a["sets"] + 1)
                    if k % NB == 0:
                        pe.wait_ge(a["xp_ready"], h + 1)
                    for jt in range(T):
                        if n % SHARE < SHARE - 1:
                            pe.wait_ge(a["m2_pool"], n - n // SHARE + 1)
                        else:
                            pe.wait_ge(a["m2_dve"], n // SHARE + 1)
                        for i in range(4):
                            for s, M in enumerate((a["M1"], a["M2"])):
                                bank = (k % a["sets"]) * 4 * a["banks"] + i * a["banks"] + (s if a["banks"] == 2 else 0)
                                col = s * 3 * w1 if a["banks"] == 1 else 0
                                m = mm(ps[:, bank, col:col + 3 * w1], M[:, n % ring, i * P:(i + 1) * P],
                                       a["XP"][h][:, jt, s, :, :].rearrange("p k c -> p (k c)"),
                                       start=(jt == 0 and (s == 0 or a["banks"] == 2)), stop=(jt == T - 1), skip_group_check=True)
                        m.then_inc(a["m_used"], 1)
                        n += 1
            attention(A1, 2, W["WVu"], D + 4)

            def experts():
                norm_transposes(3)
                pe.wait_ge(xnT_ready, NB * 4)
                for t in range(T):
                    i = mm(ps[:, 4, t * E1:(t + 1) * E1], tok(t), W["wg"][:], start=True, stop=True, skip_group_check=True)
                i.then_inc(g_ps, 1)
                units = [(b, e) for b in range(NB) for e in range(E1)]

                def up(u):
                    b, e = units[u]
                    for k in range(2):
                        n = 2 * u + k
                        if n >= 4:
                            pe.wait_ge(h1_ready, n - 3)
                        mm(ps[:, n % 4, :], W["w1e"][:, (2 * e + k) * P:(2 * e + k + 1) * P],
                           XT[:, b * BLK:(b + 1) * BLK], start=True, stop=True).then_inc(h1_ps, 1)

                def down(u):
                    b, e = units[u]
                    pe.wait_ge(h1_ready, 2 * u + 2)
                    if e == 0:
                        if b >= 2:
                            pe.wait_ge(o1_read, (b - 1) * (E1 + 1) - E1)
                        for i in range(4):
                            t = 4 * b + i
                            m = mm(ps[:, 6 + b % 2, i * D:(i + 1) * D], emT[:, t * P:(t + 1) * P], W["b2r"][:],
                                   start=True, stop=True, skip_group_check=True)
                        m.then_inc(o1_ps, 1)
                    if u >= 2:
                        pe.wait_ge(o1_read, (u - 2) + (u - 2) // E1 + 2)
                    for i in range(4):
                        for k in range(2):
                            m = mm(ps[:, 4 + u % 2, i * D:(i + 1) * D], hT1[:, u % 4, k, i * P:(i + 1) * P],
                                   w2e[:, 2 * e + k, :], start=(k == 0), stop=(k == 1), skip_group_check=True)
                    m.then_inc(o1_ps, 1)
                up(0)
                up(1)
                pe.wait_ge(emask_ready, 1)
                for t in range(T):
                    i = tr(ps[0:E1, 4 + t // 4, (t % 4) * P:(t % 4 + 1) * P], emask[:, t, :], ident[:])
                    if t % 4 == 3:
                        i.then_inc(emT_ps, 1)
                pe.wait_ge(emT_ready, NB)
                pe.wait_ge(w2e_loaded, 16)
                for u in range(len(units)):
                    if 1 < u + 1 < len(units):
                        up(u + 1)
                    down(u)
            experts()

            def cosine():
                norm_transposes(4)
                pe.wait_ge(xnT_ready, NB * 5)
                for t in range(T):
                    if t >= 4:
                        pe.wait_ge(kq_read, t - 3)
                    mm(ps[:, 4 + t % 4, 0:D], tok(t), W["wkT"][:], start=True, stop=True, skip_group_check=True)
                    mm(ps[:, 4 + t % 4, D:2 * D], tok(t), W["wqT"][:], start=True, stop=True,
                       skip_group_check=True).then_inc(kq_ps, 1)
                for b in range(NB):
                    mm(ps[:, b, :], W["wqT"][:], XT[:, b * BLK:(b + 1) * BLK], start=True, stop=True).then_inc(QT_ps, 1)
                pe.wait_ge(QT_ready, NB)
                for t in range(T):
                    pe.wait_ge(kn_ready, 1)
                    i = tr(ps[:, t // 4, (t % 4) * P:(t % 4 + 1) * P], Kt[:, t, :], ident[:])
                    if t % 4 == 3:
                        i.then_inc(KnT_ps, 1)
                pe.wait_ge(KnT_ready, NB)
                pe.wait_ge(xn1_ready, 1)
                pe.wait_ge(kq_read, T)
                items = [(b, jt) for b in range(NB) for jt in range(T)]

                def score(n):
                    b, jt = items[n]
                    if n >= 2:
                        pe.wait_ge(sc_exp, n - 1)
                    mm(ps[:, n % 2, :], QT[:, jt * P:(jt + 1) * P], KnT[:, b * BLK:(b + 1) * BLK],
                       start=True, stop=True).then_inc(sc_ps, 1)

                def apply(n):
                    b, jt = items[n]
                    pe.wait_ge(p_ready, n + 1)
                    if jt == 0 and b:
                        pe.wait_ge(a2_read, b)
                    for i in range(4):
                        m = mm(ps[:, 2 + i, 0:D + 1], Er[:, n % RE, i * P:(i + 1) * P], xn1[:, jt, :],
                               start=(jt == 0), stop=(jt == T - 1))
                    m.then_inc(p_used, 1)
                score(0)
                score(1)
                for n in range(len(items)):
                    if n + 2 < len(items):
                        score(n + 2)
                    apply(n)
            cosine()

            def depths():
                norm_transposes(5)
                HTILES = H2 // P
                for b in range(NB):
                    pe.wait_ge(xnT_ready, NB * 5 + b + 1)
                    mm(ps[:, 4 + b, :], W["wr"][:].broadcast_to([P, P]), XT[:, b * BLK:(b + 1) * BLK],
                       start=True, stop=True).then_inc(wrow_ps, 1)

                def up(b):
                    for k in range(HTILES):
                        n = b * HTILES + k
                        if n >= 3:
                            pe.wait_ge(h2_ready, n - 2)
                        mm(ps[:, n % 3, :], W["w1m"][:, k * P:(k + 1) * P], XT[:, b * BLK:(b + 1) * BLK],
                           start=True, stop=True).then_inc(h2_ps, 1)

                def down(b):
                    pe.wait_ge(h2_ready, (b + 1) * HTILES)
                    pe.wait_ge(wrow_ready, b + 1)
                    for i in range(4):
                        for k in range(HTILES):
                            m = mm(ps[:, 4 + b, i * D:(i + 1) * D], hT2[:, b % 2, k, i * P:(i + 1) * P], W["w2m"][:, k, :],
                                   start=(k == 0), stop=(k == HTILES - 1), skip_group_check=True)
                    m.then_inc(o2_ps, 1)
                pieces = [(up, 0), (up, 1), (down, 0), (up, 2), (down, 1), (up, 3), (down, 2), (down, 3)]
                for t in range(T):
                    if t % 2 == 0:
                        do, b = pieces[t // 2]
                        do(b)
                    pe.wait_ge(cmp_ready, t + 1)
                    for j in range(t + 1):
                        m = mm(ps[:, 3, j:j + 1], cmp[:, t % RC, j * P:(j + 1) * P], onesb[:, 0:1],
                               start=(t == 0), stop=(t == T - 1), skip_group_check=True)
                    m.then_inc(cmp_used, 1)
            depths()
            attention(A3, 6, W["WVu3"], D + 2)

            def tropical():
                norm_transposes(7)

                def spread(bank, sel, g, half, stop=True, blocks=(0, 1)):
                    for b in blocks:
                        c = half * 2 + b
                        m = mm(ps[:, bank + b, :], sel.broadcast_to([3 * GF, P]), xg[:, g, c * BLK:(c + 1) * BLK],
                               start=True, stop=stop)
                    return m

                def add(bank, src):
                    for b in range(2):
                        m = mm(ps[:, bank + b, :], ident[:], src[:, b * BLK:(b + 1) * BLK], start=False, stop=True)
                    return m

                def pair(j, i, g, first=False):
                    even, odd, diff = selx[:, bass.ds(i * 2, 1)], selx[:, bass.ds(i * 2 + 1, 1)], seld[:, bass.ds(i, 1)]
                    if not first:
                        pe.wait_ge(pair_step, j * 3 - 1)
                    spread(4, odd, g, 0).then_inc(odd_ps, 1)
                    if not first:
                        pe.wait_ge(pair_step, j * 3)
                    spread(6, odd, g, 1).then_inc(odd_ps, 1)
                    if not first:
                        pe.wait_ge(rise_pool, j * 3)
                    spread(0, diff, g, 0).then_inc(diff_ps, 1)
                    spread(2, diff, g, 1).then_inc(diff_ps, 1)
                    pe.wait_ge(odd_copied, j * 2 + 1)
                    spread(4, even, g, 0, blocks=(1,)).then_inc(even_ps, 1)
                    pe.wait_ge(odd_copied, j * 2 + 2)
                    spread(6, odd, g, 0, stop=False)
                    pe.wait_ge(rise_pe, j * 3 + 1)
                    add(6, rise_m[:, 0:N // 2]).then_inc(pair_ps, 1)
                    pe.wait_ge(single_step, j * 2 + 1)
                    spread(4, odd, g, 1, stop=False)
                    pe.wait_ge(rise_pe, j * 3 + 2)
                    add(4, rise_m[:, N // 2:N]).then_inc(pair_ps, 1)
                    pe.wait_ge(pair_step, j * 3 + 1)
                    spread(6, odd, g, 1, stop=False)
                    pe.wait_ge(rise_pe, j * 3 + 3)
                    add(6, rise_m[:, N:]).then_inc(pair_ps, 1)
                for g in range(NG):
                    if g == 0:
                        pe.wait_ge(xg_first, 16 * 3)
                        pair(0, 0, 0, first=True)
                    elif g == 1:
                        pe.wait_ge(xg_in, 16 * 3 * (NG - 1))
                    with pe.Fori(int(g == 0), GF // 2) as i:
                        pair(i + g * (GF // 2), i, g)
                def classical(h):
                    f, g = divmod(h, 2)
                    w = ("Wc", "Wg")[(f + g) % 2]
                    for b in range(NB):
                        if h:
                            pe.wait_ge(c_read, (h - 1) * NB + b + 1)
                        mm(ps[:, b, :], W[w][:, f * P:(f + 1) * P], XT[:, b * BLK:(b + 1) * BLK],
                           start=True, stop=True).then_inc(c_ps, 1)

                def down(n, parts):
                    for b in range(NB):
                        if n:
                            pe.wait_ge(x_summed, n)
                        for t in range(b * TB, (b + 1) * TB):
                            for k, (a, w) in enumerate(parts):
                                m = mm(ps[:, 4 + b, (t % TB) * D:(t % TB + 1) * D], a[:, t * P:(t + 1) * P], W["Wd"][:, w, :],
                                       start=(k == 0), stop=(k == len(parts) - 1))
                        m.then_inc(f_ps, 1)
                pe.wait_ge(rise_pool, 3 * D // 2)
                classical(0)
                classical(1)
                pe.wait_ge(c_read, 2 * NB)
                pe.wait_ge(pair_step, 3 * D // 2)
                down(0, [(CL[0], 0)])
                ahead = 2
                for f in range(FT):
                    while ahead < min(2 * f + 6, 2 * FT):
                        classical(ahead)
                        ahead += 1
                    pe.wait_ge(fused_ready, f + 1)
                    if f + 1 < FT:
                        pe.wait_ge(c_read, 2 * (f + 2) * NB)
                        down(f + 1, [(acc[:, f, :], f), (CL[(f + 1) % 2], f + 1)])
                    else:
                        down(f + 1, [(acc[:, f, :], f)])
            tropical()

        @block.scalar
        def _(act):
            A = act.activation

            def ain(i):
                in_turn(act, "act", act_step, i)

            for jt in range(4):
                act.dma_start(stage_adj[:, jt, :], ins["adjT"][jt * P:(jt + 1) * P, :]).then_inc(adj_in[jt], 16)

            def norm(q):
                act.wait_ge(var_ready, q + 1)
                A(lnv[:, 1, :], lnv[:, 0, :], ACT.Sqrt).then_inc(sqrt_ready, 1)
                act.wait_ge(shift_ready, q + 1)
                for t in range(2, T, 3):
                    A(xn[:, t, :], x[:, t, :], ACT.Identity, bias=lnv[:, 3, t:t + 1], scale=lnv[:, 2, t:t + 1]).then_inc(xn_act, 1)
                for b in range(NB):
                    act.wait_ge(xnT_ps, NB * q + b + 1)
                    A(XT[:, b * BLK:(b + 1) * BLK], ps[:, b, :], ACT.Copy).then_inc(xnT_ready, 1)
            norm(0)
            act.wait_ge(v0_ps, 1)
            A(XP0[:, :, 0:D], v0_of_ps, ACT.Copy).then_inc(v0_rounded, 1)
            act.wait_ge(v0_ready, 1)
            A(XP0[:, :, D:2 * D], V0, ACT.Copy).then_inc(v0_rounded, 1)

            def mamba():
                norm(1)
                act.wait_ge(wol_ps, 1)
                for k in range(2):
                    i = A(wol[:, k, :], ps[:, 4, k * P:(k + 1) * P], ACT.Copy, scale=W["nw"][:, k:k + 1])
                i.then_inc(wol_ready, 1)
                def conv_input(u):
                    m = CONV_ORDER[u]
                    if u == 2:
                        act.wait_ge(conv_done, 1)
                    for b in range(NB):
                        act.wait_ge(raw_ps, u * NB + b + 1)
                        A(raw[:, u % 2, KC - 1 + b * BLK:KC - 1 + (b + 1) * BLK], ps[:, 4 * (u % 2) + b, :], ACT.Copy)
                        A(conv[m][:, b * BLK:(b + 1) * BLK], ps[:, 4 * (u % 2) + b, :], ACT.Identity,
                          bias=W["convb"][:, m:m + 1], scale=W["convw"][:, m, KC - 1:KC]).then_inc(raw_read, 1)
                conv_input(0)
                conv_input(1)
                A(Aneg, W["alog"][:], ACT.Exp).then_inc(alog_exp, 1)
                act.wait_ge(softplus_arg, 1)
                A(small[:, 3, :], small[:, 2, :], ACT.Exp).then_inc(softplus_act, 1)
                act.wait_ge(softplus_arg, 2)
                A(small[:, 5, :], small[:, 4, :], ACT.Ln).then_inc(softplus_act, 1)
                conv_input(2)
                for u, m in enumerate(CONV_ORDER):
                    act.wait_ge(conv_done, u + 1)
                    A(conv[m], conv[m], ACT.Silu).then_inc(silu_done, 1)
                for c in range(T):
                    act.wait_ge(z_ps, c + 1)
                    A(sz[:, c, :], ps[:, 1 + c % RZ, 0:DIN], ACT.Silu).then_inc(z_read, 1)
                act.wait_ge(acum_ready, 1)
                A(small[:, 6:8, :], small[:, 6:8, :], ACT.Exp).then_inc(decay_ready, 1)
                A(small[:, 8, :], small[:, 9, :], ACT.Exp).then_inc(decay_ready, 1)

                def square(c):
                    act.wait_ge(y_done, c + 1)
                    ain(A(yscr[:, 0, :], sz[:, c, :], ACT.Square, accum_out=small[:, 11, c:c + 1]))
                for c in range(T):
                    act.wait_ge(row_ps, c + 1)
                    if c >= 2:
                        act.wait_ge(y_ps, c - 1)
                    for h in range(NH):
                        i = A(EM[:, c % 2, h, :], ps[:, c % 2, h * P:(h + 1) * P], ACT.Exp,
                              bias=small[:, 10, c * NH + h:c * NH + h + 1])
                    i.then_inc(E_ready, 1)
                    if c >= 2:
                        square(c - 2)
                square(T - 2)
                square(T - 1)
                A(small[:, 11, T:2 * T], small[:, 11, 0:T], ACT.Copy).then_inc(sq_done, 1)
                act.wait_ge(yrms_var, 1)
                A(small[:, 11, 2 * T:3 * T], small[:, 11, T:2 * T], ACT.Sqrt).then_inc(yrms_sqrt, 1)
                for c in range(T):
                    act.wait_ge(yT_ps, c + 1)
                    if c >= 3:
                        act.wait_ge(mo_ps, c - 2)
                    A(yT[:, c % 3, :, :].rearrange("p k n -> p (k n)"), ps[:, (0, 1, 4)[c % 3], 0:2 * P], ACT.Copy).then_inc(yT_ready, 1)
            mamba()

            def attention(a, q):
                norm(q)
                act.wait_ge(a["arg_ready"], a["turn"])
                A(a["ex"].rearrange("p k h t -> p (k h t)"), a["arg"].rearrange("p k h t -> p (k h t)"), ACT.Exp).then_inc(a["ex_ready"], 1)
                for h in range(a["heads"]):
                    for b in range(NB):
                        act.wait_ge(a["row_ps"], h * NB + b + 1)
                        A(a["row"][h][:, b * BLK:(b + 1) * BLK], ps[:, b, :], ACT.Copy).then_inc(a["row_ready"], 1)
            attention(A1, 2)

            def experts():
                norm(3)
                for u in range(NB * E1):
                    e = u % E1
                    if u == 2:
                        for b in range(NB):
                            act.wait_ge(emT_ps, b + 1)
                            A(emT[:, b * BLK:(b + 1) * BLK], ps[0:E1, 4 + b, :], ACT.Copy).then_inc(emT_ready, 1)
                    if u >= 4:
                        act.wait_ge(o1_ps, (u - 4) + (u - 4) // E1 + 2)
                    for k in range(2):
                        n = 2 * u + k
                        act.wait_ge(h1_ps, n + 1)
                        A(hT1[:, u % 4, k, :], ps[:, n % 4, :], ACT.Gelu, bias=W["b1c"][:, 2 * e + k:2 * e + k + 1]).then_inc(h1_ready, 1)
            experts()

            def cosine():
                norm(4)
                for b in range(NB):
                    act.wait_ge(QT_ps, b + 1)
                    A(QT[:, b * BLK:(b + 1) * BLK], ps[:, b, :], ACT.Copy).then_inc(QT_ready, 1)
                act.wait_ge(norm_sq, 1)
                A(qs[:, 2:4, :], qs[:, 0:2, :], ACT.Sqrt).then_inc(norm_sqrt, 1)
                for b in range(NB):
                    act.wait_ge(KnT_ps, b + 1)
                    A(KnT[:, b * BLK:(b + 1) * BLK], ps[:, b, :], ACT.Copy).then_inc(KnT_ready, 1)
                for n in range(NB * T):
                    jt = n % T
                    act.wait_ge(sc_ps, n + 1)
                    if n >= RE:
                        act.wait_ge(p_used, n - RE + 1)
                    A(Er[:, n % RE, :], ps[:, n % 2, :], ACT.Exp, scale=qs[:, 5, jt:jt + 1]).then_inc(sc_exp, 1)
            cosine()

            def depths():
                norm(5)
                for b in range(NB):
                    act.wait_ge(wrow_ps, b + 1)
                    A(wrow[:, b * BLK:(b + 1) * BLK], ps[:, 4 + b, :], ACT.Identity, bias=W["br"][:]).then_inc(wrow_ready, 1)
                for n in range(NB * (H2 // P)):
                    b, k = divmod(n, H2 // P)
                    act.wait_ge(h2_ps, n + 1)
                    if b >= 2 and k == 0:
                        act.wait_ge(o2_ps, b - 1)
                    A(hT2[:, b % 2, k, :], ps[:, n % 3, :], ACT.Gelu_apprx_tanh, bias=W["b1m"][:, k:k + 1]).then_inc(h2_ready, 1)
            depths()
            attention(A3, 6)
            act.wait_ge(elu_ready, 1)
            A(elu_m, elu_m, ACT.Exp).then_inc(elu_exp, 1)

            def tropical():
                norm(7)
                A(sa[:, 0, :], W["alpha"][:], ACT.Sigmoid).then_inc(sa_ready, 1)

                act.wait_ge(rise_table, 1)

                def pair(j, slot, before=2):
                    A(bias[:, slot, :], rise[:, bass.ds(j, 1), :].rearrange("p o k -> p (o k)"), ACT.Copy).then_inc(bias_ready, 1)
                    if before > 1:
                        act.wait_ge(sum_ready, j * 3 - 3)
                    for n in range(2):
                        h = slice(n * N // 2, (n + 1) * N // 2)
                        act.wait_ge(odd_ps, j * 2 + (n + 1))
                        A(oddc[:, slot, h], ps_wide[:, 1, h], ACT.Copy).then_inc(odd_copied, 1)
                    act.wait_ge(bias_ready, j + 1)
                    for n, (f, half) in enumerate(((2, 0), (2, 1), (3, 1))):
                        if n < 2:
                            act.wait_ge(diff_ps, j * 2 + (n + 1))
                        A(rise_m[:, n * N // 2:(n + 1) * N // 2], ps_wide[:, 0, half * N // 2:(half + 1) * N // 2], ACT.Relu,
                          bias=bias[:, slot, f:f + 1]).then_inc(rise_pe, 1)
                    if before > 1:
                        act.wait_ge(sum_step, j * 3 - 3)
                    A(rise0[slot], ps_wide[:, 0, :], ACT.Relu, bias=bias[:, slot, 0:1]).then_inc(rise_pool, 1)
                    A(rise3[:, slot, :], ps[:, 0, :], ACT.Relu, bias=bias[:, slot, 3:4]).then_inc(rise_pool, 1)
                    A(rise1[:, slot, :], ps_wide[:, 0, :], ACT.Relu, bias=bias[:, slot, 1:2]).then_inc(rise_pool, 1)
                pair(0, 0, before=0)
                pair(1, 1, before=1)
                with act.Fori(1, D // 4) as i:
                    for s in range(2):
                        pair(i * 2 + s, s)

                def classical(h):
                    f, g = divmod(h, 2)
                    dst, fn, b0 = ((CL, ACT.Gelu, "bc"), (G, ACT.Sigmoid, "bgt"))[(f + g) % 2]
                    for b in range(NB):
                        act.wait_ge(c_ps, h * NB + b + 1)
                        A(dst[f % 2][:, b * BLK:(b + 1) * BLK], ps[:, b, :], fn, bias=W[b0][:, f:f + 1]).then_inc(c_read, 1)
                classical(0)
                classical(1)
                act.wait_ge(lines_table, 4)
                act.wait_ge(sum_step, 3 * D // 2)
                act.wait_ge(pair_step, 3 * D // 2)
                act.wait_ge(single_step, D)
                for f in range(FT):
                    for k in range(6):
                        n, side, q = 6 * f + k, k // 3, k % 3
                        of = (2 * q + 1, 2 * q)[side]
                        if k == 3 and f + 1 < FT:
                            if f:
                                act.wait_ge(fused_ready, f)
                                act.wait_ge(f_ps, NB * f)
                            classical(2 * f + 2)
                        if k == 4 and f + 1 < FT:
                            classical(2 * f + 3)
                        if n >= 3:
                            act.wait_ge(pair_used, n - 2)
                        A(line_a[n % 3], acc[:, f, :], ACT.Relu, bias=doffs[:, side, f, q:q + 1],
                          scale=dslope[:, side, f, q:q + 1]).then_inc(line_ready, 1)
                        A(line_b[n % 3], acc[:, f, :], ACT.Identity, bias=offs[:, side, f, of:of + 1],
                          scale=W[("slx", "slc")[side]][:, f, of:of + 1]).then_inc(line_ready, 1)
            tropical()

        @block.vector
        def _(dve):
            V = nc.vector

            def din(i):
                in_turn(dve, "dve", dve_step, i)

            def newton_rsqrt(v, s, r, tmp):
                din(V.reciprocal(r, s))
                din(V.tensor_tensor(tmp, v, r, ALU.mult))
                din(V.tensor_tensor(tmp, tmp, s, ALU.add))
                din(V.tensor_scalar(tmp, tmp, 0.5, None, ALU.mult))
                din(V.reciprocal(r, tmp))

            counted = set()

            def moments(tiles):
                for t in tiles:
                    i = V.bn_stats(stats[:, t, :], x[:, t, :])
                    counted.add(t)
                return i

            def norm(q):
                din(moments([t for t in range(T) if t not in counted]))
                counted.clear()
                for t in range(T):
                    i = V.bn_aggr(mv[:, t, :], stats[:, t, :])
                din(i)
                V.tensor_scalar(lnv[:, 0, :], mv[:, :, 1], EPS, None, ALU.add).then_inc(var_ready, 1)
                dve.wait_ge(sqrt_ready, q + 1)
                newton_rsqrt(lnv[:, 0, :], lnv[:, 1, :], lnv[:, 2, :], lnv[:, 3, :])
                V.scalar_tensor_tensor(lnv[:, 3, :], mv[:, :, 0], -1.0, lnv[:, 2, :], ALU.mult, ALU.mult).then_inc(shift_ready, 1)
                for t in range(T):
                    if t % 3 < 2:
                        V.tensor_scalar(xn[:, t, :], x[:, t, :], mv[:, t, 0:1], lnv[:, 2, t:t + 1], ALU.subtract, ALU.mult).then_inc(xn_ready, 1)

            dve.wait_ge(x_loaded, 16)
            norm(0)

            def cast(jt):
                dve.wait_ge(adj_in[jt % 4], 16 * (jt // 4 + 1))
                V.tensor_scalar(mask[:, jt, :], stage_adj[:, jt % 4, :], 1.0, None, ALU.is_equal).then_inc(mask_ready, 1)
            for jt in range(4):
                cast(jt)
            dve.wait_ge(v0_rounded, 1)
            V.tensor_tensor(V0, v0_of_ps, XP0[:, :, 0:D], ALU.subtract).then_inc(v0_ready, 1)
            cast(4)
            cast(5)
            dve.wait_ge(v0_rounded, 2)
            din(V.tensor_tensor(XP0[:, :, 2 * D:3 * D], V0, XP0[:, :, D:2 * D], ALU.subtract))
            V.memset(XP0[:, :, 3 * D:3 * D + 2], 1.0).then_inc(xp0_ready, 1)
            for jt in range(6, T):
                cast(jt)
                if jt == 8:
                    dve.wait_ge(w0_loaded, 32)
                    din(V.tensor_tensor(x[:, :, :], x[:, :, :], W["b0"][:].unsqueeze(1).broadcast_to([P, T, D]), ALU.add))
            for t in range(T):
                if t:
                    dve.wait_ge(agg_read, t)
                    moments([t - 1])
                dve.wait_ge(agg_ps, t + 1)
                pv = ps[:, t % 8, 0:3 * D].rearrange("p (k d) -> p d k", k=3)
                V.tensor_copy(deg[:, t:t + 1], ps[:, t % 8, 3 * D:3 * D + 1])
                din(V.tensor_reduce(R0[:, t % 8, :], pv, AX, ALU.add))
                din(V.reciprocal(rdeg[:, t:t + 1], deg[:, t:t + 1]))
                i = V.scalar_tensor_tensor(x[:, t, :], R0[:, t % 8, :], rdeg[:, t:t + 1], x[:, t, :], ALU.mult, ALU.add)
                i.then_inc(agg_read if t < T - 1 else x_ready, 1)
            dve.wait_ge(x_ready, 1)
            dve.wait_ge(w_loaded, 16 * N_W)

            def mamba():
                norm(1)
                for h in range(NH):
                    i = V.tensor_scalar(DI[:, h, :], ident[:], W["Dh"][:, h:h + 1], None, ALU.mult)
                i.then_inc(DI_ready, 1)
                v = [small[:, k, :] for k in range(12)]

                def convolve(u):
                    m = CONV_ORDER[u]
                    dve.wait_ge(raw_read, (u + 1) * NB)
                    for k in range(KC - 1):
                        i = V.scalar_tensor_tensor(conv[m], raw[:, u % 2, k:k + N], W["convw"][:, m, k:k + 1], conv[m],
                                                   ALU.mult, ALU.add)
                        if k < KC - 2:
                            din(i)
                    i.then_inc(conv_done, 1)

                def h4(u):
                    return u.rearrange("p (c h) -> p c h", h=NH)
                dve.wait_ge(dt_ps, 1)
                V.tensor_tensor(h4(v[0]), h4(ps[:, 5, 0:T * NH]), W["dtb"][:].unsqueeze(1).broadcast_to([P, T, NH]), ALU.add).then_inc(dt_read, 1)
                dve.wait_ge(dt_read, 1)
                din(V.tensor_scalar(v[1], v[0], -1.0, None, ALU.mult))
                V.tensor_tensor(v[2], v[0], v[1], ALU.min).then_inc(softplus_arg, 1)
                dve.wait_ge(consts, 3)
                convolve(0)
                dve.wait_ge(softplus_act, 1)
                V.tensor_scalar(v[4], v[3], 1.0, None, ALU.add).then_inc(softplus_arg, 1)
                dve.wait_ge(softplus_arg, 2)
                din(V.tensor_scalar(v[6], v[4], -1.0, None, ALU.add))
                din(V.tensor_tensor(v[3], v[3], v[6], ALU.subtract))
                din(V.reciprocal(v[7], v[4]))
                din(V.tensor_tensor(v[3], v[3], v[7], ALU.mult))
                convolve(1)
                dve.wait_ge(softplus_act, 2)
                din(V.tensor_tensor(v[5], v[5], v[3], ALU.add))
                din(V.scalar_tensor_tensor(v[0], v[0], 0.0, v[5], ALU.max, ALU.add))
                dve.wait_ge(alog_exp, 1)
                din(V.tensor_tensor(h4(v[1]), h4(v[0]), Aneg.unsqueeze(1).broadcast_to([P, T, NH]), ALU.mult))
                V.tensor_scalar(v[1], v[1], -1.0, None, ALU.mult).then_inc(dA_ready, 1)
                dve.wait_ge(dA_ready, 1)
                convolve(2)
                dve.wait_ge(acum_ps, 1)
                din(V.tensor_copy(v[9], ps[:, 0, 0:T * NH]))
                V.tensor_copy(v[7], ps[:, 0, T * NH:2 * T * NH])
                din(V.tensor_scalar(v[10], v[9], -1.0, None, ALU.mult))
                V.tensor_tensor(v[6], v[7], v[9], ALU.subtract).then_inc(acum_ready, 1)
                for c in range(T):
                    dve.wait_ge(xs_ps, c + 1)
                    V.tensor_copy(xs[:, c, :], ps[:, 6 + c % 2, 0:XB]).then_inc(xs_ready, 1)
                din(V.tensor_tensor(x[:, :, :], x[:, :, :], W["blin"][:].unsqueeze(1).broadcast_to([P, T, D]), ALU.add))
                dve.wait_ge(decay_ready, 2)

                def weigh(c):
                    dve.wait_ge(E_ready, c + 1)
                    dve.wait_ge(G_ps, c + 1)
                    V.tensor_tensor(EM[:, c % 2, :, :], EM[:, c % 2, :, :],
                                    ps[:, 2 + c % 2, 0:P].unsqueeze(1).broadcast_to([P, NH, P]), ALU.mult).then_inc(M_ready, 1)
                weigh(0)
                hq = "p (h q) -> p h q"
                for c in range(T):
                    cd = small[0:DST, 7, c * NH:(c + 1) * NH]
                    ea = small[:, 8, c * NH:(c + 1) * NH]
                    if c + 1 < T:
                        Hn = Hst[:, (c + 1) % 2, :]
                        if c:
                            dve.wait_ge(h_ready, c)
                        din(V.tensor_tensor(Hn.rearrange(hq, h=NH), Hst[:, c % 2, :].rearrange(hq, h=NH), bcast(cd, HD), ALU.mult))
                        dve.wait_ge(s_ps, c + 1)
                        V.tensor_tensor(Hn, Hn, ps[0:DST, 6 + c % 2, 0:DIN], ALU.add).then_inc(h_ready, 1)
                        weigh(c + 1)
                    dve.wait_ge(y_ps, c + 1)
                    if c:
                        dve.wait_ge(y_done, c)
                    din(V.tensor_tensor(yscr[:, 1, :].rearrange(hq, h=NH), ps[:, 4 + c % 2, DIN:2 * DIN].rearrange(hq, h=NH), bcast(ea, HD), ALU.mult))
                    din(V.tensor_tensor(yscr[:, 1, :], yscr[:, 1, :], ps[:, 4 + c % 2, 0:DIN], ALU.add))
                    V.tensor_tensor(sz[:, c, :], sz[:, c, :], yscr[:, 1, :], ALU.mult).then_inc(y_done, 1)
                dve.wait_ge(sq_done, 1)
                k = small[:, 11, :]
                V.tensor_scalar(k[:, T:2 * T], k[:, T:2 * T], 1.0 / DIN, EPS, ALU.mult, ALU.add).then_inc(yrms_var, 1)
                dve.wait_ge(yrms_sqrt, 1)
                newton_rsqrt(k[:, T:2 * T], k[:, 2 * T:3 * T], k[:, 3 * T:4 * T], k[:, 0:T])
                for c in range(T):
                    if c:
                        dve.wait_ge(mo_read, c)
                        moments([c - 1])
                    dve.wait_ge(mo_ps, c + 1)
                    V.scalar_tensor_tensor(x[:, c, :], ps[:, 2 + c % 2, 0:D], k[:, 3 * T + c:3 * T + c + 1], x[:, c, :],
                                           ALU.mult, ALU.add).then_inc(mo_read if c < T - 1 else x_ready, 1)
                dve.wait_ge(x_ready, 2)
            mamba()

            def attention(a, q, nv):
                heads, dh, w1, ring, VS = a["heads"], a["dh"], a["w1"], a["ring"], a["VS"]
                dve.wait_ge(a["u_ps"], a["turn"])
                if q == 2:
                    V.tensor_copy(W["WVu"][:, D:D + 4], ps[:, 4, 0:4])
                    i = V.tensor_copy(W["vbias"][:, D:D + 4], ps[:, 4, 4:8])
                else:
                    i = V.tensor_copy(W["WVu3"][:, D:D + 2], ps[:, 4, 0:2])
                i.then_inc(a["u_ready"], 1)
                norm(q)
                for t in range(T):
                    dve.wait_ge(a["v_ps"], t + 1)
                    if q == 2:
                        V.tensor_tensor(VS[:, t, :], ps[:, 4 + t % 4, 0:nv], W["vbias"][:], ALU.add).then_inc(a["v_ready"], 1)
                    else:
                        V.tensor_copy(VS[:, t, :], ps[:, 4 + t % 4, 0:nv]).then_inc(a["v_ready"], 1)
                dve.wait_ge(a["v_ready"], T)
                s1 = VS[:, :, D:D + heads].rearrange("p t h -> p h t")
                s2 = VS[:, :, D + heads:D + 2 * heads].rearrange("p t h -> p h t")
                V.tensor_reduce(a["smax"], s2, AX, ALU.max).then_inc(a["smax_ready"], 1)
                din(V.tensor_scalar(a["thr"], s2, -1.0, None, ALU.mult))
                dve.wait_ge(a["S_ready"], a["turn"])
                Sb = bcast(a["S"], T)
                arg = a["arg"]
                din(V.tensor_tensor(arg[:, 0, :, :], s2, Sb, ALU.subtract))
                din(V.tensor_tensor(a["tt"], s1, Sb, ALU.add))
                din(V.tensor_scalar(arg[:, 1, :, :], arg[:, 0, :, :], 0.2, None, ALU.mult))
                din(V.scalar_tensor_tensor(a["cc"], a["tt"], 0.2, a["tt"], ALU.mult, ALU.max))
                din(V.tensor_tensor(arg[:, 2, :, :], a["tt"], a["cc"], ALU.subtract))
                V.scalar_tensor_tensor(arg[:, 3, :, :], a["tt"], 0.2, a["cc"], ALU.mult, ALU.subtract).then_inc(a["arg_ready"], 1)
                dve.wait_ge(a["ex_ready"], a["turn"])
                ex = a["ex"]

                def values(h):
                    Fv, XP = a["Fv"], a["XP"][h]
                    for k in range(2):
                        V.tensor_tensor(Fv[:, :, k, 0:dh], VS[:, :, h * dh:(h + 1) * dh], bcast(ex[:, k, h, :], dh), ALU.mult)
                        i = V.tensor_copy(Fv[:, :, k, dh:w1], ex[:, k, h, :].unsqueeze(2))
                    din(i)
                    din(V.tensor_copy(XP[:, :, :, 0, :], Fv))
                    din(V.tensor_tensor(Fv, Fv, XP[:, :, :, 0, :], ALU.subtract))
                    din(V.tensor_copy(XP[:, :, :, 1, :], Fv))
                    V.tensor_tensor(XP[:, :, :, 2, :], Fv, XP[:, :, :, 1, :], ALU.subtract).then_inc(a["xp_ready"], 1)
                    dve.wait_ge(a["xp_ready"], h + 1)
                values(0)

                def masks(k, jt):
                    h, b = divmod(k, NB)
                    n = k * T + jt
                    if jt == 0:
                        dve.wait_ge(a["row_ready"], NB * h + b + 1)
                    if n >= ring:
                        dve.wait_ge(a["m_used"], n - ring + 1)
                    mk = mask[:, jt, b * BLK:(b + 1) * BLK]
                    V.scalar_tensor_tensor(a["M1"][:, n % ring, :], a["row"][h][:, b * BLK:(b + 1) * BLK],
                                           a["thr"][:, h, jt:jt + 1], mk, ALU.is_ge, ALU.mult).then_inc(a["m1_ready"], 1)
                    if n and n % SHARE == 0:
                        other(n - 1)

                def other(n):
                    b, jt = n // T % NB, n % T
                    dve.wait_ge(a["m1_ready"], n + 1)
                    V.tensor_tensor(a["M2"][:, n % ring, :], mask[:, jt, b * BLK:(b + 1) * BLK], a["M1"][:, n % ring, :],
                                    ALU.subtract).then_inc(a["m2_dve"], 1)

                def evacuate(k):
                    h, b = divmod(k, NB)
                    dve.wait_ge(a["m_used"], (k + 1) * T)
                    base = (k % a["sets"]) * 4 * a["banks"]
                    for i in range(4):
                        if a["banks"] == 1:
                            m = V.tensor_reduce(a["R"][:, i, :, :], ps[:, base + i, 0:6 * w1].rearrange("p (s k c) -> p s c k", s=2, k=3), AX, ALU.add)
                        else:
                            for s in range(2):
                                m = V.tensor_reduce(a["R"][:, i, s, :], ps[:, base + 2 * i + s, 0:3 * w1].rearrange("p (k c) -> p c k", k=3), AX, ALU.add)
                    m.then_inc(a["acc_read"], 1)
                    dve.wait_ge(a["acc_read"], k + 1)
                    for s in range(2):
                        m = V.tensor_tensor(a["R"][:, :, s, :], a["R"][:, :, s, :], bcast(ex[:, 2 + s, h, 4 * b:4 * b + 4], w1), ALU.mult)
                    din(m)
                    din(V.tensor_tensor(a["num"], a["R"][:, :, 0, :], a["R"][:, :, 1, :], ALU.add))
                    din(V.reciprocal(a["rd"], a["num"][:, :, dh]))
                    if q == 6:
                        m = V.tensor_tensor(h3[:, 4 * b:4 * b + 4, :], a["num"][:, :, 0:dh], bcast(a["rd"], dh), ALU.mult)
                        din(m)
                    else:
                        din(V.tensor_tensor(a["num"][:, :, 0:dh], a["num"][:, :, 0:dh], bcast(a["rd"], dh), ALU.mult))
                        xv = x[:, 4 * b:4 * b + 4, h * dh:(h + 1) * dh]
                        m = V.tensor_tensor(xv, xv, a["num"][:, :, 0:dh], ALU.add)
                        if k == heads * NB - 1:
                            m.then_inc(x_ready, 1)
                            dve.wait_ge(x_ready, q + 1)
                for k in range(heads * NB):
                    for jt in range(T):
                        masks(k, jt)
                        if jt == ring - 1 and k:
                            evacuate(k - 1)
                    if k == 0 and heads > 1:
                        values(1)
                other(heads * NB * T - 1)
                evacuate(heads * NB - 1)
            attention(A1, 2, D + 4)

            def experts():
                norm(3)
                dve.wait_ge(g_ps, 1)
                V.memset(gates[:, :, E1:], FILL)
                V.memset(top8, FILL)
                din(V.tensor_tensor(gates[:, :, 0:E1], ps[:, 4, 0:T * E1].rearrange("p (t e) -> p t e", e=E1),
                                    W["bg"][:].unsqueeze(1).broadcast_to([P, T, E1]), ALU.add))
                for t in range(T):
                    i = V.max(emask[:, t, :], gates[:, t, 0:E1])
                din(i)
                din(V.tensor_copy(top8[:, :, 0:2], emask[:, :, 0:2]))
                for t in range(T):
                    i = V.match_replace(out=marked[:, t, :], in_to_replace=top8[:, t, :], in_values=gates[:, t, :], imm_value=-FILL)
                din(i)
                V.tensor_scalar(emask, marked[:, :, 0:E1], -FILL, None, ALU.is_equal).then_inc(emask_ready, 1)
                dve.wait_ge(emask_ready, 1)
                n = 0
                for u in range(NB * E1):
                    b, e = divmod(u, E1)
                    xb = x[:, 4 * b:4 * b + 4, :]
                    if e == 0:
                        dve.wait_ge(o1_ps, n + 1)
                        n += 1
                        V.tensor_tensor(xb, xb, ps[:, 6 + b % 2, :].rearrange("p (i d) -> p i d", i=4), ALU.add).then_inc(o1_read, 1)
                        dve.wait_ge(o1_read, n)
                    dve.wait_ge(o1_ps, n + 1)
                    n += 1
                    for i in range(4):
                        m = V.scalar_tensor_tensor(x[:, 4 * b + i, :], ps[:, 4 + u % 2, i * D:(i + 1) * D],
                                                   emask[:, 4 * b + i, e:e + 1], x[:, 4 * b + i, :], ALU.mult, ALU.add)
                    m.then_inc(o1_read if u < NB * E1 - 1 else x_ready, 1)
                    dve.wait_ge(*((o1_read, n) if u < NB * E1 - 1 else (x_ready, 4)))
                    if e == E1 - 1 and b < NB - 1:
                        moments(range(4 * b, 4 * b + 4))
            experts()

            def cosine():
                norm(4)
                for t in range(T):
                    dve.wait_ge(kq_ps, t + 1)
                    V.tensor_copy(Kt[:, t, :], ps[:, 4 + t % 4, 0:D])
                    din(V.tensor_copy(Er[:, 0, 0:D], ps[:, 4 + t % 4, D:2 * D]))
                    V.scalar_tensor_tensor(sqj, Er[:, 0, 0:D], 1.0, Er[:, 0, 0:D], ALU.mult, ALU.mult, accum_out=qs[:, 1, t:t + 1])
                    din(V.scalar_tensor_tensor(Er[:, 1, 0:D], Kt[:, t, :], 1.0, Kt[:, t, :], ALU.mult, ALU.mult, accum_out=qs[:, 0, t:t + 1]))
                    V.tensor_copy(ab[:, 3, t:t + 1], qs[:, 0, t:t + 1]).then_inc(kq_read, 1)
                din(V.tensor_scalar(qs[:, 6:8, :], qs[:, 0:2, :], 1e-30, None, ALU.max))
                V.tensor_copy(qs[:, 0:2, :], qs[:, 6:8, :]).then_inc(norm_sq, 1)
                dve.wait_ge(norm_sqrt, 1)
                din(V.reciprocal(qs[:, 4:6, :], qs[:, 2:4, :]))
                din(V.tensor_tensor(qs[:, 6:8, :], qs[:, 0:2, :], qs[:, 4:6, :], ALU.mult))
                din(V.tensor_tensor(qs[:, 6:8, :], qs[:, 6:8, :], qs[:, 2:4, :], ALU.add))
                din(V.tensor_scalar(qs[:, 6:8, :], qs[:, 6:8, :], 0.5, 1e-4, ALU.mult, ALU.max))
                din(V.reciprocal(qs[:, 4:6, :], qs[:, 6:8, :]))
                V.tensor_tensor(Kt, Kt, bcast(qs[:, 4, :], D), ALU.mult).then_inc(kn_ready, 1)
                V.memset(xn1[:, :, D:D + 1], 1.0)
                V.tensor_copy(xn1[:, :, 0:D], xn[:, :, :]).then_inc(xn1_ready, 1)
                din(V.tensor_scalar(ab[:, 0, :], deg[:], 0.0, 0.5, ALU.is_gt, ALU.mult))
                din(V.tensor_scalar(ab[:, 1, :], ab[:, 0, :], -1.0, 1.0, ALU.mult, ALU.add))
                for t in range(T):
                    i = V.scalar_tensor_tensor(x[:, t, :], xn[:, t, :], ab[:, 1, t:t + 1], x[:, t, :], ALU.mult, ALU.add)
                din(i)

                def evacuate(b):
                    dve.wait_ge(p_used, T * (b + 1))
                    for i in range(4):
                        m = V.reciprocal(ab[:, 2, 4 * b + i:4 * b + i + 1], ps[:, 2 + i, D:D + 1])
                    din(m)
                    din(V.tensor_tensor(ab[:, 2, 4 * b:4 * b + 4], ab[:, 2, 4 * b:4 * b + 4], ab[:, 0, 4 * b:4 * b + 4], ALU.mult))
                    for i in range(4):
                        t = 4 * b + i
                        m = V.scalar_tensor_tensor(x[:, t, :], ps[:, 2 + i, 0:D], ab[:, 2, t:t + 1], x[:, t, :], ALU.mult, ALU.add)
                    m.then_inc(a2_read if b < NB - 1 else x_ready, 1)
                for n in range(NB * T):
                    b, jt = divmod(n, T)
                    dve.wait_ge(sc_exp, n + 1)
                    V.tensor_tensor(Er[:, n % RE, :], Er[:, n % RE, :], mask[:, jt, b * BLK:(b + 1) * BLK], ALU.mult).then_inc(p_ready, 1)
                    if jt == 1 and b:
                        evacuate(b - 1)
                    if jt == 2 and b:
                        dve.wait_ge(a2_read, b)
                        moments(range(4 * (b - 1), 4 * b))
                evacuate(NB - 1)
                dve.wait_ge(x_ready, 5)
            cosine()

            def depths():
                norm(5)
                dve.wait_ge(xn_ready, 6 * 11)
                dve.wait_ge(xn_act, 6 * 5)
                din(V.tensor_tensor(x[:, :, :], x[:, :, :], xn[:, :, :], ALU.add))
                for t in range(T):
                    dve.wait_ge(wrow_ready, t // TB + 1)
                    i = V.scalar_tensor_tensor(own[:, t, :], wrow[:, t * P:(t + 1) * P], 1.0, ident[:], ALU.mult, ALU.mult,
                                               accum_out=wcol[:, t:t + 1])
                din(i)
                V.memset(onesb, 1.0)
                din(V.memset(rank, 0.0))
                for t in range(T):
                    w = wcol[:, t:t + 1]
                    a0, a1 = t * P, (t + 1) * P
                    if t >= RC:
                        dve.wait_ge(cmp_used, t - RC + 1)
                    if t:
                        V.tensor_scalar(cmp[:, t % RC, 0:a0], wrow[:, 0:a0], w, None, ALU.is_ge, ALU.add, accum_out=rank[:, 0, t:t + 1])
                    V.scalar_tensor_tensor(cmp[:, t % RC, a0:a1], wrow[:, a0:a1], w, tri[:], ALU.is_ge, ALU.mult,
                                           accum_out=rank[:, 1, t:t + 1]).then_inc(cmp_ready, 1)
                dve.wait_ge(cmp_ready, T)
                din(V.tensor_tensor(rank[:, 0, :], rank[:, 0, :], rank[:, 1, :], ALU.add))
                dve.wait_ge(cmp_used, T)
                din(V.tensor_tensor(rank[:, 0, :], rank[:, 0, :], ps[:, 3, 0:T], ALU.subtract))
                din(V.tensor_tensor(rank[:, 0, :], rank[:, 0, :], W["limit"][:], ALU.is_lt))
                din(V.tensor_tensor(sw, rank[:, 0, :], wcol, ALU.mult))
                for b in range(NB):
                    dve.wait_ge(o2_ps, b + 1)
                    din(V.tensor_tensor(y2[:, b % 2, :, :], ps[:, 4 + b, :].rearrange("p (t d) -> p t d", t=TB),
                                        W["b2m"][:].unsqueeze(1).broadcast_to([P, TB, D]), ALU.add))
                    for t in range(b * TB, (b + 1) * TB):
                        i = V.scalar_tensor_tensor(x[:, t, :], y2[:, b % 2, t % TB, :], sw[:, t:t + 1], x[:, t, :], ALU.mult,
                                                   ALU.add)
                    i.then_inc(o2_read if b < NB - 1 else x_ready, 1)
                    if b < NB - 1:
                        dve.wait_ge(o2_read, b + 1)
                        moments(range(b * TB, (b + 1) * TB))
                dve.wait_ge(x_ready, 6)
            depths()

            def elu():
                V.tensor_scalar(elu_m, h3, 0.0, None, ALU.min).then_inc(elu_ready, 1)
                din(V.scalar_tensor_tensor(x[:, :, :], h3, 0.0, x[:, :, :], ALU.max, ALU.add))
                dve.wait_ge(elu_exp, 1)
                V.scalar_tensor_tensor(x[:, :, :], elu_m, -1.0, x[:, :, :], ALU.add, ALU.add).then_inc(x_ready, 1)
                dve.wait_ge(x_ready, 7)
            attention(A3, 6, D + 2)
            elu()

            def tropical():
                norm(7)
                dve.wait_ge(xnT_ready, 8 * NB)
                din(V.tensor_copy(xp3[:, 0, :], XT))
                din(V.tensor_tensor(res, XT, xp3[:, 0, :], ALU.subtract))
                din(V.tensor_copy(xp3[:, 1, :], res))
                V.tensor_tensor(xp3[:, 2, :], res, xp3[:, 1, :], ALU.subtract).then_inc(xp3_ready, 1)
                V.tensor_tensor(rise[:].rearrange("p j f -> p f j"), W["Wt"][:, :, 0:D:2], W["Wt"][:, :, 1:D:2],
                                ALU.subtract).then_inc(rise_table, 1)
                dve.wait_ge(xn_ready, 8 * 11)
                dve.wait_ge(xn_act, 8 * 5)
                din(V.tensor_tensor(x[:, :, :], x[:, :, :], W["bd"][:].unsqueeze(1).broadcast_to([P, T, D]), ALU.add))
                for side, sl in enumerate((W["slx"], W["slc"])):
                    i = V.tensor_tensor(offs[:, side], sl[:], bcast(W["bt"][:], PP), ALU.mult)
                din(i)
                for side, of in enumerate((W["ofx"], W["ofc"])):
                    i = V.tensor_tensor(offs[:, side], offs[:, side], of[:], ALU.add)
                din(i)
                for side, sl in enumerate((W["slx"], W["slc"])):
                    V.tensor_tensor(dslope[:, side], sl[:, :, 0:PP:2], sl[:, :, 1:PP:2], ALU.subtract).then_inc(lines_table, 1)
                V.tensor_tensor(doffs[:], offs[:, :, :, 0:PP:2], offs[:, :, :, 1:PP:2], ALU.subtract).then_inc(lines_table, 1)
                dve.wait_ge(sa_ready, 1)
                V.tensor_scalar(sa[:, 1, :], sa[:, 0, :], -1.0, 1.0, ALU.mult, ALU.add).then_inc(lines_table, 1)
                lo, hi, block1 = slice(0, N // 2), slice(N // 2, N), slice(BLK, 2 * BLK)

                dve.wait_ge(fill_done, FT)

                def step(f, cols, src, feature):
                    return V.scalar_tensor_tensor(acc[:, f, cols], src, W["Wt"][:, f, bass.ds(feature, 1)],
                                                  acc[:, f, cols], ALU.add, ALU.max)

                def last_sum(j, slot, n, second=False):
                    f, cols, src = ((0, slice(0, N), rise0[slot]), (3, slice(0, BLK), rise3[:, slot, :]),
                                    (1, slice(0, N), rise1[:, slot, :]))[n]
                    dve.wait_ge(sum_ready, j * 3 + (n + 1))
                    if second:
                        dve.wait_ge(sum_step, j * 3 + (n - 2))
                    step(f, cols, src, j * 2 + 1).then_inc(sum_step, 1)

                def pair(j, slot, before=2):
                    dve.wait_ge(even_ps, j + 1)
                    if before:
                        dve.wait_ge(single_step, j * 2)
                    step(3, block1, ps[:, 5, :], j * 2).then_inc(single_step, 1)
                    if before:
                        last_sum(j - 1, 1 - slot, 0, second=before > 1)
                    dve.wait_ge(pair_ps, j * 3 + 1)
                    if before:
                        dve.wait_ge(pair_step, j * 3 - 2)
                    step(2, lo, ps_wide[:, 1, hi], j * 2 + 1).then_inc(pair_step, 1)
                    if before:
                        last_sum(j - 1, 1 - slot, 1, second=before > 1)
                    dve.wait_ge(pair_ps, j * 3 + 2)
                    if before:
                        dve.wait_ge(pair_step, j * 3 - 1)
                    step(2, hi, ps_wide[:, 1, lo], j * 2 + 1).then_inc(pair_step, 1)
                    dve.wait_ge(single_step, j * 2 + 1)
                    step(3, block1, oddc[:, slot, block1], j * 2 + 1).then_inc(single_step, 1)
                    dve.wait_ge(pair_ps, j * 3 + 3)
                    if before:
                        dve.wait_ge(pair_step, j * 3)
                    step(3, hi, ps_wide[:, 1, hi], j * 2 + 1).then_inc(pair_step, 1)
                    if before:
                        last_sum(j - 1, 1 - slot, 2, second=before > 1)
                pair(0, 0, before=0)
                pair(1, 1, before=1)
                with dve.Fori(1, D // 4) as i:
                    for s in range(2):
                        pair(i * 2 + s, s)
                for n in range(3):
                    last_sum(D // 2 - 1, 1, n, second=True)
                dve.wait_ge(sum_step, 3 * D // 2)
                dve.wait_ge(pair_step, 3 * D // 2)
                dve.wait_ge(single_step, D)
                used = 0

                def take(dst, op):
                    nonlocal used
                    dve.wait_ge(pair_line, used + 1)
                    V.tensor_tensor(dst, dst, line_a[used % 3], op).then_inc(pair_used, 1)
                    used += 1
                    dve.wait_ge(pair_used, used)

                def own_line(dst, side, f, p):
                    din(V.tensor_scalar(dst, acc[:, f, :], W[("slx", "slc")[side]][:, f, p:p + 1],
                                        offs[:, side, f, p:p + 1], ALU.mult, ALU.add))
                def add_out(f):
                    dve.wait_ge(f_ps, NB * (f + 1))
                    V.tensor_tensor(x[:, :, :], x[:, :, :], ps[:, 4:8, :].rearrange("p b (t d) -> p (b t) d", t=TB),
                                    ALU.add).then_inc(x_summed, 1)
                    dve.wait_ge(x_summed, f + 1)
                for f in range(FT):
                    if f:
                        dve.wait_ge(fused_ready, f)
                    for dst, side, op in ((cvx, 0, ALU.max), (ccv, 1, ALU.min)):
                        own_line(dst, side, f, PP - 2)
                        take(dst, op)
                        own_line(line, side, f, PP - 1)
                        din(V.tensor_tensor(dst, dst, line, op))
                        take(dst, op)
                        take(dst, op)
                    add_out(f)
                    dve.wait_ge(c_read, 2 * (f + 1) * NB)
                    din(V.scalar_tensor_tensor(ccv, ccv, sa[:, 1, f:f + 1], CL[f % 2], ALU.mult, ALU.subtract))
                    din(V.scalar_tensor_tensor(cvx, cvx, sa[:, 0, f:f + 1], ccv, ALU.mult, ALU.add))
                    V.tensor_tensor(acc[:, f, :], cvx, G[f % 2], ALU.mult).then_inc(fused_ready, 1)
                for b in range(NB):
                    dve.wait_ge(f_ps, NB * FT + b + 1)
                    V.tensor_tensor(x[:, b * TB:(b + 1) * TB, :], x[:, b * TB:(b + 1) * TB, :],
                                    ps[:, 4 + b, :].rearrange("p (t d) -> p t d", t=TB), ALU.add).then_inc(x_ready, 1)
            tropical()


def layout(i):
    def tiles(w):
        return w.reshape(-1, P, w.shape[-1]).transpose(1, 0, 2)

    def cols(v):
        return v.reshape(-1, P).T
    win = i["L0_ffn_W_in"]
    order = np.concatenate([win[:, 0:DIN], win[:, 2 * DIN + 2 * DST:], win[:, DIN:2 * DIN + 2 * DST]], axis=1)
    return {
        "x": i["x"], "adjT": i["adj"].T,
        "W0T": i["L0_gnn_W"].T, "b0": i["L0_gnn_b"],
        "win": order, "convw": tiles(i["L0_ffn_conv_w"]), "convb": cols(i["L0_ffn_conv_b"]),
        "dtb": i["L0_ffn_dt_bias"], "alog": i["L0_ffn_A_log"], "Dh": i["L0_ffn_D"], "nw": cols(i["L0_ffn_norm_w"]),
        "woutT": i["L0_ffn_W_out"].T, "wlin": i["L0_ffn_W_lin"], "blin": i["L0_ffn_b_lin"],
        "W1n": i["L1_gnn_W1"], "W2n": i["L1_gnn_W2"], "W3T": i["L1_gnn_W3"].T,
        "b12": np.stack([i["L1_gnn_b1"], i["L1_gnn_b2"]], axis=1), "b3": i["L1_gnn_b3"], "a": i["L1_gnn_a"],
        "wg": i["L1_ffn_Wg"], "bg": i["L1_ffn_bg"],
        "w1e": i["L1_ffn_W1"].transpose(1, 0, 2).reshape(D, E1 * H1), "b1c": cols(i["L1_ffn_b1"].reshape(-1)),
        "w2e": tiles(i["L1_ffn_W2"].reshape(E1 * H1, D)), "b2r": i["L1_ffn_b2"],
        "wqT": i["L2_gnn_Wq"].T, "wkT": i["L2_gnn_Wk"].T,
        "limit": (KSEL - (N - 1) + np.arange(N, dtype=np.float32)).reshape(T, P).T,
        "wr": i["L2_ffn_wr"], "br": i["L2_ffn_br"], "w1m": i["L2_ffn_w1"], "b1m": cols(i["L2_ffn_b1"]),
        "w2m": tiles(i["L2_ffn_w2"]), "b2m": i["L2_ffn_b2"],
        "W3W": i["L3_gnn_W"], "W3WT": i["L3_gnn_W"].T, "a3": i["L3_gnn_a"].reshape(2, D).T,
        "Wt": tiles(i["L3_ffn_Wt"]), "bt": cols(i["L3_ffn_bt"]),
        "slx": tiles(i["L3_ffn_sl_cvx"]), "ofx": tiles(i["L3_ffn_of_cvx"]),
        "slc": tiles(i["L3_ffn_sl_ccv"]), "ofc": tiles(i["L3_ffn_of_ccv"]),
        "alpha": cols(i["L3_ffn_alpha"]), "Wc": i["L3_ffn_Wc"], "bc": cols(i["L3_ffn_bc"]),
        "Wg": i["L3_ffn_Wg"], "bgt": cols(i["L3_ffn_bg"]), "Wd": tiles(i["L3_ffn_Wd"]), "bd": i["L3_ffn_bd"],
    }


def kernel(**inputs):
    import concourse.bacc as bacc
    from concourse.bass_utils import run_bass_kernel_spmd

    nc = bacc.Bacc("TRN2", target_bir_lowering=False, num_devices=1)
    arrays, aps = {}, {}
    for name, a in layout({k: np.asarray(v) for k, v in inputs.items()}).items():
        a = np.ascontiguousarray(a)
        arrays[f"in_{name}"] = a
        aps[name] = nc.dram_tensor(f"in_{name}", a.shape, mybir.dt.from_np(a.dtype), kind="ExternalInput").ap()
    out = nc.dram_tensor("out_dram", (N, D), F32, kind="ExternalOutput").ap()
    build(nc, aps, out)
    r = run_bass_kernel_spmd(nc, [arrays], core_ids=[0])
    return r.results[0]["out_dram"]
```
